# Optimizing a Trainium2 kernel written in Bass

```python
import numpy as np
import jax
import jax.numpy as jnp

def _softmax(x, axis=-1):
    return jax.nn.softmax(x, axis=axis)

def _gelu(x):
    return jax.nn.gelu(x, approximate=True)

def _silu(x):
    return jax.nn.silu(x)

def _sigmoid(x):
    return jax.nn.sigmoid(x)

def _layernorm(x, axis=-1, eps=1e-05):
    m = jnp.mean(x, axis=axis, keepdims=True)
    v = jnp.var(x, axis=axis, keepdims=True)
    return (x - m) / jnp.sqrt(v + eps)

def _scatter_add(tgt, idx, src, axis=0):
    return tgt.at[idx].add(src)

def _segment_sum(src, seg, n):
    return jax.ops.segment_sum(src, seg, n)
kernel_name = 'mk_decoder_preln_d2_seqx_r8_344a38'

def setup_inputs(seed: int=0):
    np.random.seed(seed)
    _w = jnp.asarray

    def _rec_inputs():
        import jax
        import jax.numpy as jnp
        _rk = jax.random.key(seed)
        x = -0.0005146 + 1 * jax.random.normal(jax.random.fold_in(_rk, 1), (8, 256, 128), jnp.float32)
        _lenS = 256 - jax.random.randint(jax.random.fold_in(_rk, 7), (8,), 0, max(1, 256 // 4) + 1, jnp.int32)
        _lenS2 = 512 - jax.random.randint(jax.random.fold_in(_rk, 8), (8,), 0, max(1, 512 // 4) + 1, jnp.int32)
        _ctx_768P = jax.random.normal(jax.random.fold_in(_rk, 11), (8, 16, 96), jnp.float32)
        _ctx_768c = jax.random.dirichlet(jax.random.fold_in(_rk, 511), 0.3 * jnp.ones((16,), jnp.float32), (8, 512))
        _ctx_768t = jnp.einsum('bsk,bkd->bsd', _ctx_768c, _ctx_768P)
        _ctx_768t = _ctx_768t * jax.lax.rsqrt(jnp.mean(jnp.square(_ctx_768t)) + 1e-12) * 0.953939
        ctx_768 = -0.00040386 + 0.999972 * (_ctx_768t + 0.3 * jax.random.normal(jax.random.fold_in(_rk, 611), (8, 512, 96), jnp.float32))
        _validS = jnp.arange(256)[None, :] < _lenS[:, None]
        _validS2 = jnp.arange(512)[None, :] < _lenS2[:, None]
        _causal = jnp.tril(jnp.ones((256, 256), dtype=bool))
        mask_BxS2_bk0 = jnp.logical_not(jnp.broadcast_to(_validS2[:, :], (8, 512)))
        return (x, ctx_768, mask_BxS2_bk0)
    x, ctx_768, mask_BxS2_bk0 = _rec_inputs()

    def _L0_attn_setup():
        import jax, jax.numpy as jnp
        import numpy as np
        HEAD_SIZE = 64
        key = jax.random.key(seed)
        ks = jax.random.split(key, 5)
        B, N, D, H, E, O = (2, 256, 128, 16, HEAD_SIZE, 128)
        return {'query': jax.random.normal(ks[0], (B, N, D), dtype=jnp.float32), 'Wq': jax.random.normal(ks[1], (H, D, E), dtype=jnp.float32) / np.sqrt(D), 'Wk': jax.random.normal(ks[2], (H, D, E), dtype=jnp.float32) / np.sqrt(D), 'Wv': jax.random.normal(ks[3], (H, D, E), dtype=jnp.float32) / np.sqrt(D), 'Wp': jax.random.normal(ks[4], (H * E, O), dtype=jnp.float32) / np.sqrt(H * E), 'bp': jnp.zeros((O,), dtype=jnp.float32)}
    _L0_attn_all = _L0_attn_setup()
    _L0_attn_in = {k: v for k, v in _L0_attn_all.items() if k in ('Wq', 'Wk', 'Wv', 'Wp', 'bp')}
    del _L0_attn_all

    def _L0_xattn_setup():
        import jax, jax.numpy as jnp
        import numpy as np
        DIM_IN, DIM_LAT, DIM_HEAD = (96, 128, 64)
        INNER = max(DIM_LAT, DIM_IN)
        HEADS = INNER // DIM_HEAD
        SCALE = DIM_HEAD ** (-0.5)
        RMS_EPS = 1e-08
        LN_EPS = 1e-05

        def layernorm(x, g, b):
            mu = jnp.mean(x, axis=-1, keepdims=True)
            var = jnp.mean((x - mu) ** 2, axis=-1, keepdims=True)
            return (x - mu) * jax.lax.rsqrt(var + LN_EPS) * g + b

        def rmsnorm(x, gamma):
            norm = jnp.sqrt(jnp.sum(x * x, axis=-1, keepdims=True)) * x.shape[-1] ** (-0.5)
            return x / jnp.maximum(norm, RMS_EPS) * gamma
        key = jax.random.key(seed)
        ks = jax.random.split(key, 12)
        b, n, m = (4, 512, 64)
        x = jax.random.normal(ks[0], (b, n, DIM_IN), jnp.float32)
        latents = jax.random.normal(ks[1], (b, m, DIM_LAT), jnp.float32)
        mask = jax.random.randint(ks[2], (b, n), 0, 2).astype(bool)
        s = lambda k, sh, fan: jax.random.normal(k, sh, jnp.float32) * fan ** (-0.5)
        return {'x': x, 'latents': latents, 'mask': mask, 'ln_x_g': jnp.ones((DIM_IN,), jnp.float32), 'ln_x_b': jnp.zeros((DIM_IN,), jnp.float32), 'ln_l_g': jnp.ones((DIM_LAT,), jnp.float32), 'ln_l_b': jnp.zeros((DIM_LAT,), jnp.float32), 'qn_g': jnp.ones((DIM_HEAD,), jnp.float32), 'kn_g': jnp.ones((DIM_HEAD,), jnp.float32), 'Wq': s(ks[3], (INNER, DIM_LAT), DIM_LAT), 'Wkv': s(ks[4], (2 * INNER, DIM_IN), DIM_IN), 'Wlkv': s(ks[5], (2 * INNER, DIM_LAT), DIM_LAT), 'Wo': s(ks[6], (DIM_LAT, INNER), INNER), 'bo': jnp.zeros((DIM_LAT,), jnp.float32)}
    _L0_xattn_all = _L0_xattn_setup()
    _L0_xattn_in = {k: v for k, v in _L0_xattn_all.items() if k in ('ln_x_g', 'ln_x_b', 'ln_l_g', 'ln_l_b', 'qn_g', 'kn_g', 'Wq', 'Wkv', 'Wlkv', 'Wo', 'bo')}
    del _L0_xattn_all

    def _L0_ffn_setup():
        import jax, jax.numpy as jnp
        import numpy as np
        TOP_K = 2
        key = jax.random.key(seed)
        k0, k1, k2, k3, k4 = jax.random.split(key, 5)
        B, S, H, I, E = (1, 512, 128, 256, 8)
        hidden_states = jax.random.normal(k0, (B, S, H), dtype=jnp.float32)
        wg = jax.random.normal(k1, (E, H), dtype=jnp.float32) * 0.02
        w1 = jax.random.normal(k2, (E, I, H), dtype=jnp.float32) * 0.02
        w3 = jax.random.normal(k3, (E, I, H), dtype=jnp.float32) * 0.02
        w2 = jax.random.normal(k4, (E, H, I), dtype=jnp.float32) * 0.02
        return {'hidden_states': hidden_states, 'wg': wg, 'w1': w1, 'w3': w3, 'w2': w2}
    _L0_ffn_all = _L0_ffn_setup()
    _L0_ffn_in = {k: v for k, v in _L0_ffn_all.items() if k in ('wg', 'w1', 'w3', 'w2')}
    del _L0_ffn_all

    def _L1_attn_setup():
        import jax, jax.numpy as jnp
        import numpy as np
        EMBED_DIM = 128
        key = jax.random.key(seed)
        ks = jax.random.split(key, 9)
        B, S, D = (4, 512, EMBED_DIM)
        s = 1.0 / np.sqrt(D)
        inp = {'x': jax.random.normal(ks[0], (B, S, D), dtype=jnp.float32)}
        names = ['q', 'k', 'v', 'out']
        for i, n in enumerate(names):
            inp[f'w_{n}'] = jax.random.uniform(ks[1 + 2 * i], (D, D), jnp.float32, -s, s)
            inp[f'b_{n}'] = jax.random.uniform(ks[2 + 2 * i], (D,), jnp.float32, -s, s)
        return inp
    _L1_attn_all = _L1_attn_setup()
    _L1_attn_in = {k: v for k, v in _L1_attn_all.items() if k in ('w_q', 'b_q', 'w_k', 'b_k', 'w_v', 'b_v', 'w_out', 'b_out')}
    del _L1_attn_all

    def _L1_xattn_setup():
        import jax, jax.numpy as jnp
        import numpy as np
        IMAGE_DIM = 128
        TEXT_DIM = 96
        NUM_HEADS = 16
        HEAD_DIM = IMAGE_DIM // NUM_HEADS
        key = jax.random.key(seed)
        ks = jax.random.split(key, 14)
        B, N, M = (4, 512, 64)
        s_img = 1.0 / np.sqrt(IMAGE_DIM)
        s_txt = 1.0 / np.sqrt(TEXT_DIM)
        s_ff = 1.0 / np.sqrt(2 * IMAGE_DIM)
        return {'x': jax.random.normal(ks[0], (B, N, IMAGE_DIM), jnp.float32), 'y': jax.random.normal(ks[1], (B, M, TEXT_DIM), jnp.float32), 'Wq': jax.random.normal(ks[2], (IMAGE_DIM, IMAGE_DIM), jnp.float32) * s_img, 'bq': jax.random.normal(ks[3], (IMAGE_DIM,), jnp.float32) * s_img, 'Wk': jax.random.normal(ks[4], (TEXT_DIM, IMAGE_DIM), jnp.float32) * s_txt, 'bk': jax.random.normal(ks[5], (IMAGE_DIM,), jnp.float32) * s_txt, 'Wv': jax.random.normal(ks[6], (TEXT_DIM, IMAGE_DIM), jnp.float32) * s_txt, 'bv': jax.random.normal(ks[7], (IMAGE_DIM,), jnp.float32) * s_txt, 'W1': jax.random.normal(ks[8], (IMAGE_DIM, 2 * IMAGE_DIM), jnp.float32) * s_img, 'b1': jax.random.normal(ks[9], (2 * IMAGE_DIM,), jnp.float32) * s_img, 'W2': jax.random.normal(ks[10], (2 * IMAGE_DIM, IMAGE_DIM), jnp.float32) * s_ff, 'b2': jax.random.normal(ks[11], (IMAGE_DIM,), jnp.float32) * s_ff}
    _L1_xattn_all = _L1_xattn_setup()
    _L1_xattn_in = {k: v for k, v in _L1_xattn_all.items() if k in ('Wq', 'bq', 'Wk', 'bk', 'Wv', 'bv', 'W1', 'b1', 'W2', 'b2')}
    del _L1_xattn_all

    def _L1_ffn_setup():
        import jax, jax.numpy as jnp
        import numpy as np
        B, S, D = (2, 64, 128)
        E, K, I = (16, 8, 128)
        I_SH = 128
        ROUTE_SCALE = 2.826
        key = jax.random.key(seed)
        ks = jax.random.split(key, 8)
        s = 0.02
        return {'x': jax.random.normal(ks[0], (B, S, D), dtype=jnp.float32), 'gate_w': jax.random.normal(ks[1], (E, D), dtype=jnp.float32) * s, 'expert_bias': jnp.zeros((E,), dtype=jnp.float32), 'w_gate': jax.random.normal(ks[2], (E, I, D), dtype=jnp.float32) * s, 'w_up': jax.random.normal(ks[3], (E, I, D), dtype=jnp.float32) * s, 'w_down': jax.random.normal(ks[4], (E, D, I), dtype=jnp.float32) * s, 'shared_gate_w': jax.random.normal(ks[5], (I_SH, D), dtype=jnp.float32) * s, 'shared_up_w': jax.random.normal(ks[6], (I_SH, D), dtype=jnp.float32) * s, 'shared_down_w': jax.random.normal(ks[7], (D, I_SH), dtype=jnp.float32) * s}
    _L1_ffn_all = _L1_ffn_setup()
    _L1_ffn_in = {k: v for k, v in _L1_ffn_all.items() if k in ('gate_w', 'expert_bias', 'w_gate', 'w_up', 'w_down', 'shared_gate_w', 'shared_up_w', 'shared_down_w')}
    del _L1_ffn_all
    return {'x': x, 'ctx_768': ctx_768, 'mask_BxS2_bk0': mask_BxS2_bk0, 'L0_attn_Wq': _L0_attn_in['Wq'], 'L0_attn_Wk': _L0_attn_in['Wk'], 'L0_attn_Wv': _L0_attn_in['Wv'], 'L0_attn_Wp': _L0_attn_in['Wp'], 'L0_attn_bp': _L0_attn_in['bp'], 'L0_xattn_ln_x_g': _L0_xattn_in['ln_x_g'], 'L0_xattn_ln_x_b': _L0_xattn_in['ln_x_b'], 'L0_xattn_ln_l_g': _L0_xattn_in['ln_l_g'], 'L0_xattn_ln_l_b': _L0_xattn_in['ln_l_b'], 'L0_xattn_qn_g': _L0_xattn_in['qn_g'], 'L0_xattn_kn_g': _L0_xattn_in['kn_g'], 'L0_xattn_Wq': _L0_xattn_in['Wq'], 'L0_xattn_Wkv': _L0_xattn_in['Wkv'], 'L0_xattn_Wlkv': _L0_xattn_in['Wlkv'], 'L0_xattn_Wo': _L0_xattn_in['Wo'], 'L0_xattn_bo': _L0_xattn_in['bo'], 'L0_ffn_wg': _L0_ffn_in['wg'], 'L0_ffn_w1': _L0_ffn_in['w1'], 'L0_ffn_w3': _L0_ffn_in['w3'], 'L0_ffn_w2': _L0_ffn_in['w2'], 'L1_attn_w_q': _L1_attn_in['w_q'], 'L1_attn_b_q': _L1_attn_in['b_q'], 'L1_attn_w_k': _L1_attn_in['w_k'], 'L1_attn_b_k': _L1_attn_in['b_k'], 'L1_attn_w_v': _L1_attn_in['w_v'], 'L1_attn_b_v': _L1_attn_in['b_v'], 'L1_attn_w_out': _L1_attn_in['w_out'], 'L1_attn_b_out': _L1_attn_in['b_out'], 'L1_xattn_Wq': _L1_xattn_in['Wq'], 'L1_xattn_bq': _L1_xattn_in['bq'], 'L1_xattn_Wk': _L1_xattn_in['Wk'], 'L1_xattn_bk': _L1_xattn_in['bk'], 'L1_xattn_Wv': _L1_xattn_in['Wv'], 'L1_xattn_bv': _L1_xattn_in['bv'], 'L1_xattn_W1': _L1_xattn_in['W1'], 'L1_xattn_b1': _L1_xattn_in['b1'], 'L1_xattn_W2': _L1_xattn_in['W2'], 'L1_xattn_b2': _L1_xattn_in['b2'], 'L1_ffn_gate_w': _L1_ffn_in['gate_w'], 'L1_ffn_expert_bias': _L1_ffn_in['expert_bias'], 'L1_ffn_w_gate': _L1_ffn_in['w_gate'], 'L1_ffn_w_up': _L1_ffn_in['w_up'], 'L1_ffn_w_down': _L1_ffn_in['w_down'], 'L1_ffn_shared_gate_w': _L1_ffn_in['shared_gate_w'], 'L1_ffn_shared_up_w': _L1_ffn_in['shared_up_w'], 'L1_ffn_shared_down_w': _L1_ffn_in['shared_down_w']}

def reference(x, ctx_768, mask_BxS2_bk0, L0_attn_Wq, L0_attn_Wk, L0_attn_Wv, L0_attn_Wp, L0_attn_bp, L0_xattn_ln_x_g, L0_xattn_ln_x_b, L0_xattn_ln_l_g, L0_xattn_ln_l_b, L0_xattn_qn_g, L0_xattn_kn_g, L0_xattn_Wq, L0_xattn_Wkv, L0_xattn_Wlkv, L0_xattn_Wo, L0_xattn_bo, L0_ffn_wg, L0_ffn_w1, L0_ffn_w3, L0_ffn_w2, L1_attn_w_q, L1_attn_b_q, L1_attn_w_k, L1_attn_b_k, L1_attn_w_v, L1_attn_b_v, L1_attn_w_out, L1_attn_b_out, L1_xattn_Wq, L1_xattn_bq, L1_xattn_Wk, L1_xattn_bk, L1_xattn_Wv, L1_xattn_bv, L1_xattn_W1, L1_xattn_b1, L1_xattn_W2, L1_xattn_b2, L1_ffn_gate_w, L1_ffn_expert_bias, L1_ffn_w_gate, L1_ffn_w_up, L1_ffn_w_down, L1_ffn_shared_gate_w, L1_ffn_shared_up_w, L1_ffn_shared_down_w):
    import jax
    import jax.numpy as jnp

    def _L0_attn_ref(query, Wq, Wk, Wv, Wp, bp):
        import jax, jax.numpy as jnp
        import numpy as np
        HEAD_SIZE = 64
        B, N, D = query.shape
        H, _, E = Wq.shape
        scale = 1.0 / jnp.sqrt(jnp.asarray(E, query.dtype))
        q = jnp.einsum('bnd,hde->bhne', query, Wq) * scale
        k = jnp.einsum('bmd,hde->bhme', query, Wk)
        v = jnp.einsum('bmd,hde->bhme', query, Wv)
        logits = jnp.einsum('bhne,bhme->bhnm', q, k)
        attn = jax.nn.softmax(logits, axis=-1)
        out = jnp.einsum('bhnm,bhme->bnhe', attn, v)
        out = jnp.swapaxes(out, -1, -2).reshape(B, N, E * H)
        return jnp.dot(out, Wp) + bp

    def _L0_xattn_ref(x, latents, mask, ln_x_g, ln_x_b, ln_l_g, ln_l_b, qn_g, kn_g, Wq, Wkv, Wlkv, Wo, bo):
        import jax, jax.numpy as jnp
        import numpy as np
        DIM_IN, DIM_LAT, DIM_HEAD = (96, 128, 64)
        INNER = max(DIM_LAT, DIM_IN)
        HEADS = INNER // DIM_HEAD
        SCALE = DIM_HEAD ** (-0.5)
        RMS_EPS = 1e-08
        LN_EPS = 1e-05

        def layernorm(x, g, b):
            mu = jnp.mean(x, axis=-1, keepdims=True)
            var = jnp.mean((x - mu) ** 2, axis=-1, keepdims=True)
            return (x - mu) * jax.lax.rsqrt(var + LN_EPS) * g + b

        def rmsnorm(x, gamma):
            norm = jnp.sqrt(jnp.sum(x * x, axis=-1, keepdims=True)) * x.shape[-1] ** (-0.5)
            return x / jnp.maximum(norm, RMS_EPS) * gamma
        b, n, _ = x.shape
        m = latents.shape[1]
        xn = layernorm(x, ln_x_g, ln_x_b)
        ln = layernorm(latents, ln_l_g, ln_l_b)
        q = ln @ Wq.T
        kv = jnp.concatenate([xn @ Wkv.T, ln @ Wlkv.T], axis=1)
        k, v = (kv[..., :INNER], kv[..., INNER:])
        split_heads = lambda t: t.reshape(t.shape[0], t.shape[1], HEADS, DIM_HEAD).transpose(0, 2, 1, 3)
        q, k, v = (split_heads(q), split_heads(k), split_heads(v))
        qn = rmsnorm(q, qn_g) * SCALE
        kn = rmsnorm(k, kn_g)
        attn = jnp.einsum('bhid,bhjd->bhij', qn, kn)
        full_mask = jnp.pad(mask, ((0, 0), (0, m)), constant_values=True)
        attn = jnp.where(full_mask[:, None, None, :], attn, -jnp.finfo(attn.dtype).max)
        attn = jax.nn.softmax(attn, axis=-1)
        out = jnp.einsum('bhij,bhjd->bhid', attn, v)
        out = out.transpose(0, 2, 1, 3).reshape(b, m, INNER)
        return out @ Wo.T + bo

    def _L0_ffn_ref(hidden_states, wg, w1, w3, w2):
        import jax, jax.numpy as jnp
        import numpy as np
        TOP_K = 2
        orig_shape = hidden_states.shape
        H = orig_shape[-1]
        E = wg.shape[0]
        x = hidden_states.reshape(-1, H)
        router_logits = x @ wg.T
        probs = jax.nn.softmax(router_logits, axis=-1)
        topk_w, topk_idx = jax.lax.top_k(probs, TOP_K)
        topk_w = topk_w / jnp.sum(topk_w, axis=-1, keepdims=True)
        expert_w = jnp.sum(jax.nn.one_hot(topk_idx, E, dtype=x.dtype) * topk_w[..., None], axis=1)
        h1 = jnp.einsum('th,eih->tei', x, w1)
        h3 = jnp.einsum('th,eih->tei', x, w3)
        y = jnp.einsum('tei,ehi->teh', jax.nn.silu(h1) * h3, w2)
        out = jnp.einsum('te,teh->th', expert_w, y)
        return out.reshape(orig_shape)

    def _L1_attn_ref(x, w_q, b_q, w_k, b_k, w_v, b_v, w_out, b_out):
        import jax, jax.numpy as jnp
        import numpy as np
        EMBED_DIM = 128
        D = x.shape[-1]
        scaling = 1.0 / jnp.sqrt(jnp.asarray(D, x.dtype))
        q = jnp.einsum('bsd,ed->bse', x, w_q) + b_q
        k = jnp.einsum('bsd,ed->bse', x, w_k) + b_k
        v = jnp.einsum('bsd,ed->bse', x, w_v) + b_v
        scores = jnp.einsum('bqd,bkd->bqk', q, k) * scaling
        attn = jax.nn.softmax(scores, axis=-1)
        out = jnp.einsum('bqk,bkd->bqd', attn, v)
        return jnp.einsum('bsd,ed->bse', out, w_out) + b_out

    def _L1_xattn_ref(x, y, Wq, bq, Wk, bk, Wv, bv, W1, b1, W2, b2):
        import jax, jax.numpy as jnp
        import numpy as np
        IMAGE_DIM = 128
        TEXT_DIM = 96
        NUM_HEADS = 16
        HEAD_DIM = IMAGE_DIM // NUM_HEADS
        B, N, _ = x.shape
        M = y.shape[1]
        q = (x @ Wq + bq).reshape(B, N, NUM_HEADS, HEAD_DIM)
        k = (y @ Wk + bk).reshape(B, M, NUM_HEADS, HEAD_DIM)
        v = (y @ Wv + bv).reshape(B, M, NUM_HEADS, HEAD_DIM)
        scale = 1.0 / np.sqrt(HEAD_DIM)
        scores = jnp.einsum('bnhd,bmhd->bhnm', q, k) * scale
        attn = jax.nn.softmax(scores, axis=-1)
        out = jnp.einsum('bhnm,bmhd->bnhd', attn, v).reshape(B, N, IMAGE_DIM)
        h = jax.nn.relu(out @ W1 + b1)
        return h @ W2 + b2

    def _L1_ffn_ref(x, gate_w, expert_bias, w_gate, w_up, w_down, shared_gate_w, shared_up_w, shared_down_w):
        import jax, jax.numpy as jnp
        import numpy as np
        B, S, D = (2, 64, 128)
        E, K, I = (16, 8, 128)
        I_SH = 128
        ROUTE_SCALE = 2.826
        gates = jnp.einsum('bsd,ed->bse', x, gate_w)
        scores = jax.nn.sigmoid(gates.astype(jnp.float32))
        sel_scores = scores + expert_bias
        _, inds = jax.lax.top_k(sel_scores, K)
        selected = jnp.take_along_axis(scores, inds, axis=-1)
        selected = selected / selected.sum(axis=-1, keepdims=True)
        selected = selected * ROUTE_SCALE
        onehot = jax.nn.one_hot(inds, E, dtype=selected.dtype)
        combine = jnp.einsum('bske,bsk->bse', onehot, selected)
        hg = jnp.einsum('bsd,eid->bsei', x, w_gate)
        hu = jnp.einsum('bsd,eid->bsei', x, w_up)
        h = jax.nn.silu(hg) * hu
        ye = jnp.einsum('bsei,edi->bsed', h, w_down)
        y = jnp.einsum('bsed,bse->bsd', ye, combine).astype(x.dtype)
        g = jnp.einsum('bsd,id->bsi', x, shared_gate_w)
        u = jnp.einsum('bsd,id->bsi', x, shared_up_w)
        y = y + jnp.einsum('bsi,di->bsd', jax.nn.silu(g) * u, shared_down_w)
        return y
    x = x + _L0_attn_ref(_layernorm(x, axis=-1), L0_attn_Wq, L0_attn_Wk, L0_attn_Wv, L0_attn_Wp, L0_attn_bp)
    x = x + _L0_xattn_ref(ctx_768, _layernorm(x, axis=-1), mask_BxS2_bk0, L0_xattn_ln_x_g, L0_xattn_ln_x_b, L0_xattn_ln_l_g, L0_xattn_ln_l_b, L0_xattn_qn_g, L0_xattn_kn_g, L0_xattn_Wq, L0_xattn_Wkv, L0_xattn_Wlkv, L0_xattn_Wo, L0_xattn_bo)
    x = x + _L0_ffn_ref(_layernorm(x, axis=-1), L0_ffn_wg, L0_ffn_w1, L0_ffn_w3, L0_ffn_w2)
    x = x + _L1_attn_ref(_layernorm(x, axis=-1), L1_attn_w_q, L1_attn_b_q, L1_attn_w_k, L1_attn_b_k, L1_attn_w_v, L1_attn_b_v, L1_attn_w_out, L1_attn_b_out)
    x = x + _L1_xattn_ref(_layernorm(x, axis=-1), ctx_768, L1_xattn_Wq, L1_xattn_bq, L1_xattn_Wk, L1_xattn_bk, L1_xattn_Wv, L1_xattn_bv, L1_xattn_W1, L1_xattn_b1, L1_xattn_W2, L1_xattn_b2)
    x = x + _L1_ffn_ref(_layernorm(x, axis=-1), L1_ffn_gate_w, L1_ffn_expert_bias, L1_ffn_w_gate, L1_ffn_w_up, L1_ffn_w_down, L1_ffn_shared_gate_w, L1_ffn_shared_up_w, L1_ffn_shared_down_w)
    return x

_drawn_inputs = setup_inputs


def setup_inputs(seed=0):
    import zlib

    import numpy as np

    out = dict(_drawn_inputs(seed))
    spreads = {'L0_attn_bp': (0.0, 0.1),
     'L0_xattn_ln_x_g': (1.0, 0.58),
     'L0_xattn_ln_x_b': (0.0, 0.347),
     'L0_xattn_ln_l_g': (1.0, 0.2),
     'L0_xattn_ln_l_b': (0.0, 0.1),
     'L0_xattn_qn_g': (1.0, 0.6),
     'L0_xattn_kn_g': (1.0, 0.6),
     'L0_xattn_bo': (0.0, 0.1),
     'L1_ffn_expert_bias': (0.0, 0.8)}
    factors = {'L0_ffn_wg': 8.0,
     'L0_ffn_w1': 8.0,
     'L0_ffn_w3': 8.0,
     'L0_ffn_w2': 8.0,
     'L1_attn_w_q': 5.317,
     'L1_attn_b_q': 8.0,
     'L1_attn_w_k': 5.206,
     'L1_attn_b_k': 64.0,
     'L1_xattn_bq': 4.215,
     'L1_xattn_bk': 64.0,
     'L1_ffn_gate_w': 8.0,
     'L1_ffn_w_gate': 8.0,
     'L1_ffn_w_up': 8.0,
     'L1_ffn_w_down': 8.0,
     'L1_ffn_shared_gate_w': 8.0,
     'L1_ffn_shared_up_w': 8.0,
     'L1_ffn_shared_down_w': 8.0,
     'L1_attn_b_v': 2.679}
    for name, (base, spread) in spreads.items():
        noise = np.random.default_rng([zlib.crc32(name.encode()), seed]).standard_normal(out[name].shape)
        drawn = base * np.exp(spread * noise) if base else spread * noise
        out[name] = jnp.asarray(drawn.astype(out[name].dtype))
    for name, factor in factors.items():
        out[name] = (out[name] * factor).astype(out[name].dtype)
    return out
```

```python
import math
from contextlib import ExitStack

import concourse.bass as bass
from concourse import mybir

B, N, M, D, DC = 8, 256, 512, 128, 96
P = 128
NT, MT = N // P, M // P
HA, EA = 16, 64
HX, EX = 2, 64
HY, EY = 16, 8
E0, I0 = 8, 256
E1, K1, I1 = 16, 8, 128
TK = N + M
CH = 512
NCH = B * N // CH
CT = CH // P
ROUTE_SCALE = 2.826
LN_EPS = 1e-5
STG = (E1 + 1) * I1


def decoder(nc, t, out):
    f32, f32r, u8 = mybir.dt.float32, mybir.dt.float32r, mybir.dt.uint8
    ALU, ACT, AX = mybir.AluOpType, mybir.ActivationFunctionType, mybir.AxisListType

    ctx = ExitStack()
    with ctx:
        def sem(name):
            return ctx.enter_context(nc.semaphore(name))

        class Arena:

            def __init__(self):
                self.stack = ExitStack()
                self.free = nc.sbuf_bytes_remaining

            def sb(self, name, cols, dt=f32, parts=P):
                made = self.stack.enter_context(nc.sbuf_tensor(name, [parts, cols], dt))
                self.used = self.free - nc.sbuf_bytes_remaining
                return made

        def keep(name, cols, dt=f32, parts=P):
            return ctx.enter_context(nc.sbuf_tensor(name, [parts, cols], dt))

        X = keep("X", B * NT * D)
        Xt = X[:, :].rearrange("p (t d) -> p t d", d=D)
        stage = [keep("stage0", STG), keep("stage1", STG)]
        ident = keep("ident", P)
        onesrow = keep("onesrow", P, parts=1)
        halves = keep("halves", 32)
        st = keep("st", 8 * 6)
        mv = keep("mv", 8 * 2)
        vs = keep("vs", 8)
        rs = keep("rs", 8)
        xn = keep("xn", NT * D)
        XH = keep("XH", N, f32r)
        XL = keep("XL", N, f32r)
        sm = keep("sm", 1024)
        st3 = st[:, :].rearrange("p (t s) -> p t s", s=6)
        mv3 = mv[:, :].rearrange("p (t s) -> p t s", s=2)
        xn3 = xn[:, :].rearrange("p (t d) -> p t d", d=D)

        a = Arena()
        MH, ML = a.sb("MH", HA * D, f32r), a.sb("ML", HA * D, f32r)
        WVH, WVL = a.sb("WVH", HA * EA, f32r), a.sb("WVL", HA * EA, f32r)
        WP = a.sb("WP", HA * EA)
        bp = a.sb("bp", D, parts=1)
        GH = [a.sb(f"GH{i}", 2 * N, f32r) for i in range(2)]
        GL = [a.sb(f"GL{i}", 2 * N, f32r) for i in range(2)]
        PA = [a.sb(f"PA{i}", NT * N) for i in range(2)]
        PTA = [a.sb(f"PTA{i}", NT * N) for i in range(2)]
        VA = a.sb("VA", NT * HA * EA)
        ONA = a.sb("ONA", NT * HA * EA)
        OTA = a.sb("OTA", HA * EA // P * N)
        a.stack.close()
        e = Arena()
        WKSH, WKSL = e.sb("WKSH", 4 * P, f32r), e.sb("WKSL", 4 * P, f32r)
        WQSH, WQSL = e.sb("WQSH", 4 * P, f32r), e.sb("WQSL", 4 * P, f32r)
        WVE = e.sb("WVE", D)
        bqs = e.sb("bqs", 4)
        W1E, W2E = e.sb("W1E", 2 * D), e.sb("W2E", 2 * D)
        b1E, b2E = e.sb("b1E", 2), e.sb("b2E", D, parts=1)
        CU, CD = e.sb("CU", 4 * P), e.sb("CD", 4 * P)
        selq, selk, seln, hmask = e.sb("selq", 1), e.sb("selk", 1), e.sb("seln", 1), e.sb("hmask", 4)
        CTE = e.sb("CTE", M)
        CEH, CEL = e.sb("CEH", M, f32r), e.sb("CEL", M, f32r)
        KS = e.sb("KS", 4 * M, f32r)
        QT0, QHt, QSt = e.sb("QT0", N), e.sb("QHt", N), e.sb("QSt", N)
        QM = e.sb("QM", HY * N, f32r)
        VO = e.sb("VO", MT * HY * 32)
        NMX = e.sb("NMX", NT * P)
        NRH = e.sb("NRH", N)
        NRL = e.sb("NRL", N)
        PTE = [e.sb(f"PTE{i}", 4 * MT * N) for i in range(2)]
        UD = e.sb("UD", 4 * N)
        KHt = PTE[1][:, 0:M]
        RDE, OE, H1E = PTE[0][:, 0:N], PTE[0][:, N:2 * N], PTE[0][:, 2 * N:4 * N]
        e.stack.close()
        big = Arena()
        big.sb("arena1_space", max(a.used, e.used) // 4)
        ctx.enter_context(big.stack)

        c = Arena()
        W1H, W1L = c.sb("W1H", E0 * I0, f32r), c.sb("W1L", E0 * I0, f32r)
        W3H, W3L = c.sb("W3H", E0 * I0, f32r), c.sb("W3L", E0 * I0, f32r)
        W2C = c.sb("W2C", 2 * E0 * D)
        WGC = c.sb("WGC", E0)
        c.stack.close()
        f = Arena()
        FGH, FGL = f.sb("FGH", STG, f32r), f.sb("FGL", STG, f32r)
        FUH, FUL = f.sb("FUH", STG, f32r), f.sb("FUL", STG, f32r)
        FD = f.sb("FD", STG)
        WGF = f.sb("WGF", E1)
        ebF = f.sb("ebF", E1)
        f.stack.close()
        big2 = Arena()
        big2.sb("arena2_space", max(c.used, f.used) // 4)
        ctx.enter_context(big2.stack)

        x = Arena()
        WQX, WOX = x.sb("WQX", D), x.sb("WOX", D)
        WKVX, WLKV = x.sb("WKVX", 2 * D), x.sb("WLKV", 2 * D)
        boX = x.sb("boX", D, parts=1)
        gcol = x.sb("gcol", 6)
        CX = x.sb("CX", MT * DC)
        CN = x.sb("CN", MT * DC)
        LN2 = x.sb("LN2", NT * D)
        CXT, LT = x.sb("CXT", M), x.sb("LT", N)
        QKN = x.sb("QKN", 8 * D)
        SQ = QKN
        VX = x.sb("VX", 6 * D)
        QTX, KTX = x.sb("QTX", N), x.sb("KTX", TK)
        mk8 = x.sb("mk8", M, u8, parts=1)
        mkb = x.sb("mkb", M, parts=1)
        PX = [x.sb(f"PX{i}", TK) for i in range(2)]
        PTX = x.sb("PTX", TK)
        ONX, OTX = x.sb("ONX", N), x.sb("OTX", N)
        x.stack.close()
        x = Arena()
        WQD, WKD, WVD, WOD = (x.sb(n, D) for n in ("WQD", "WKD", "WVD", "WOD"))
        bqk = x.sb("bqk", 2)
        bvD, boD = x.sb("bvD", D, parts=1), x.sb("boD", D, parts=1)
        XF = x.sb("XF", N)
        QD, KD, VD = x.sb("QD", N), x.sb("KD", N), x.sb("VD", N)
        PD, PTD = x.sb("PD", NT * N), x.sb("PTD", NT * N)
        OND, OTD = x.sb("OND", N), x.sb("OTD", N)
        x.stack.close()
        w = Arena()
        SG = [w.sb(f"SG{i}", 2 * N) for i in range(2)]
        H2 = [w.sb(f"H2{i}", 2 * N) for i in range(2)]
        XF2 = w.sb("XF2", N)
        gt = w.sb("gt", 512)
        w.stack.close()

        PB = [ctx.enter_context(nc.psum_tensor(f"PB{i}", [P, 512], f32)) for i in range(8)]

        def mm3(o, lh, ll, rh, rl, first=True, last=True):
            nc.tensor.matmul(o, lh, rh, start=first, stop=False)
            nc.tensor.matmul(o, ll, rh, start=False, stop=False)
            return nc.tensor.matmul(o, lh, rl, start=False, stop=last)

        def mm(o, l, r, first=True, last=True):
            return nc.tensor.matmul(o, l, r, start=first, stop=last)

        consts_loaded = sem("consts_loaded")
        x_loaded = sem("x_loaded")
        out_stored = sem("out_stored")
        own = sem("vector_own")
        pool_own = sem("pool_own")
        layer_done = [sem(f"layer{i}_done") for i in range(6)]
        LAYERS = [B] * 2 + [B] + [B] * 2 + [B]

        class Front:

            def __init__(self, n):
                self.var_ready = sem(f"var{n}_ready")
                self.rstd_ready = sem(f"rstd{n}_ready")
                self.xn_ready = sem(f"xn{n}_ready")
                self.xt_ready = sem(f"xt{n}_ready")
                self.xh_ready = sem(f"xh{n}_ready")
                self.xl_ready = sem(f"xl{n}_ready")

        fronts = [Front(i) for i in range(6)]
        own_count = [0]

        class Own:

            def __init__(self, eng, s):
                self.eng, self.s, self.base, self.k, self.per, self.b = eng, s, 0, 0, 0, 0

            def loop(self, b, per):
                self.b, self.per, self.k = b, per, 0

            def end(self, times):
                assert self.k == self.per, (self.k, self.per)
                self.base += self.per * times
                self.k = self.per = self.b = 0

            def did(self, ins):
                self.k += 1
                ins.then_inc(self.s, 1)

            def wait(self):
                self.eng.wait_ge(self.s, self.b * self.per + (self.base + self.k))

            def wait_alone(self):
                wait_alone(self.eng, self.s, self.b * self.per + (self.base + self.k))

        BANK_X = 7

        def front_vector(dve, o, F, b, tiles=NT):
            for i in range(NT):
                last = nc.vector.bn_stats(st3[:, i, :], X[:, bass.ds((b * NT + i) * D, D)])
            o.did(last)
            o.wait_alone()
            for i in range(NT):
                last = nc.vector.bn_aggr(mv3[:, i, :], st3[:, i, :])
            last.then_inc(F.var_ready, 1)
            dve.wait_ge(F.rstd_ready, b + 1)
            for i in range(NT):
                last = nc.vector.tensor_scalar(xn3[:, i, :], X[:, bass.ds((b * NT + i) * D, D)], mv3[:, i, 0:1],
                                               rs[:, i:i + 1], ALU.subtract, ALU.mult)
            last.then_inc(F.xn_ready, 1)

        def front_pool(pool, po, F, b):
            wait_alone(pool, F.var_ready, b + 1)
            po.did(nc.gpsimd.tensor_scalar(vs[:, 0:NT], mv3[:, 0:NT, 1], LN_EPS, None, ALU.add))
            po.wait()
            nc.gpsimd.tensor_tensor(rs[:, 0:NT], vs[:, 0:NT], halves[:, 0:NT], ALU.pow).then_inc(F.rstd_ready, 1)

        def front_tensor(pe, F, b):
            pe.wait_ge(F.xn_ready, b + 1)
            for i in range(NT):
                last = nc.tensor.transpose(PB[BANK_X][:, i * P:(i + 1) * P], xn3[:, i, :], ident[:, :])
            last.then_inc(F.xt_ready, 1)

        def front_scalar(act, F, b):
            act.wait_ge(F.xt_ready, b + 1)
            nc.scalar.activation(XH[:, :], PB[BANK_X][:, 0:N], ACT.Copy).then_inc(F.xh_ready, 1)

        def front_low(dve, F, b):
            dve.wait_ge(F.xh_ready, b + 1)
            nc.vector.tensor_tensor(XL[:, :], PB[BANK_X][:, 0:N], XH[:, :].bitcast(f32),
                                    ALU.subtract).then_inc(F.xl_ready, 1)

        S = {}
        for name in ("a_mready a_mh a_ml a_v a_vc a_g a_gh a_gl a_s a_max a_exp a_pt a_ptc a_o a_on a_ot a_otc a_y "
                     "b_ctx b_var b_rstd b_cn b_ln2 b_lt b_ltc b_qkv b_sq b_ss b_rr b_qkn b_v b_qkt b_qktc b_mk "
                     "b_s b_max b_exp b_pt b_ptc b_o b_on b_ot b_otc b_y "
                     "c_r c_h c_sg c_h2 c_y c_yd c_xf c_sig "
                     "d_q d_qc d_v d_vc d_s d_max d_exp d_pt d_ptc d_o d_on d_ot d_otc d_y "
                     "e_ctx e_split e_k e_kh e_ks e_v e_vc e_q e_qc e_qs e_qm e_s e_max e_nr e_nm e_st e_exp e_u e_uc "
                     "e_od e_o e_h e_hc e_y e_vo0 "
                     "f_r f_sig f_h f_sg f_h2 f_y f_yd "
                     "qk_in w_in0 w_in1 w_split").split():
            S[name] = sem(name)

        wait_passed = sem("wait_passed")

        def wait_alone(eng, s, value):
            eng.wait_ge(s, value)
            eng.sem_inc(wait_passed, 1)

        split_a = [("wv", P, HA * EA, WVH, WVL)]
        split_c = [("w1", P, E0 * I0, W1H, W1L), ("w3", P, E0 * I0, W3H, W3L)]
        split_e = [("wks", P, 4 * P, WKSH, WKSL), ("wqs", P, 4 * P, WQSH, WQSL)]
        split_f = [("fg", P, STG, FGH, FGL), ("fu", P, STG, FUH, FUL)]
        splits = [(i, None) for i in split_a] + [(i, None) for i in split_c] + [(i, 0) for i in split_e] \
            + [(i, 2) for i in split_f]
        SPLIT_A, SPLIT_C, SPLIT_E, SPLIT_F = 1, 3, 5, 7

        plain = {
            "a": [(WP, "wp"), (bp, "bp")],
            "x": [(WQX, "wqx"), (WOX, "wox"), (WKVX[0:DC, :], "wkvx"), (WLKV, "wlkv"), (boX, "box"), (gcol, "gcol")],
            "c": [(W2C, "w2"), (WGC, "wgc")],
            "d": [(WQD, "wqd"), (WKD, "wkd"), (WVD, "wvd"), (WOD, "wod"), (bqk, "bqk"), (bvD, "bvd"), (boD, "bod")],
            "e": [(WVE[0:DC + 1, :], "wve"), (bqs, "bqs"), (W1E, "w1e"), (W2E, "w2e"), (b1E, "b1e"), (b2E, "b2e"),
                  (CU, "cu"), (CD, "cd"), (selq, "selq"), (selk, "selk"), (seln, "seln"), (hmask, "hmask")],
            "f": [(FD, "fd"), (WGF, "wgf"), (ebF, "ebf")],
        }
        loaded = {k: sem(f"loaded_{k}") for k in plain}

        block = ctx.enter_context(nc.Block())

        @block.sync
        def _(sp):
            sp.dma_start(ident[:, :], t["ident"]).then_inc(consts_loaded, 16)
            sp.dma_start(onesrow[:, :], t["onesrow"]).then_inc(consts_loaded, 16)
            sp.dma_start(X[:, :], t["x"]).then_inc(x_loaded, 16)
            sp.dma_start(stage[0][0:EA, 0:HA * D], t["wqT"]).then_inc(S["qk_in"], 16)
            sp.dma_start(stage[1][0:EA, 0:HA * D], t["wkT"]).then_inc(S["qk_in"], 16)

            def plain_loads(k):
                for dst, name in plain[k]:
                    sp.dma_start(dst if isinstance(dst, bass.AP) else dst[:, :], t[name]).then_inc(loaded[k], 16)

            def split_load(i):
                (name, parts, cols, hi, lo), after = splits[i]
                if i < 2:
                    sp.wait_ge(S["a_ml"], 4)
                else:
                    sp.wait_ge(S["w_split"], 2 * (i - 1))
                sp.dma_start(stage[i % 2][0:parts, 0:cols], t[name]).then_inc(S[f"w_in{i % 2}"], 16)

            plain_loads("a")
            plain_loads("x")
            plain_loads("c")
            for i in range(SPLIT_C):
                split_load(i)

            def context_load(dst, b, src, s):
                sp.dma_start(dst, src[bass.ds(b, 1)].rearrange("b p n -> p (b n)")).then_inc(s, 16)

            def load_context(b):
                context_load(CX[:, :], b, t["ctx"], S["b_ctx"])
                sp.dma_start(mk8[:, :], t["mask"][bass.ds(b, 1), :]).then_inc(S["b_ctx"], 16)

            load_context(0)
            with sp.Fori(1, B) as b:
                sp.wait_ge(S["b_cn"], b)
                sp.wait_ge(S["b_mk"], b)
                load_context(b)
            sp.wait_ge(layer_done[0], B)
            plain_loads("e")
            for i in range(SPLIT_C, SPLIT_E):
                split_load(i)
            sp.wait_ge(layer_done[2], B)
            plain_loads("d")
            plain_loads("f")
            for i in range(SPLIT_E, SPLIT_F):
                split_load(i)
            context_load(CTE[0:DC + 1, :], 0, t["ctxT"], S["e_ctx"])
            with sp.Fori(1, B) as b:
                sp.wait_ge(S["e_v"], b)
                context_load(CTE[0:DC + 1, :], b, t["ctxT"], S["e_ctx"])
            sp.wait_ge(layer_done[5], B)
            sp.dma_start(out, X[:, :]).then_inc(out_stored, 16)
            sp.wait_ge(out_stored, 16)

        @block.gpsimd
        def _(pool):
            po = Own(pool, pool_own)
            nc.gpsimd.memset(halves[:, :], -0.5)
            po.did(nc.gpsimd.memset(sm[:, 1022:1023], 0.0))
            po.wait()
            po.base, po.k = 1, 0

            def split(i):
                (name, parts, cols, hi, lo), after = splits[i]
                if after is not None:
                    pool.wait_ge(layer_done[after], B)
                pool.wait_ge(S[f"w_in{i % 2}"], 16 * (i // 2 + 1))
                src = stage[i % 2][0:parts, 0:cols]
                nc.gpsimd.tensor_copy(hi[0:parts, 0:cols], src).then_inc(S["w_split"], 1)
                pool.wait_ge(S["w_split"], 2 * i + 1)
                nc.gpsimd.tensor_tensor(lo[0:parts, 0:cols], src, hi[0:parts, 0:cols].bitcast(f32),
                                        ALU.subtract).then_inc(S["w_split"], 1)

            for i in range(SPLIT_A):
                split(i)
            with pool.Fori(0, B) as b:
                po.loop(b, 1)
                front_pool(pool, po, fronts[0], b)
            po.end(B)
            for i in range(SPLIT_A, SPLIT_C):
                split(i)
            pool.wait_ge(layer_done[0], B)
            with pool.Fori(0, B) as b:
                po.loop(b, 4)
                wait_alone(pool, S["b_var"], 2 * b + 1)
                po.did(nc.gpsimd.tensor_scalar(vs[:, 2:6], mv3[:, 2:6, 1], LN_EPS, None, ALU.add))
                po.wait()
                nc.gpsimd.tensor_tensor(rs[:, 2:6], vs[:, 2:6], halves[:, 0:4], ALU.pow).then_inc(S["b_rstd"], 1)
                front_pool(pool, po, fronts[1], b)
                wait_alone(pool, S["b_var"], 2 * b + 2)
                po.did(nc.gpsimd.tensor_scalar(vs[:, 6:8], mv3[:, 6:8, 1], LN_EPS, None, ALU.add))
                po.wait()
                nc.gpsimd.tensor_tensor(rs[:, 6:8], vs[:, 6:8], halves[:, 0:2], ALU.pow).then_inc(S["b_rstd"], 1)
                wait_alone(pool, S["b_ss"], b + 1)
                po.did(nc.gpsimd.tensor_scalar(sm[:, 16:32], sm[:, 0:16], 1.0 / EX, 1e-16, ALU.mult, ALU.max))
                po.wait()
                nc.gpsimd.tensor_tensor(sm[:, 32:48], sm[:, 16:32], halves[:, 0:16], ALU.pow).then_inc(S["b_rr"], 1)
            po.end(B)
            for layer in (2, 3, 4, 5):
                if layer == 3:
                    for i in range(SPLIT_C, SPLIT_E):
                        split(i)
                if layer == 4:
                    for i in range(SPLIT_E, SPLIT_F):
                        split(i)
                pool.wait_ge(layer_done[layer - 1], B)
                if layer == 4:
                    pool.wait_ge(loaded["e"], 16 * len(plain["e"]))
                    nc.gpsimd.memset(VO[:, :], 0.0).then_inc(S["e_vo0"], 1)
                    pool.wait_ge(S["e_vo0"], 1)
                    nc.gpsimd.memset(VO[:, :].rearrange("p (h c) -> p h c", c=32)[:, :, EY:2 * EY], 1.0)
                    nc.gpsimd.memset(NMX[:, :], 0.0).then_inc(S["e_vo0"], 1)
                with pool.Fori(0, B) as b:
                    po.loop(b, 1)
                    if layer == 4:
                        wait_alone(pool, S["e_ctx"], 16 * b + 16)
                        nc.gpsimd.tensor_copy(CEH[0:DC + 1, :], CTE[0:DC + 1, :]).then_inc(S["e_split"], 1)
                        wait_alone(pool, S["e_split"], 2 * b + 1)
                        nc.gpsimd.tensor_tensor(CEL[0:DC + 1, :], CTE[0:DC + 1, :], CEH[0:DC + 1, :].bitcast(f32),
                                                ALU.subtract).then_inc(S["e_split"], 1)
                    front_pool(pool, po, fronts[layer], b)
                    if layer == 4:
                        for g in range(4):
                            wait_alone(pool, S["e_qs"], 8 * b + 2 * g + 2)
                            for j in range(4):
                                h = 4 * g + j
                                last = nc.gpsimd.tensor_scalar(QM[:, h * N:(h + 1) * N], QSt[:, :], hmask[:, j:j + 1],
                                                               None, ALU.mult)
                            last.then_inc(S["e_qm"], 1)
                po.end(B)

        @block.tensor
        def _(pe):
            pe.wait_ge(S["qk_in"], 32)
            pe.wait_ge(consts_loaded, 32)
            for q in range(4):
                for i in range(4):
                    h = 4 * q + i
                    last = mm(PB[q][:, i * D:(i + 1) * D], stage[0][0:EA, h * D:(h + 1) * D],
                              stage[1][0:EA, h * D:(h + 1) * D])
                last.then_inc(S["a_mready"], 1)
            pe.wait_ge(S["a_ml"], 4)
            pe.wait_ge(S["w_split"], 2 * SPLIT_A)
            pe.wait_ge(loaded["a"], 16 * len(plain["a"]))
            with pe.Fori(0, B) as b:
                F = fronts[0]
                front_tensor(pe, F, b)
                pe.wait_ge(F.xh_ready, b + 1)
                pe.wait_ge(F.xl_ready, b + 1)
                for u in range(4):
                    mt, half = u // 2, u % 2
                    if u == 3:
                        pe.wait_ge(S["a_vc"], 4 * b + 1)
                    cs = slice(half * 512, half * 512 + 512)
                    mm3(PB[5 + u % 3][:, :], XH[:, mt * P:(mt + 1) * P], XL[:, mt * P:(mt + 1) * P], WVH[:, cs],
                        WVL[:, cs]).then_inc(S["a_v"], 1)

                def project(p):
                    if p >= 1:
                        pe.wait_ge(S["a_gl"], 8 * b + p)
                    for i in range(2):
                        hs = slice((2 * p + i) * D, (2 * p + i + 1) * D)
                        last = mm3(PB[4][:, i * N:(i + 1) * N], MH[:, hs], ML[:, hs], XH[:, :], XL[:, :])
                    last.then_inc(S["a_g"], 1)

                def scores(h):
                    if h % 2 == 0:
                        pe.wait_ge(S["a_gl"], 8 * b + h // 2 + 1)
                    if h >= 2:
                        pe.wait_ge(S["a_exp"], 16 * b + h - 1)
                    gh, gl = GH[h // 2 % 2], GL[h // 2 % 2]
                    for i in range(NT):
                        cs = slice(h % 2 * N + i * P, h % 2 * N + (i + 1) * P)
                        last = mm3(PB[h % 2][:, i * N:(i + 1) * N], gh[:, cs], gl[:, cs], XH[:, :], XL[:, :])
                    last.then_inc(S["a_s"], 1)

                def turn(h):
                    pe.wait_ge(S["a_exp"], 16 * b + h + 1)
                    if h >= 2:
                        pe.wait_ge(S["a_ptc"], 16 * b + h - 1)
                    for mt in range(NT):
                        for i in range(NT):
                            last = nc.tensor.transpose(
                                PB[2 + h % 2][:, mt * N + i * P:mt * N + (i + 1) * P],
                                PA[h % 2][:, i * N + mt * P:i * N + (mt + 1) * P], ident[:, :])
                    last.then_inc(S["a_pt"], 1)

                def weigh(h):
                    pe.wait_ge(S["a_ptc"], 16 * b + h + 1)
                    if h == 0:
                        pe.wait_ge(S["a_vc"], 4 * b + 4)
                    if h == 8:
                        pe.wait_ge(S["a_on"], 2 * b + 1)
                    for i in range(NT):
                        for mt in range(NT):
                            last = mm(PB[5 + i][:, h % 8 * EA:(h % 8 + 1) * EA],
                                      PTA[h % 2][:, mt * N + i * P:mt * N + (i + 1) * P],
                                      VA[:, mt * HA * EA + h * EA:mt * HA * EA + (h + 1) * EA],
                                      first=mt == 0, last=mt == NT - 1)
                    if h % 8 == 7:
                        last.then_inc(S["a_o"], 1)

                def turn_out(q):
                    pe.wait_ge(S["a_on"], 2 * b + q // 2 + 1)
                    if q >= 1:
                        pe.wait_ge(S["a_otc"], 4 * b + q)
                    for k in range(2):
                        for i in range(NT):
                            c0 = i * HA * EA + (2 * q + k) * P
                            last = nc.tensor.transpose(PB[7][:, k * N + i * P:k * N + (i + 1) * P], ONA[:, c0:c0 + P],
                                                       ident[:, :])
                    last.then_inc(S["a_ot"], 1)

                project(0)
                for s in range(HA + 2):
                    if s < HA:
                        scores(s)
                        if s % 2 == 0 and s + 2 < HA:
                            project(s // 2 + 1)
                    if 1 <= s <= HA:
                        turn(s - 1)
                    if s >= 2:
                        weigh(s - 2)
                    if s in (12, 14):
                        turn_out((s - 12) // 2)
                turn_out(2)
                turn_out(3)
                pe.wait_ge(S["a_otc"], 4 * b + 4)
                for i in range(NT):
                    o = PB[5][:, i * D:(i + 1) * D]
                    for k in range(HA * EA // P):
                        mm(o, OTA[:, k * N + i * P:k * N + (i + 1) * P], WP[:, k * D:(k + 1) * D], first=k == 0,
                           last=False)
                    last = mm(o, onesrow[:, :], bp[:, :], first=False)
                last.then_inc(S["a_y"], 1)

            pe.wait_ge(layer_done[0], B)
            pe.wait_ge(loaded["x"], 16 * len(plain["x"]))
            with pe.Fori(0, B) as b:
                pe.wait_ge(S["b_cn"], b + 1)
                for i in range(MT):
                    nc.tensor.transpose(PB[6][0:DC, i * P:(i + 1) * P], CN[:, i * DC:(i + 1) * DC], ident[:, :])
                pe.wait_ge(S["b_ln2"], b + 1)
                for i in range(NT):
                    last = nc.tensor.transpose(PB[7][:, i * P:(i + 1) * P], LN2[:, i * D:(i + 1) * D], ident[:, :])
                last.then_inc(S["b_lt"], 1)
                pe.wait_ge(S["b_ltc"], b + 1)
                for i in range(NT):
                    mm(PB[0][:, i * D:(i + 1) * D], LT[:, i * P:(i + 1) * P], WQX[:, :])
                for i in range(MT):
                    mm(PB[2 + i // 2][:, i % 2 * 2 * D:(i % 2 + 1) * 2 * D], CXT[0:DC, i * P:(i + 1) * P], WKVX[0:DC, :])
                for i in range(NT):
                    last = mm(PB[1][:, i * 2 * D:(i + 1) * 2 * D], LT[:, i * P:(i + 1) * P], WLKV[:, :])
                last.then_inc(S["b_qkv"], 1)
                pe.wait_ge(S["b_qkn"], b + 1)
                for i in range(NT):
                    nc.tensor.transpose(PB[7][:, i * P:(i + 1) * P], QKN[:, i * D:(i + 1) * D], ident[:, :])
                for i in range(6):
                    last = nc.tensor.transpose(PB[4 + i // 4][:, i % 4 * P:(i % 4 + 1) * P],
                                               QKN[:, (2 + i) * D:(3 + i) * D], ident[:, :])
                last.then_inc(S["b_qkt"], 1)
                pe.wait_ge(S["b_qktc"], b + 1)
                pe.wait_ge(S["b_mk"], b + 1)
                pe.wait_ge(S["b_v"], b + 1)

                def scores(u):
                    hd, i = u // NT, u % NT
                    r = slice(hd * EX, (hd + 1) * EX)
                    if u >= 2:
                        pe.wait_ge(S["b_exp"], 4 * b + u - 1)
                    lo, hi = PB[2 * (u % 2)], PB[2 * (u % 2) + 1]
                    mm(lo[:, :], QTX[r, i * P:(i + 1) * P], KTX[r, 0:M], last=False)
                    mm(lo[:, :], onesrow[:, :], mkb[:, :], first=False)
                    mm(hi[:, 0:N], QTX[r, i * P:(i + 1) * P], KTX[r, M:TK]).then_inc(S["b_s"], 1)

                scores(0)
                for u in range(4):
                    if u < 3:
                        scores(u + 1)
                    hd, i = u // NT, u % NT
                    pe.wait_ge(S["b_exp"], 4 * b + u + 1)
                    for mt in range(6):
                        last = nc.tensor.transpose(PB[4 + mt // 4][:, mt % 4 * P:(mt % 4 + 1) * P],
                                                   PX[u % 2][:, mt * P:(mt + 1) * P], ident[:, :])
                    last.then_inc(S["b_pt"], 1)
                    pe.wait_ge(S["b_ptc"], 4 * b + u + 1)
                    for mt in range(6):
                        last = mm(PB[6][:, i * D + hd * EX:i * D + (hd + 1) * EX], PTX[:, mt * P:(mt + 1) * P],
                                  VX[:, mt * D + hd * EX:mt * D + (hd + 1) * EX], first=mt == 0, last=mt == 5)
                last.then_inc(S["b_o"], 1)
                pe.wait_ge(S["b_on"], b + 1)
                for i in range(NT):
                    last = nc.tensor.transpose(PB[7][:, i * P:(i + 1) * P], ONX[:, i * D:(i + 1) * D], ident[:, :])
                last.then_inc(S["b_ot"], 1)
                pe.wait_ge(S["b_otc"], b + 1)
                for i in range(NT):
                    mm(PB[7][:, N + i * D:N + (i + 1) * D], OTX[:, i * P:(i + 1) * P], WOX[:, :], last=False)
                    last = mm(PB[7][:, N + i * D:N + (i + 1) * D], onesrow[:, :], boX[:, :], first=False)
                last.then_inc(S["b_y"], 1)

            def experts(layer, names, inner, wr, nexp, up, ups, gate, gates, down):
                r, hs, sg, h2s, ys, yd = names
                F = fronts[layer]
                pairs = len(inner)
                with pe.Fori(0, B) as b:
                    front_tensor(pe, F, b)
                    pe.wait_ge(F.xh_ready, b + 1)
                    pe.wait_ge(F.xl_ready, b + 1)
                    for i in range(NT):
                        last = mm(PB[6][:, i * 32:i * 32 + nexp], XF2[:, i * P:(i + 1) * P], wr[:, 0:nexp])
                    last.then_inc(S[r], 1)

                    def hidden(q):
                        n = inner[q][0]
                        if q >= 2:
                            pe.wait_ge(S[h2s], pairs * b + q - 1)
                        for k in range(n):
                            cs = slice((2 * q + k) * P, (2 * q + k + 1) * P)
                            mm3(PB[2 * (q % 2)][:, k * N:(k + 1) * N], gate[:, cs], gates[:, cs], XH[:, :], XL[:, :])
                        for k in range(n):
                            cs = slice((2 * q + k) * P, (2 * q + k + 1) * P)
                            last = mm3(PB[2 * (q % 2) + 1][:, k * N:(k + 1) * N], up[:, cs], ups[:, cs], XH[:, :],
                                       XL[:, :])
                        last.then_inc(S[hs], 1)

                    hidden(0)
                    for q in range(pairs):
                        if q + 1 < pairs:
                            hidden(q + 1)
                        pe.wait_ge(S[h2s], pairs * b + q + 1)
                        if q >= 2:
                            pe.wait_ge(S[yd], (pairs - 1) * b + q - 1)
                        n, joint = inner[q]
                        y = PB[4 + q % 2]
                        for i in range(NT):
                            for k in range(n):
                                o = y[:, i * D:(i + 1) * D] if joint else y[:, (k * NT + i) * D:(k * NT + i + 1) * D]
                                last = mm(o, H2[q % 2][:, k * N + i * P:k * N + (i + 1) * P],
                                          down[:, (2 * q + k) * D:(2 * q + k + 1) * D],
                                          first=k == 0 or not joint, last=k == n - 1 or not joint)
                        last.then_inc(S[ys], 1)

            pe.wait_ge(layer_done[1], B)
            pe.wait_ge(S["w_split"], 2 * SPLIT_C)
            pe.wait_ge(loaded["c"], 16 * len(plain["c"]))
            experts(2, ("c_r", "c_h", "c_sg", "c_h2", "c_y", "c_yd"), [(2, True)] * E0, WGC, E0, W3H, W3L, W1H,
                    W1L, W2C)

            pe.wait_ge(layer_done[2], B)
            pe.wait_ge(loaded["d"], 16 * len(plain["d"]))
            with pe.Fori(0, B) as b:
                F = fronts[3]
                front_tensor(pe, F, b)
                pe.wait_ge(F.xh_ready, b + 1)
                mm(PB[0][:, 0:N], WQD[:, :], XF[:, :])
                mm(PB[0][:, N:2 * N], WKD[:, :], XF[:, :]).then_inc(S["d_q"], 1)
                for i in range(NT):
                    mm(PB[1][:, i * D:(i + 1) * D], XF[:, i * P:(i + 1) * P], WVD[:, :], last=False)
                    last = mm(PB[1][:, i * D:(i + 1) * D], onesrow[:, :], bvD[:, :], first=False)
                last.then_inc(S["d_v"], 1)
                pe.wait_ge(S["d_qc"], b + 1)
                for i in range(NT):
                    last = mm(PB[2][:, i * N:(i + 1) * N], QD[:, i * P:(i + 1) * P], KD[:, :])
                last.then_inc(S["d_s"], 1)
                pe.wait_ge(S["d_exp"], b + 1)
                for mt in range(NT):
                    for i in range(NT):
                        last = nc.tensor.transpose(PB[3][:, mt * N + i * P:mt * N + (i + 1) * P],
                                                   PD[:, i * N + mt * P:i * N + (mt + 1) * P], ident[:, :])
                last.then_inc(S["d_pt"], 1)
                pe.wait_ge(S["d_ptc"], b + 1)
                pe.wait_ge(S["d_vc"], b + 1)
                for i in range(NT):
                    for mt in range(NT):
                        last = mm(PB[4][:, i * D:(i + 1) * D], PTD[:, mt * N + i * P:mt * N + (i + 1) * P],
                                  VD[:, mt * D:(mt + 1) * D], first=mt == 0, last=mt == NT - 1)
                last.then_inc(S["d_o"], 1)
                pe.wait_ge(S["d_on"], b + 1)
                for i in range(NT):
                    last = nc.tensor.transpose(PB[5][:, i * P:(i + 1) * P], OND[:, i * D:(i + 1) * D], ident[:, :])
                last.then_inc(S["d_ot"], 1)
                pe.wait_ge(S["d_otc"], b + 1)
                for i in range(NT):
                    mm(PB[6][:, i * D:(i + 1) * D], OTD[:, i * P:(i + 1) * P], WOD[:, :], last=False)
                    last = mm(PB[6][:, i * D:(i + 1) * D], onesrow[:, :], boD[:, :], first=False)
                last.then_inc(S["d_y"], 1)

            pe.wait_ge(layer_done[3], B)
            pe.wait_ge(S["w_split"], 2 * SPLIT_E)
            pe.wait_ge(loaded["e"], 16 * len(plain["e"]))
            pe.wait_ge(S["e_vo0"], 2)
            with pe.Fori(0, B) as b:
                F = fronts[4]
                pe.wait_ge(S["e_split"], 2 * b + 2)
                for g in range(4):
                    cs = slice(g * P, (g + 1) * P)
                    if g >= 2:
                        pe.wait_ge(S["e_ks"], 4 * b + g - 1)
                    mm3(PB[g % 2][:, :], WKSH[0:DC + 1, cs], WKSL[0:DC + 1, cs], CEH[0:DC + 1, :],
                        CEL[0:DC + 1, :]).then_inc(S["e_k"], 1)
                for i in range(MT):
                    last = mm(PB[6][:, i * D:(i + 1) * D], CTE[0:DC + 1, i * P:(i + 1) * P], WVE[0:DC + 1, :])
                last.then_inc(S["e_v"], 1)
                front_tensor(pe, F, b)
                pe.wait_ge(F.xh_ready, b + 1)
                pe.wait_ge(F.xl_ready, b + 1)
                for g in range(4):
                    cs = slice(g * P, (g + 1) * P)
                    if g >= 2:
                        pe.wait_ge(S["e_qc"], 4 * b + g - 1)
                    mm3(PB[4 + g % 2][:, 0:N], WQSH[:, cs], WQSL[:, cs], XH[:, :], XL[:, :]).then_inc(S["e_q"], 1)

                pe.wait_ge(S["e_ks"], 4 * b + 4)
                pe.wait_ge(S["e_qc"], 4 * b + 4)

                def scores(g):
                    pe.wait_ge(S["e_qm"], 4 * b + g + 1)
                    for j in range(4):
                        h = 4 * g + j
                        for i in range(NT):
                            n = 8 * g + 2 * j + i
                            if n >= 3:
                                pe.wait_ge(S["e_max"], 32 * b + n - 2)
                            mm(PB[n % 3][:, :], QM[:, h * N + i * P:h * N + (i + 1) * P],
                               KS[:, g * M:(g + 1) * M]).then_inc(S["e_s"], 1)
                def rows(g):
                    pe.wait_ge(S["e_max"], 32 * b + 8 * g + 8)
                    for i in range(NT):
                        last = nc.tensor.transpose(PB[7][:, i * P:(i + 1) * P], NMX[:, i * P:(i + 1) * P], ident[:, :])
                    last.then_inc(S["e_nr"], 1)

                def turned_scores(g):
                    pe.wait_ge(S["e_nm"], 4 * b + g + 1)
                    for j in range(4):
                        h = 4 * g + j
                        for k in range(2):
                            n = 8 * g + 2 * j + k
                            if n >= 3:
                                pe.wait_ge(S["e_exp"], 32 * b + n - 2)
                            for q in range(2):
                                mt = 2 * k + q
                                last = mm(PB[3 + n % 3][:, q * N:(q + 1) * N],
                                          KS[:, g * M + mt * P:g * M + (mt + 1) * P], QM[:, h * N:(h + 1) * N])
                            last.then_inc(S["e_st"], 1)

                def weigh(g):
                    pe.wait_ge(S["e_exp"], 32 * b + 8 * g + 8)
                    if g == 0:
                        pe.wait_ge(S["e_vc"], b + 1)
                    else:
                        pe.wait_ge(S["e_uc"], 4 * b + g)
                    for mt in range(MT):
                        for j in range(4):
                            h = 4 * g + j
                            last = mm(PB[6][32 * j:32 * j + 32, 0:N], VO[:, (mt * HY + h) * 32:(mt * HY + h + 1) * 32],
                                      PTE[g % 2][:, (j * MT + mt) * N:(j * MT + mt + 1) * N], first=mt == 0,
                                      last=mt == MT - 1)
                    last.then_inc(S["e_u"], 1)

                scores(0)
                for g in range(4):
                    rows(g)
                    if g < 3:
                        scores(g + 1)
                    turned_scores(g)
                    if g >= 1:
                        weigh(g - 1)
                weigh(3)
                pe.wait_ge(S["e_uc"], 4 * b + 4)
                for g in range(4):
                    mm(PB[6][:, 0:N], CU[:, g * P:(g + 1) * P], UD[:, g * N:(g + 1) * N], first=g == 0, last=g == 3)
                for g in range(4):
                    last = mm(PB[6][:, N:2 * N], CD[:, g * P:(g + 1) * P], UD[:, g * N:(g + 1) * N], first=g == 0,
                              last=g == 3)
                last.then_inc(S["e_od"], 1)
                pe.wait_ge(S["e_o"], b + 1)
                for k in range(2):
                    last = mm(PB[3][:, k * N:(k + 1) * N], W1E[:, k * P:(k + 1) * P], OE[:, :])
                last.then_inc(S["e_h"], 1)
                pe.wait_ge(S["e_hc"], b + 1)
                for i in range(NT):
                    for k in range(2):
                        mm(PB[4][:, i * D:(i + 1) * D], H1E[:, k * N + i * P:k * N + (i + 1) * P],
                           W2E[:, k * D:(k + 1) * D], first=k == 0, last=False)
                    last = mm(PB[4][:, i * D:(i + 1) * D], onesrow[:, :], b2E[:, :], first=False)
                last.then_inc(S["e_y"], 1)

            pe.wait_ge(layer_done[4], B)
            pe.wait_ge(S["w_split"], 2 * SPLIT_F)
            pe.wait_ge(loaded["f"], 16 * len(plain["f"]))
            experts(5, ("f_r", "f_h", "f_sg", "f_h2", "f_y", "f_yd"), [(2, False)] * (E1 // 2) + [(1, False)],
                    WGF, E1, FUH, FUL, FGH, FGL, FD)

        @block.scalar
        def _(act):
            for q in range(4):
                act.wait_ge(S["a_mready"], q + 1)
                nc.scalar.activation(MH[:, q * 512:(q + 1) * 512], PB[q][:, :], ACT.Copy,
                                     scale=1.0 / math.sqrt(EA)).then_inc(S["a_mh"], 1)
            with act.Fori(0, B) as b:
                front_scalar(act, fronts[0], b)
                for u in range(4):
                    act.wait_ge(S["a_v"], 4 * b + u + 1)
                    mt, half = u // 2, u % 2
                    nc.scalar.activation(VA[:, mt * HA * EA + half * 512:mt * HA * EA + (half + 1) * 512],
                                         PB[5 + u % 3][:, :], ACT.Copy).then_inc(S["a_vc"], 1)

                def high(p):
                    act.wait_ge(S["a_g"], 8 * b + p + 1)
                    nc.scalar.activation(GH[p % 2][:, :], PB[4][:, :], ACT.Copy).then_inc(S["a_gh"], 1)

                high(0)
                for h in range(HA):
                    if h % 2 == 0 and h + 2 < HA:
                        high(h // 2 + 1)
                    act.wait_ge(S["a_max"], 16 * b + h + 1)
                    for i in range(NT):
                        last = nc.scalar.activation(PA[h % 2][:, i * N:(i + 1) * N], PB[h % 2][:, i * N:(i + 1) * N],
                                                    ACT.Exp, bias=sm[:, 128 + 2 * h + i:129 + 2 * h + i],
                                                    accum_out=sm[:, 192 + i * HA + h:193 + i * HA + h])
                    last.then_inc(S["a_exp"], 1)
                    if h in (12, 14):
                        q = (h - 12) // 2
                        act.wait_ge(S["a_ot"], 4 * b + q + 1)
                        nc.scalar.activation(OTA[:, q * 512:(q + 1) * 512], PB[7][:, :],
                                             ACT.Copy).then_inc(S["a_otc"], 1)
                for q in (2, 3):
                    act.wait_ge(S["a_ot"], 4 * b + q + 1)
                    nc.scalar.activation(OTA[:, q * 512:(q + 1) * 512], PB[7][:, :], ACT.Copy).then_inc(S["a_otc"], 1)

            act.wait_ge(loaded["x"], 16 * len(plain["x"]))
            with act.Fori(0, B) as b:
                act.wait_ge(S["b_lt"], b + 1)
                nc.scalar.activation(CXT[0:DC, :], PB[6][0:DC, :], ACT.Identity, scale=gcol[0:DC, 0:1],
                                     bias=gcol[0:DC, 1:2])
                nc.scalar.activation(LT[:, :], PB[7][:, 0:N], ACT.Identity, scale=gcol[:, 2:3],
                                     bias=gcol[:, 3:4]).then_inc(S["b_ltc"], 1)
                act.wait_ge(S["b_qkv"], b + 1)
                nc.scalar.activation(SQ[:, 0:2 * D], PB[0][:, 0:2 * D], ACT.Square)
                for k, bank in ((0, 2), (2, 3), (4, 1)):
                    src = PB[bank][:, :].rearrange("p (t c) -> p t c", c=2 * D)
                    dst = SQ[:, (2 + k) * D:(4 + k) * D].rearrange("p (t c) -> p t c", c=D)
                    last = nc.scalar.activation(dst, src[:, :, 0:D], ACT.Square)
                last.then_inc(S["b_sq"], 1)
                for k, bank in ((0, 2), (2, 3), (4, 1)):
                    src = PB[bank][:, :].rearrange("p (t c) -> p t c", c=2 * D)
                    dst = VX[:, k * D:(2 + k) * D].rearrange("p (t c) -> p t c", c=D)
                    last = nc.scalar.activation(dst, src[:, :, D:2 * D], ACT.Copy)
                last.then_inc(S["b_v"], 1)
                act.wait_ge(S["b_qkt"], b + 1)
                nc.scalar.activation(QTX[:, :], PB[7][:, 0:N], ACT.Copy, scale=gcol[:, 4:5])
                nc.scalar.activation(KTX[:, 0:M], PB[4][:, :], ACT.Copy, scale=gcol[:, 5:6])
                nc.scalar.activation(KTX[:, M:TK], PB[5][:, 0:N], ACT.Copy, scale=gcol[:, 5:6]).then_inc(S["b_qktc"], 1)
                for u in range(4):
                    act.wait_ge(S["b_max"], 4 * b + u + 1)
                    k = 2 * (u % 2)
                    nc.scalar.activation(PX[u % 2][:, 0:M], PB[k][:, :], ACT.Exp, scale=1.0 / math.sqrt(EX),
                                         bias=sm[:, 64 + u:65 + u], accum_out=sm[:, 68 + u:69 + u])
                    nc.scalar.activation(PX[u % 2][:, M:TK], PB[k + 1][:, 0:N], ACT.Exp, scale=1.0 / math.sqrt(EX),
                                         bias=sm[:, 64 + u:65 + u],
                                         accum_out=sm[:, 72 + u:73 + u]).then_inc(S["b_exp"], 1)
                act.wait_ge(S["b_ot"], b + 1)
                nc.scalar.activation(OTX[:, :], PB[7][:, 0:N], ACT.Copy).then_inc(S["b_otc"], 1)

            def experts(layer, names, inner):
                r, hs, sg, h2s, ys, yd = names
                F = fronts[layer]
                pairs = len(inner)
                with act.Fori(0, B) as b:
                    act.wait_ge(F.xt_ready, b + 1)
                    nc.scalar.activation(XF2[:, :], PB[BANK_X][:, 0:N], ACT.Copy)
                    nc.scalar.activation(XH[:, :], PB[BANK_X][:, 0:N], ACT.Copy).then_inc(F.xh_ready, 1)
                    if layer == 5:
                        act.wait_ge(S["f_r"], b + 1)
                        for i in range(NT):
                            last = nc.scalar.activation(gt[:, i * E1:(i + 1) * E1], PB[6][:, i * 32:i * 32 + E1],
                                                        ACT.Sigmoid)
                        last.then_inc(S["f_sig"], 1)
                    else:
                        act.wait_ge(S["c_xf"], b + 1)
                        nc.scalar.activation(gt[:, 96:96 + 2 * E0], gt[:, 64:64 + 2 * E0],
                                             ACT.Sigmoid).then_inc(S["c_sig"], 1)
                    for q in range(pairs):
                        n = inner[q][0]
                        act.wait_ge(S[hs], pairs * b + q + 1)
                        nc.scalar.activation(SG[q % 2][:, 0:n * N], PB[2 * (q % 2)][:, 0:n * N],
                                             ACT.Silu).then_inc(S[sg], 1)

            act.wait_ge(layer_done[1], B)
            experts(2, ("c_r", "c_h", "c_sg", "c_h2", "c_y", "c_yd"), [(2, True)] * E0)

            act.wait_ge(layer_done[2], B)
            act.wait_ge(loaded["d"], 16 * len(plain["d"]))
            with act.Fori(0, B) as b:
                F = fronts[3]
                act.wait_ge(F.xt_ready, b + 1)
                nc.scalar.activation(XF[:, :], PB[BANK_X][:, 0:N], ACT.Copy).then_inc(F.xh_ready, 1)
                act.wait_ge(S["d_q"], b + 1)
                nc.scalar.activation(QD[:, :], PB[0][:, 0:N], ACT.Identity, bias=bqk[:, 0:1])
                nc.scalar.activation(KD[:, :], PB[0][:, N:2 * N], ACT.Identity, bias=bqk[:, 1:2]).then_inc(S["d_qc"], 1)
                act.wait_ge(S["d_v"], b + 1)
                nc.scalar.activation(VD[:, :], PB[1][:, 0:N], ACT.Copy).then_inc(S["d_vc"], 1)
                act.wait_ge(S["d_max"], b + 1)
                for i in range(NT):
                    last = nc.scalar.activation(PD[:, i * N:(i + 1) * N], PB[2][:, i * N:(i + 1) * N], ACT.Exp,
                                                scale=1.0 / math.sqrt(D), bias=sm[:, 64 + i:65 + i],
                                                accum_out=sm[:, 68 + i:69 + i])
                last.then_inc(S["d_exp"], 1)
                act.wait_ge(S["d_ot"], b + 1)
                nc.scalar.activation(OTD[:, :], PB[5][:, 0:N], ACT.Copy).then_inc(S["d_otc"], 1)

            act.wait_ge(layer_done[3], B)
            act.wait_ge(loaded["e"], 16 * len(plain["e"]))
            act.wait_ge(S["e_vo0"], 2)
            with act.Fori(0, B) as b:
                for g in range(4):
                    act.wait_ge(S["e_k"], 4 * b + g + 1)
                    nc.scalar.activation(KHt[:, :].bitcast(f32r), PB[g % 2][:, :], ACT.Copy).then_inc(S["e_kh"], 1)
                    act.wait_ge(S["e_ks"], 4 * b + g + 1)
                act.wait_ge(S["e_v"], b + 1)
                for i in range(MT):
                    dst = VO[:, i * HY * 32:(i + 1) * HY * 32].rearrange("p (h c) -> p h c", c=32)[:, :, 0:EY]
                    src = PB[6][:, i * D:(i + 1) * D].rearrange("p (h c) -> p h c", c=EY)
                    last = nc.scalar.activation(dst, src, ACT.Copy)
                last.then_inc(S["e_vc"], 1)
                front_scalar(act, fronts[4], b)
                for g in range(4):
                    act.wait_ge(S["e_q"], 4 * b + g + 1)
                    if g >= 1:
                        act.wait_ge(S["e_qs"], 8 * b + 2 * g)
                    nc.scalar.activation(QT0[:, :], PB[4 + g % 2][:, 0:N], ACT.Identity,
                                         bias=bqs[:, g:g + 1]).then_inc(S["e_qc"], 1)
                for g in range(4):
                    for j in range(4):
                        for k in range(2):
                            n = 8 * g + 2 * j + k
                            act.wait_ge(S["e_st"], 32 * b + n + 1)
                            nc.scalar.activation(PTE[g % 2][:, (j * MT + 2 * k) * N:(j * MT + 2 * k + 2) * N],
                                                 PB[3 + n % 3][:, :], ACT.Exp,
                                                 scale=1.0 / math.sqrt(EY)).then_inc(S["e_exp"], 1)
                    if g >= 1:
                        act.wait_ge(S["e_u"], 4 * b + g)
                        nc.scalar.activation(UD[:, (g - 1) * N:g * N], PB[6][:, 0:N], ACT.Copy).then_inc(S["e_uc"], 1)
                act.wait_ge(S["e_u"], 4 * b + 4)
                nc.scalar.activation(UD[:, 3 * N:4 * N], PB[6][:, 0:N], ACT.Copy).then_inc(S["e_uc"], 1)
                act.wait_ge(S["e_h"], b + 1)
                for k in range(2):
                    last = nc.scalar.activation(H1E[:, k * N:(k + 1) * N], PB[3][:, k * N:(k + 1) * N], ACT.Relu,
                                                bias=b1E[:, k:k + 1])
                last.then_inc(S["e_hc"], 1)

            act.wait_ge(layer_done[4], B)
            experts(5, ("f_r", "f_h", "f_sg", "f_h2", "f_y", "f_yd"), [(2, False)] * (E1 // 2) + [(1, False)])

        @block.vector
        def _(dve):
            o = Own(dve, own)

            def add_to_x(b, src, layer):
                nc.vector.tensor_tensor(Xt[:, bass.ds(b * NT, NT), :], Xt[:, bass.ds(b * NT, NT), :],
                                        src.rearrange("p (t d) -> p t d", d=D), ALU.add).then_inc(layer_done[layer], 1)

            for q in range(4):
                dve.wait_ge(S["a_mh"], q + 1)
                nc.vector.scalar_tensor_tensor(out=ML[:, q * 512:(q + 1) * 512], in0=PB[q][:, :],
                                               scalar=1.0 / math.sqrt(EA), in1=MH[:, q * 512:(q + 1) * 512].bitcast(f32),
                                               op0=ALU.mult, op1=ALU.subtract).then_inc(S["a_ml"], 1)
            dve.wait_ge(x_loaded, 16)
            with dve.Fori(0, B) as b:
                o.loop(b, 3)
                F = fronts[0]
                front_vector(dve, o, F, b)
                front_low(dve, F, b)

                def low(p):
                    dve.wait_ge(S["a_gh"], 8 * b + p + 1)
                    nc.vector.tensor_tensor(GL[p % 2][:, :], PB[4][:, :], GH[p % 2][:, :].bitcast(f32),
                                            ALU.subtract).then_inc(S["a_gl"], 1)

                def normalise(half):
                    dve.wait_ge(S["a_o"], 2 * b + half + 1)
                    for i in range(NT):
                        last = nc.vector.reciprocal(sm[:, 256 + i * HA + 8 * half:256 + i * HA + 8 * half + 8],
                                                    sm[:, 192 + i * HA + 8 * half:192 + i * HA + 8 * half + 8])
                    o.did(last)
                    o.wait()
                    for i in range(NT):
                        dst = ONA[:, i * HA * EA + half * 512:i * HA * EA + (half + 1) * 512]
                        rd = sm[:, 256 + i * HA + 8 * half:256 + i * HA + 8 * half + 8]
                        last = nc.vector.tensor_tensor(
                            dst.rearrange("p (h e) -> p h e", e=EA), PB[5 + i][:, :].rearrange("p (h e) -> p h e", e=EA),
                            rd.rearrange("p (h o) -> p h o", o=1).broadcast_to([P, 8, EA]), ALU.mult)
                    last.then_inc(S["a_on"], 1)

                low(0)
                for s in range(HA + 1):
                    if s < HA:
                        dve.wait_ge(S["a_s"], 16 * b + s + 1)
                        nc.vector.tensor_reduce(sm[:, 128 + 2 * s:130 + 2 * s],
                                                PB[s % 2][:, :].rearrange("p (t m) -> p t m", m=N), AX.X, ALU.max,
                                                negate=True).then_inc(S["a_max"], 1)
                        if s % 2 == 0 and s + 2 < HA:
                            low(s // 2 + 1)
                    if s >= 1:
                        dve.wait_ge(S["a_pt"], 16 * b + s)
                        nc.vector.tensor_copy(PTA[(s - 1) % 2][:, :], PB[2 + (s - 1) % 2][:, :]).then_inc(S["a_ptc"], 1)
                    if s == 10:
                        normalise(0)
                normalise(1)
                dve.wait_ge(S["a_y"], b + 1)
                add_to_x(b, PB[5][:, 0:N], 0)
            o.end(B)

            dve.wait_ge(layer_done[0], B)
            dve.wait_ge(loaded["x"], 16 * len(plain["x"]))
            with dve.Fori(0, B) as b:
                o.loop(b, 9)
                F = fronts[1]
                dve.wait_ge(S["b_ctx"], 32 * b + 32)
                for i in range(MT):
                    last = nc.vector.bn_stats(st3[:, 2 + i, :], CX[:, i * DC:(i + 1) * DC])
                o.did(last)
                o.wait_alone()
                for i in range(MT):
                    last = nc.vector.bn_aggr(mv3[:, 2 + i, :], st3[:, 2 + i, :])
                last.then_inc(S["b_var"], 1)
                dve.wait_ge(S["b_rstd"], 2 * b + 1)
                for i in range(MT):
                    last = nc.vector.tensor_scalar(CN[:, i * DC:(i + 1) * DC], CX[:, i * DC:(i + 1) * DC],
                                                   mv3[:, 2 + i, 0:1], rs[:, 2 + i:3 + i], ALU.subtract, ALU.mult)
                nc.vector.tensor_scalar(mkb[:, :], mk8[:, :], -1.0, 1e30, ALU.add,
                                        ALU.mult).then_inc(S["b_mk"], 1)
                last.then_inc(S["b_cn"], 1)
                front_vector(dve, o, F, b)
                dve.wait_ge(F.xn_ready, b + 1)
                for i in range(NT):
                    last = nc.vector.bn_stats(st3[:, 6 + i, :], xn3[:, i, :])
                o.did(last)
                o.wait_alone()
                for i in range(NT):
                    last = nc.vector.bn_aggr(mv3[:, 6 + i, :], st3[:, 6 + i, :])
                last.then_inc(S["b_var"], 1)
                dve.wait_ge(S["b_rstd"], 2 * b + 2)
                for i in range(NT):
                    last = nc.vector.tensor_scalar(LN2[:, i * D:(i + 1) * D], xn3[:, i, :], mv3[:, 6 + i, 0:1],
                                                   rs[:, 6 + i:7 + i], ALU.subtract, ALU.mult)
                last.then_inc(S["b_ln2"], 1)
                dve.wait_ge(S["b_sq"], b + 1)
                nc.vector.reduce_sum(sm[:, 0:16], SQ[:, :].rearrange("p (n e) -> p n e", e=EX), AX.X).then_inc(S["b_ss"], 1)
                dve.wait_ge(S["b_rr"], b + 1)
                dve.wait_ge(S["b_v"], b + 1)
                last = nc.vector.tensor_tensor(
                    QKN[:, 0:2 * D].rearrange("p (n e) -> p n e", e=EX),
                    PB[0][:, 0:2 * D].rearrange("p (n e) -> p n e", e=EX),
                    sm[:, 32:36].rearrange("p (n o) -> p n o", o=1).broadcast_to([P, 4, EX]), ALU.mult)
                for k, bank in ((0, 2), (2, 3), (4, 1)):
                    for q in range(2):
                        c0, r0 = (2 + k + q) * D, 36 + 2 * (k + q)
                        last = nc.vector.tensor_tensor(
                            QKN[:, c0:c0 + D].rearrange("p (n e) -> p n e", e=EX),
                            PB[bank][:, q * 2 * D:q * 2 * D + D].rearrange("p (n e) -> p n e", e=EX),
                            sm[:, r0:r0 + 2].rearrange("p (n o) -> p n o", o=1).broadcast_to([P, 2, EX]), ALU.mult)
                last.then_inc(S["b_qkn"], 1)

                def maximum(u):
                    dve.wait_ge(S["b_s"], 4 * b + u + 1)
                    k = 2 * (u % 2)
                    nc.vector.tensor_reduce(sm[:, 80:81], PB[k][:, :], AX.X, ALU.max)
                    o.did(nc.vector.tensor_reduce(sm[:, 81:82], PB[k + 1][:, 0:N], AX.X, ALU.max))
                    o.wait()
                    nc.vector.tensor_scalar(sm[:, 64 + u:65 + u], sm[:, 80:81], sm[:, 81:82], -1.0 / math.sqrt(EX),
                                            ALU.max, ALU.mult).then_inc(S["b_max"], 1)
                    dve.wait_ge(S["b_max"], 4 * b + u + 1)

                maximum(0)
                for u in range(4):
                    if u < 3:
                        maximum(u + 1)
                    dve.wait_ge(S["b_pt"], 4 * b + u + 1)
                    nc.vector.tensor_copy(PTX[:, 0:M], PB[4][:, :])
                    nc.vector.tensor_copy(PTX[:, M:TK], PB[5][:, 0:N]).then_inc(S["b_ptc"], 1)
                dve.wait_ge(S["b_o"], b + 1)
                o.did(nc.vector.tensor_tensor(sm[:, 76:80], sm[:, 68:72], sm[:, 72:76], ALU.add))
                o.wait()
                o.did(nc.vector.reciprocal(sm[:, 84:88], sm[:, 76:80]))
                o.wait()
                for u in range(4):
                    hd, i = u // NT, u % NT
                    cs = slice(i * D + hd * EX, i * D + (hd + 1) * EX)
                    last = nc.vector.tensor_scalar(ONX[:, cs], PB[6][:, cs], sm[:, 84 + u:85 + u], None, ALU.mult)
                last.then_inc(S["b_on"], 1)
                dve.wait_ge(S["b_y"], b + 1)
                add_to_x(b, PB[7][:, N:2 * N], 1)
            o.end(B)

            def experts(layer, names, inner, router, weight):
                r, hs, sg, h2s, ys, yd = names
                F = fronts[layer]
                pairs = len(inner)
                with dve.Fori(0, B) as b:
                    o.loop(b, 6 if layer == 2 else 16)
                    front_vector(dve, o, F, b)
                    front_low(dve, F, b)
                    router(b)

                    def add(q):
                        dve.wait_ge(S[ys], pairs * b + q + 1)
                        n, joint = inner[q]
                        for k in range(1 if joint else n):
                            if k == 0 and q > 0:
                                dve.wait_ge(S[yd], (pairs - 1) * b + q)
                            else:
                                o.wait()
                            for i in range(NT):
                                xs = X[:, bass.ds((b * NT + i) * D, D)]
                                last = nc.vector.scalar_tensor_tensor(
                                    out=xs, in0=PB[4 + q % 2][:, (k * NT + i) * D:(k * NT + i + 1) * D],
                                    scalar=weight(i, q if joint else 2 * q + k), in1=xs, op0=ALU.mult, op1=ALU.add)
                            if not joint and k < n - 1:
                                o.did(last)
                        last.then_inc(S[yd] if q < pairs - 1 else layer_done[layer], 1)

                    for q in range(pairs):
                        n = inner[q][0]
                        dve.wait_ge(S[sg], pairs * b + q + 1)
                        nc.vector.tensor_tensor(H2[q % 2][:, 0:n * N], SG[q % 2][:, 0:n * N],
                                                PB[2 * (q % 2) + 1][:, 0:n * N], ALU.mult).then_inc(S[h2s], 1)
                        if q >= 1:
                            add(q - 1)
                    add(pairs - 1)
                o.end(B)

            LOW, TAKEN = -3e38, -1e38

            def router0(b):
                dve.wait_ge(S["c_r"], b + 1)
                for i in range(NT):
                    last = nc.vector.tensor_copy(gt[:, 16 * i:16 * i + E0], PB[6][:, 32 * i:32 * i + E0])
                o.did(last)
                o.wait_alone()
                for i in range(NT):
                    last = nc.vector.max(gt[:, 32 + 8 * i:40 + 8 * i], gt[:, 16 * i:16 * i + E0])
                o.did(last)
                o.wait()
                for i in range(NT):
                    last = nc.vector.tensor_tensor(gt[:, 48 + i:49 + i], gt[:, 32 + 8 * i:33 + 8 * i],
                                                   gt[:, 33 + 8 * i:34 + 8 * i], ALU.add)
                    nc.vector.memset(gt[:, 34 + 8 * i:40 + 8 * i], LOW)
                o.did(nc.vector.memset(gt[:, 50:51], 0.0))
                o.wait()
                for i in range(NT):
                    last = nc.vector.tensor_scalar(gt[:, 64 + 8 * i:72 + 8 * i], gt[:, 16 * i:16 * i + E0], 2.0,
                                                   gt[:, 48 + i:49 + i], ALU.mult, ALU.subtract)
                last.then_inc(S["c_xf"], 1)
                for i in range(NT):
                    last = nc.vector.match_replace(gt[:, 128 + 16 * i:142 + 16 * i], gt[:, 32 + 8 * i:40 + 8 * i],
                                                   gt[:, 16 * i:16 * i + 14], TAKEN)
                o.did(last)
                o.wait()
                dve.wait_ge(S["c_sig"], b + 1)
                for i in range(NT):
                    last = nc.vector.scalar_tensor_tensor(
                        out=gt[:, 160 + 8 * i:168 + 8 * i], in0=gt[:, 128 + 16 * i:136 + 16 * i], scalar=TAKEN,
                        in1=gt[:, 96 + 8 * i:104 + 8 * i], op0=ALU.is_equal, op1=ALU.mult)
                o.did(last)
                o.wait()

            def router1(b):
                dve.wait_ge(S["f_sig"], b + 1)
                for i in range(NT):
                    last = nc.vector.tensor_tensor(gt[:, 32 + 16 * i:48 + 16 * i], gt[:, 16 * i:16 * i + E1], ebF[:, :],
                                                   ALU.add)
                o.did(last)
                o.wait_alone()
                for i in range(NT):
                    last = nc.vector.max(gt[:, 64 + 8 * i:72 + 8 * i], gt[:, 32 + 16 * i:48 + 16 * i])
                o.did(last)
                o.wait_alone()
                for i in range(NT):
                    last = nc.vector.match_replace(gt[:, 80 + 16 * i:96 + 16 * i], gt[:, 64 + 8 * i:72 + 8 * i],
                                                   gt[:, 32 + 16 * i:48 + 16 * i], TAKEN)
                o.did(last)
                o.wait()
                for i in range(NT):
                    last = nc.vector.scalar_tensor_tensor(
                        out=gt[:, 112 + 16 * i:128 + 16 * i], in0=gt[:, 80 + 16 * i:96 + 16 * i], scalar=TAKEN,
                        in1=gt[:, 16 * i:16 * i + E1], op0=ALU.is_equal, op1=ALU.mult)
                o.did(last)
                o.wait()
                o.did(nc.vector.reduce_sum(gt[:, 144:146], gt[:, 112:144].rearrange("p (t e) -> p t e", e=E1), AX.X))
                o.wait()
                o.did(nc.vector.reciprocal(gt[:, 146:148], gt[:, 144:146]))
                o.wait()
                for i in range(NT):
                    last = nc.vector.tensor_scalar(gt[:, 160 + 32 * i:176 + 32 * i], gt[:, 112 + 16 * i:128 + 16 * i],
                                                   gt[:, 146 + i:147 + i], ROUTE_SCALE, ALU.mult, ALU.mult)
                o.did(last)
                o.wait()

            dve.wait_ge(layer_done[1], B)
            for i in range(NT):
                last = nc.vector.memset(gt[:, 16 * i + E0:16 * i + 16], LOW)
            last.then_inc(own, 1)
            o.base += 1
            o.wait()
            experts(2, ("c_r", "c_h", "c_sg", "c_h2", "c_y", "c_yd"), [(2, True)] * E0, router0,
                    lambda i, x: gt[:, 160 + 8 * i + x:161 + 8 * i + x])

            dve.wait_ge(layer_done[2], B)
            with dve.Fori(0, B) as b:
                o.loop(b, 3)
                F = fronts[3]
                front_vector(dve, o, F, b)
                dve.wait_ge(S["d_s"], b + 1)
                o.did(nc.vector.tensor_reduce(sm[:, 88:90], PB[2][:, :].rearrange("p (t m) -> p t m", m=N), AX.X,
                                              ALU.max))
                o.wait()
                nc.vector.tensor_scalar(sm[:, 64:66], sm[:, 88:90], -1.0 / math.sqrt(D), None,
                                        ALU.mult).then_inc(S["d_max"], 1)
                dve.wait_ge(S["d_pt"], b + 1)
                nc.vector.tensor_copy(PTD[:, :], PB[3][:, :]).then_inc(S["d_ptc"], 1)
                dve.wait_ge(S["d_o"], b + 1)
                o.did(nc.vector.reciprocal(sm[:, 72:74], sm[:, 68:70]))
                o.wait()
                for i in range(NT):
                    last = nc.vector.tensor_scalar(OND[:, i * D:(i + 1) * D], PB[4][:, i * D:(i + 1) * D],
                                                   sm[:, 72 + i:73 + i], None, ALU.mult)
                last.then_inc(S["d_on"], 1)
                dve.wait_ge(S["d_y"], b + 1)
                add_to_x(b, PB[6][:, 0:N], 3)
            o.end(B)

            dve.wait_ge(layer_done[3], B)
            dve.wait_ge(loaded["e"], 16 * len(plain["e"]))
            dve.wait_ge(S["e_vo0"], 2)
            with dve.Fori(0, B) as b:
                o.loop(b, 14)
                F = fronts[4]
                for g in range(4):
                    dve.wait_ge(S["e_kh"], 4 * b + g + 1)
                    nc.vector.scalar_tensor_tensor(out=KS[:, g * M:(g + 1) * M], in0=KHt[:, :], scalar=selk[:, 0:1],
                                                   in1=PB[g % 2][:, :], op0=ALU.mult, op1=ALU.add).then_inc(S["e_ks"], 1)
                front_vector(dve, o, F, b)
                front_low(dve, F, b)
                for g in range(4):
                    dve.wait_ge(S["e_qc"], 4 * b + g + 1)
                    nc.vector.tensor_copy(QHt[:, :].bitcast(f32r), QT0[:, :]).then_inc(S["e_qs"], 1)
                    dve.wait_ge(S["e_qs"], 8 * b + 2 * g + 1)
                    if g >= 1:
                        dve.wait_ge(S["e_qm"], 4 * b + g)
                    nc.vector.scalar_tensor_tensor(out=QSt[:, :].bitcast(f32r), in0=QHt[:, :], scalar=selq[:, 0:1],
                                                   in1=QT0[:, :], op0=ALU.mult, op1=ALU.add).then_inc(S["e_qs"], 1)
                nm4 = NMX[:, :].rearrange("p (t c) -> p t c", c=P)
                for g in range(4):
                    if g >= 1:
                        dve.wait_ge(S["e_nr"], 4 * b + g)
                    for j in range(4):
                        for i in range(NT):
                            n = 8 * g + 2 * j + i
                            dve.wait_ge(S["e_s"], 32 * b + n + 1)
                            last = nc.vector.tensor_reduce(NMX[:, i * P + 96 + j:i * P + 97 + j], PB[n % 3][:, :], AX.X,
                                                           ALU.max, negate=True)
                            if (j, i) != (3, 1):
                                last.then_inc(S["e_max"], 1)
                            else:
                                o.did(last)
                                o.wait()
                    nc.vector.tensor_copy(nm4[:, :, 100:104], nm4[:, :, 96:100]).then_inc(S["e_max"], 1)
                    dve.wait_ge(S["e_nr"], 4 * b + g + 1)
                    o.did(nc.vector.tensor_copy(NRH[96:P, :].bitcast(f32r), PB[7][96:P, 0:N]))
                    o.wait()
                    o.did(nc.vector.scalar_tensor_tensor(out=NRL[96:P, :].bitcast(f32r), in0=NRH[96:P, :],
                                                         scalar=seln[96:P, 0:1], in1=PB[7][96:P, 0:N], op0=ALU.mult,
                                                         op1=ALU.add))
                    o.wait()
                    dve.wait_ge(S["e_qm"], 4 * b + g + 1)
                    for j in range(4):
                        h = 4 * g + j
                        last = nc.vector.tensor_scalar(QM[96:P, h * N:(h + 1) * N], NRL[96:P, :], hmask[96:P, j:j + 1],
                                                       None, ALU.mult)
                    last.then_inc(S["e_nm"], 1)
                dve.wait_ge(S["e_od"], b + 1)
                o.did(nc.vector.reciprocal(RDE[:, :], PB[6][:, N:2 * N]))
                o.wait()
                nc.vector.tensor_tensor(OE[:, :], PB[6][:, 0:N], RDE[:, :], ALU.mult).then_inc(S["e_o"], 1)
                dve.wait_ge(S["e_y"], b + 1)
                add_to_x(b, PB[4][:, 0:N], 4)
            o.end(B)

            dve.wait_ge(layer_done[4], B)
            dve.wait_ge(loaded["f"], 16 * len(plain["f"]))
            for i in range(NT):
                last = nc.vector.memset(gt[:, 176 + 32 * i:177 + 32 * i], 1.0)
            last.then_inc(own, 1)
            o.base += 1
            o.wait()
            experts(5, ("f_r", "f_h", "f_sg", "f_h2", "f_y", "f_yd"), [(2, False)] * (E1 // 2) + [(1, False)],
                    router1, lambda i, x: gt[:, 160 + 32 * i + x:161 + 32 * i + x])


def kernel(**inputs):
    import numpy as np
    import concourse.bacc as bacc
    from concourse import mybir as mb
    from concourse.bass_utils import run_bass_kernel_spmd

    v = {k: np.asarray(a) for k, a in inputs.items()}
    f4 = np.float32

    def cols(a, k):
        return a.reshape(-1, P, k).transpose(1, 0, 2).reshape(P, -1)

    wq, wk, wv = (v["L0_attn_W" + n] for n in "qkv")
    g4 = np.arange(P)
    quad, off = g4 // 32, g4 % 32
    a = {
        "ident": np.eye(P, dtype=f4), "onesrow": np.ones((1, P), f4),
        "x": cols(v["x"].reshape(B * N, D), D),
        "wqT": wq.transpose(2, 0, 1).reshape(EA, HA * D), "wkT": wk.transpose(2, 0, 1).reshape(EA, HA * D),
        "wv": wv.transpose(1, 0, 2).reshape(D, HA * EA),
        "wp": cols(v["L0_attn_Wp"].reshape(EA, HA, D).transpose(1, 0, 2).reshape(HA * EA, D), D),
        "bp": v["L0_attn_bp"][None],
        "wqx": v["L0_xattn_Wq"].T, "wox": v["L0_xattn_Wo"].T, "wkvx": v["L0_xattn_Wkv"].T, "wlkv": v["L0_xattn_Wlkv"].T,
        "box": v["L0_xattn_bo"][None],
        "ctx": v["ctx_768"].reshape(B, MT, P, DC).transpose(0, 2, 1, 3).reshape(B, P, MT * DC),
        "mask": v["mask_BxS2_bk0"].reshape(B, M),
    }
    gcol = np.zeros((P, 6), f4)
    gcol[:DC, 0], gcol[:DC, 1] = v["L0_xattn_ln_x_g"], v["L0_xattn_ln_x_b"]
    gcol[:, 2], gcol[:, 3] = v["L0_xattn_ln_l_g"], v["L0_xattn_ln_l_b"]
    gcol[:, 4], gcol[:, 5] = np.tile(v["L0_xattn_qn_g"], HX), np.tile(v["L0_xattn_kn_g"], HX)
    a["gcol"] = gcol
    a["w1"] = v["L0_ffn_w1"].transpose(2, 0, 1).reshape(D, E0 * I0)
    a["w3"] = v["L0_ffn_w3"].transpose(2, 0, 1).reshape(D, E0 * I0)
    a["w2"] = v["L0_ffn_w2"].transpose(2, 0, 1).reshape(2, P, E0, D).transpose(1, 2, 0, 3).reshape(P, 2 * E0 * D)
    a["wgc"] = v["L0_ffn_wg"].T
    for n, s in (("wqd", "w_q"), ("wkd", "w_k"), ("wvd", "w_v"), ("wod", "w_out")):
        a[n] = v["L1_attn_" + s].T
    a["bqk"] = np.stack([v["L1_attn_b_q"], v["L1_attn_b_k"]], 1)
    a["bvd"], a["bod"] = v["L1_attn_b_v"][None], v["L1_attn_b_out"][None]

    wks, wqs = np.zeros((DC + 1, 4, P), f4), np.zeros((D, 4, P), f4)
    bqs = np.zeros((P, 4), f4)
    for g in range(4):
        for r in range(3):
            hc, to = slice(32 * g, 32 * g + 32), slice(32 * r, 32 * r + 32)
            wks[:DC, g, to], wks[DC, g, to] = v["L1_xattn_Wk"][:, hc], v["L1_xattn_bk"][hc]
            wqs[:, g, to], bqs[to, g] = v["L1_xattn_Wq"][:, hc], v["L1_xattn_bq"][hc]
        wks[DC, g, 96:104] = 1.0
    a["wks"], a["wqs"], a["bqs"] = wks.reshape(DC + 1, 4 * P), wqs.reshape(D, 4 * P), bqs
    wks_full = np.zeros((P, 4 * P), f4)
    wks_full[:DC + 1] = a["wks"]
    a["wks"] = wks_full
    a["wve"] = np.concatenate([v["L1_xattn_Wv"], v["L1_xattn_bv"][None]])
    a["w1e"] = v["L1_xattn_W1"]
    a["w2e"] = cols(v["L1_xattn_W2"], D)
    a["b1e"], a["b2e"] = v["L1_xattn_b1"].reshape(2, P).T, v["L1_xattn_b2"][None]
    a["ctxT"] = np.concatenate([v["ctx_768"].transpose(0, 2, 1), np.ones((B, 1, M), f4)], 1)
    cu, cd = np.zeros((P, 4, P), f4), np.zeros((P, 4, P), f4)
    for g in range(4):
        for j in range(4):
            for d in range(EY):
                cu[32 * j + d, g, 8 * (4 * g + j) + d] = 1.0
                cd[32 * j + EY, g, 8 * (4 * g + j) + d] = 1.0
    a["cu"], a["cd"] = cu.reshape(P, 4 * P), cd.reshape(P, 4 * P)
    a["selq"] = -(quad == 1).astype(f4)[:, None]
    a["selk"] = -(quad == 2).astype(f4)[:, None]
    a["seln"] = -((quad == 3) & (off >= 4) & (off < 8)).astype(f4)[:, None]
    head = np.where(quad < 3, off // EY, np.where(off < 8, off % 4, -1))
    a["hmask"] = (head[:, None] == np.arange(4)[None]).astype(f4)

    def fuse(routed, shared):
        return np.concatenate([routed, shared[None]]).transpose(2, 0, 1).reshape(P, STG)

    a["fg"] = fuse(v["L1_ffn_w_gate"], v["L1_ffn_shared_gate_w"])
    a["fu"] = fuse(v["L1_ffn_w_up"], v["L1_ffn_shared_up_w"])
    a["fd"] = fuse(v["L1_ffn_w_down"], v["L1_ffn_shared_down_w"])
    a["wgf"] = v["L1_ffn_gate_w"].T
    a["ebf"] = np.broadcast_to(v["L1_ffn_expert_bias"][None], (P, E1))

    nc = bacc.Bacc("TRN2", target_bir_lowering=False, num_devices=1)
    arrays, aps = {}, {}
    for name, arr in a.items():
        arr = np.ascontiguousarray(arr)
        arrays[f"in_{name}"] = arr
        aps[name] = nc.dram_tensor(f"in_{name}", arr.shape, mb.dt.from_np(arr.dtype), kind="ExternalInput").ap()
    out = nc.dram_tensor("out_0", (P, B * NT * D), mb.dt.float32, kind="ExternalOutput").ap()
    decoder(nc, aps, out)
    r = run_bass_kernel_spmd(nc, [arrays], core_ids=[0])
    y = r.results[0]["out_0"]
    return y.reshape(P, B * NT, D).transpose(1, 0, 2).reshape(B, N, D)
```

```python
import math
from contextlib import ExitStack

import concourse.bass as bass
from concourse import mybir

B, N, M, D, DC = 8, 256, 512, 128, 96
P = 128
NT, MT = N // P, M // P
HA, EA = 16, 64
HX, EX = 2, 64
HY, EY = 16, 8
E0, I0 = 8, 256
E1, K1, I1 = 16, 8, 128
TK = N + M
CH = 512
NCH = B * N // CH
CT = CH // P
ROUTE_SCALE = 2.826
LN_EPS = 1e-5
STG = (E1 + 1) * I1


def decoder(nc, t, out):
    f32, f32r, u8, bf16 = mybir.dt.float32, mybir.dt.float32r, mybir.dt.uint8, mybir.dt.bfloat16
    ALU, ACT, AX = mybir.AluOpType, mybir.ActivationFunctionType, mybir.AxisListType

    ctx = ExitStack()
    with ctx:
        def sem(name):
            return ctx.enter_context(nc.semaphore(name))

        class Arena:

            def __init__(self):
                self.stack = ExitStack()
                self.free = nc.sbuf_bytes_remaining

            def sb(self, name, cols, dt=f32, parts=P):
                made = self.stack.enter_context(nc.sbuf_tensor(name, [parts, cols], dt))
                self.used = self.free - nc.sbuf_bytes_remaining
                return made

        def keep(name, cols, dt=f32, parts=P):
            return ctx.enter_context(nc.sbuf_tensor(name, [parts, cols], dt))

        X = keep("X", B * NT * D)
        Xt = X[:, :].rearrange("p (t d) -> p t d", d=D)
        stage = [keep("stage0", STG), keep("stage1", STG)]
        ident = keep("ident", P)
        onesrow = keep("onesrow", P, parts=1)
        halves = keep("halves", 32)
        st = keep("st", 8 * 6)
        mv = keep("mv", 8 * 2)
        vs = keep("vs", 8)
        rs = keep("rs", 8)
        xn = keep("xn", NT * D)
        XH = keep("XH", N, f32r)
        XL = keep("XL", N, f32r)
        sm = keep("sm", 1024)
        st3 = st[:, :].rearrange("p (t s) -> p t s", s=6)
        mv3 = mv[:, :].rearrange("p (t s) -> p t s", s=2)
        xn3 = xn[:, :].rearrange("p (t d) -> p t d", d=D)

        a = Arena()
        MH, ML = a.sb("MH", HA * D, f32r), a.sb("ML", HA * D, f32r)
        WVH, WVL = a.sb("WVH", HA * EA, f32r), a.sb("WVL", HA * EA, f32r)
        WP = a.sb("WP", HA * EA)
        bp = a.sb("bp", D, parts=1)
        GH = [a.sb(f"GH{i}", 2 * N, f32r) for i in range(2)]
        GL = [a.sb(f"GL{i}", 2 * N, f32r) for i in range(2)]
        PA = [a.sb(f"PA{i}", NT * N) for i in range(2)]
        PTA = [a.sb(f"PTA{i}", NT * N) for i in range(4)]
        VA = a.sb("VA", NT * HA * EA)
        RA = [a.sb(f"RA{i}", N) for i in range(2)]
        RB = [a.sb(f"RB{i}", NT * 2 * EA) for i in range(2)]
        OTA = a.sb("OTA", HA * EA // P * N)
        a.stack.close()
        e = Arena()
        WKSH, WKSL = e.sb("WKSH", 4 * P, f32r), e.sb("WKSL", 4 * P, f32r)
        WQSH, WQSL = e.sb("WQSH", 4 * P, f32r), e.sb("WQSL", 4 * P, f32r)
        WVE = e.sb("WVE", D)
        bqs = e.sb("bqs", 4)
        W1E, W2E = e.sb("W1E", 2 * D), e.sb("W2E", 2 * D)
        b1E, b2E = e.sb("b1E", 2), e.sb("b2E", D, parts=1)
        CU, CD = e.sb("CU", 4 * P), e.sb("CD", 4 * P)
        selq, selk, seln, hmask = e.sb("selq", 1), e.sb("selk", 1), e.sb("seln", 1), e.sb("hmask", 4)
        CTE = e.sb("CTE", M)
        CEH, CEL = e.sb("CEH", M, f32r), e.sb("CEL", M, f32r)
        KS = e.sb("KS", 4 * M, f32r)
        QT0, QHt, QSt = e.sb("QT0", N), e.sb("QHt", N), e.sb("QSt", N)
        QM = e.sb("QM", HY * N, f32r)
        VO = e.sb("VO", MT * HY * 32)
        NMX = e.sb("NMX", NT * P)
        NRH = e.sb("NRH", N)
        NRL = e.sb("NRL", N)
        PTE = [e.sb(f"PTE{i}", 2 * MT * N) for i in range(2)]
        VS = e.sb("VS", M)
        UD = e.sb("UD", 4 * N)
        KHt = e.sb("KHt", M)
        RDE, OE, H1E = e.sb("RDE", N), e.sb("OE", N), e.sb("H1E", 2 * N)
        e.stack.close()
        big = Arena()
        big.sb("arena1_space", max(a.used, e.used) // 4)
        ctx.enter_context(big.stack)

        c = Arena()
        W1H, W1L = c.sb("W1H", E0 * I0, f32r), c.sb("W1L", E0 * I0, f32r)
        W3H, W3L = c.sb("W3H", E0 * I0, f32r), c.sb("W3L", E0 * I0, f32r)
        W2C = c.sb("W2C", 2 * E0 * D)
        WGC = c.sb("WGC", E0)
        c.stack.close()
        f = Arena()
        FGH, FGL = f.sb("FGH", STG, f32r), f.sb("FGL", STG, f32r)
        FUH, FUL = f.sb("FUH", STG, f32r), f.sb("FUL", STG, f32r)
        FD = f.sb("FD", STG)
        WGF = f.sb("WGF", E1)
        ebF = f.sb("ebF", E1)
        f.stack.close()
        big2 = Arena()
        big2.sb("arena2_space", max(c.used, f.used) // 4)
        ctx.enter_context(big2.stack)

        x = Arena()
        WQX, WOX = x.sb("WQX", D), x.sb("WOX", D)
        WKVX, WLKV = x.sb("WKVX", 2 * D), x.sb("WLKV", 2 * D)
        boX = x.sb("boX", D, parts=1)
        gcol = x.sb("gcol", 7)
        CX = x.sb("CX", MT * DC)
        CN = x.sb("CN", MT * DC)
        LN2 = xn
        CXT, LT = x.sb("CXT", M), x.sb("LT", N)
        RQ, RKV = x.sb("RQ", NT * D), x.sb("RKV", 6 * 2 * D)
        QKN = x.sb("QKN", 8 * D)
        SQ = QKN
        VX = x.sb("VX", 6 * D)
        KXH, KXL = x.sb("KXH", TK, f32r), x.sb("KXL", TK, f32r)
        QXH, QXL = x.sb("QXH", HX * N, f32r), x.sb("QXL", HX * N, f32r)
        mk8 = x.sb("mk8", M, u8, parts=1)
        mkb = x.sb("mkb", M, bf16, parts=1)
        onesb = x.sb("onesb", P, bf16, parts=1)
        PX = [x.sb(f"PX{i}", TK) for i in range(2)]
        PTX = x.sb("PTX", TK)
        ONX, OTX = sm[:, 448:448 + N], sm[:, 704:704 + N]
        x.stack.close()
        x = Arena()
        WQD, WKD, WVD, WOD = (x.sb(n, D) for n in ("WQD", "WKD", "WVD", "WOD"))
        bqk = x.sb("bqk", 2)
        bvD, boD = x.sb("bvD", D, parts=1), x.sb("boD", D, parts=1)
        XF = x.sb("XF", N)
        QD, KD, VD = x.sb("QD", N), x.sb("KD", N), x.sb("VD", N)
        PD, PTD = x.sb("PD", NT * N), x.sb("PTD", NT * N)
        OND, OTD = x.sb("OND", N), x.sb("OTD", N)
        x.stack.close()
        w = Arena()
        SG = [w.sb(f"SG{i}", 2 * N) for i in range(2)]
        H2 = [w.sb(f"H2{i}", 2 * N) for i in range(2)]
        XF2 = w.sb("XF2", N)
        gt = w.sb("gt", 512)
        w.stack.close()

        PB = [ctx.enter_context(nc.psum_tensor(f"PB{i}", [P, 512], f32)) for i in range(8)]

        def mm3(o, lh, ll, rh, rl, first=True, last=True):
            nc.tensor.matmul(o, lh, rh, start=first, stop=False)
            nc.tensor.matmul(o, ll, rh, start=False, stop=False)
            return nc.tensor.matmul(o, lh, rl, start=False, stop=last)

        def mm(o, l, r, first=True, last=True):
            return nc.tensor.matmul(o, l, r, start=first, stop=last)

        consts_loaded = sem("consts_loaded")
        x_loaded = sem("x_loaded")
        out_stored = sem("out_stored")
        own = sem("vector_own")
        pool_own = sem("pool_own")
        layer_done = [sem(f"layer{i}_done") for i in range(6)]
        LAYERS = [B] * 2 + [B] + [B] * 2 + [B]

        class Front:

            def __init__(self, n):
                self.var_ready = sem(f"var{n}_ready")
                self.rstd_ready = sem(f"rstd{n}_ready")
                self.xn_ready = sem(f"xn{n}_ready")
                self.xt_ready = sem(f"xt{n}_ready")
                self.xh_ready = sem(f"xh{n}_ready")
                self.xl_ready = sem(f"xl{n}_ready")

        fronts = [Front(i) if i != 1 else None for i in range(6)]
        own_count = [0]

        class Own:

            def __init__(self, eng, s):
                self.eng, self.s, self.base, self.k, self.per, self.b = eng, s, 0, 0, 0, 0

            def loop(self, b, per):
                self.b, self.per, self.k = b, per, 0

            def end(self, times):
                assert self.k == self.per, (self.k, self.per)
                self.base += self.per * times
                self.k = self.per = self.b = 0

            def did(self, ins):
                self.k += 1
                ins.then_inc(self.s, 1)

            def wait(self):
                self.eng.wait_ge(self.s, self.b * self.per + (self.base + self.k))

            def wait_alone(self):
                wait_alone(self.eng, self.s, self.b * self.per + (self.base + self.k))

        BANK_X = 7

        def front_statistics(o, F, b):
            for i in range(NT):
                last = nc.vector.bn_stats(st3[:, i, :], X[:, bass.ds((b * NT + i) * D, D)])
            o.did(last)
            o.wait_alone()
            for i in range(NT):
                last = nc.vector.bn_aggr(mv3[:, i, :], st3[:, i, :])
            last.then_inc(F.var_ready, 1)

        def front_normalise(dve, F, b):
            dve.wait_ge(F.rstd_ready, b + 1)
            for i in range(NT):
                last = nc.vector.tensor_scalar(xn3[:, i, :], X[:, bass.ds((b * NT + i) * D, D)], mv3[:, i, 0:1],
                                               rs[:, i:i + 1], ALU.subtract, ALU.mult)
            last.then_inc(F.xn_ready, 1)

        def front_vector(dve, o, F, b):
            front_statistics(o, F, b)
            front_normalise(dve, F, b)

        def front_pool(pool, po, F, b):
            wait_alone(pool, F.var_ready, b + 1)
            po.did(nc.gpsimd.tensor_scalar(vs[:, 0:NT], mv3[:, 0:NT, 1], LN_EPS, None, ALU.add))
            po.wait()
            nc.gpsimd.tensor_tensor(rs[:, 0:NT], vs[:, 0:NT], halves[:, 0:NT], ALU.pow).then_inc(F.rstd_ready, 1)

        def front_tensor(pe, F, b):
            pe.wait_ge(F.xn_ready, b + 1)
            for i in range(NT):
                last = nc.tensor.transpose(PB[BANK_X][:, i * P:(i + 1) * P], xn3[:, i, :], ident[:, :])
            last.then_inc(F.xt_ready, 1)

        def front_scalar(act, F, b):
            act.wait_ge(F.xt_ready, b + 1)
            nc.scalar.activation(XH[:, :], PB[BANK_X][:, 0:N], ACT.Copy).then_inc(F.xh_ready, 1)

        def front_low(dve, F, b):
            dve.wait_ge(F.xh_ready, b + 1)
            nc.vector.tensor_tensor(XL[:, :], PB[BANK_X][:, 0:N], XH[:, :].bitcast(f32),
                                    ALU.subtract).then_inc(F.xl_ready, 1)

        S = {}
        for name in ("a_mready a_mh a_ml a_v a_vc a_g a_gh a_gl a_s a_max a_exp a_pt a_ptc a_rb a_o a_rc a_on a_y "
                     "b_ctx b_mask b_ones b_var b_rstd b_cn b_r b_rc b_sq b_ss b_rr b_qkn b_kt b_kh b_kl b_vx b_mk "
                     "b_s b_max b_exp b_pt b_ptc b_ptd b_o b_on b_ot b_otc b_y "
                     "c_r c_h c_sg c_h2 c_y c_yd c_xf c_sig "
                     "d_q d_qc d_v d_vc d_s d_max d_exp d_pt d_ptc d_o d_on d_ot d_otc d_y "
                     "e_ctx e_w e_vo e_split e_k e_kh e_ks e_v e_vc e_q e_qc e_qs e_qm e_s e_max e_nr e_nm e_st e_exp e_uc "
                     "e_od e_o e_h e_hc e_y e_vo0 "
                     "f_r f_sig f_h f_sg f_h2 f_y f_yd "
                     "qk_in w_in0 w_in1 w_split").split():
            S[name] = sem(name)

        wait_passed = sem("wait_passed")

        def wait_alone(eng, s, value):
            eng.wait_ge(s, value)
            eng.sem_inc(wait_passed, 1)

        split_a = [("wv", P, HA * EA, WVH, WVL)]
        split_c = [("w1", P, E0 * I0, W1H, W1L), ("w3", P, E0 * I0, W3H, W3L)]
        split_e = [("wks", P, 4 * P, WKSH, WKSL), ("wqs", P, 4 * P, WQSH, WQSL)]
        split_f = [("fg", P, STG, FGH, FGL), ("fu", P, STG, FUH, FUL)]
        splits = [(i, None) for i in split_a] + [(i, None) for i in split_c] + [(i, 0) for i in split_e] \
            + [(i, 2) for i in split_f]
        SPLIT_A, SPLIT_C, SPLIT_E, SPLIT_F = 1, 3, 5, 7

        plain = {
            "a": [(WP, "wp"), (bp, "bp")],
            "x": [(WQX, "wqx"), (WOX, "wox"), (WKVX[0:DC, :], "wkvx"), (WLKV, "wlkv"), (boX, "box"), (gcol, "gcol")],
            "c": [(W2C, "w2"), (WGC, "wgc")],
            "d": [(WQD, "wqd"), (WKD, "wkd"), (WVD, "wvd"), (WOD, "wod"), (bqk, "bqk"), (bvD, "bvd"), (boD, "bod")],
            "e": [(WVE[0:DC + 1, :], "wve"), (bqs, "bqs"), (W1E, "w1e"), (W2E, "w2e"), (b1E, "b1e"), (b2E, "b2e"),
                  (CU, "cu"), (CD, "cd"), (selq, "selq"), (selk, "selk"), (seln, "seln"), (hmask, "hmask")],
            "f": [(FD, "fd"), (WGF, "wgf"), (ebF, "ebf")],
        }
        loaded = {k: sem(f"loaded_{k}") for k in plain}

        block = ctx.enter_context(nc.Block())

        @block.sync
        def _(sp):
            sp.dma_start(stage[0][0:EA, 0:HA * D], t["wqT"]).then_inc(S["qk_in"], 16)
            sp.dma_start(stage[1][0:EA, 0:HA * D], t["wkT"]).then_inc(S["qk_in"], 16)
            sp.dma_start(X[:, :], t["x"]).then_inc(x_loaded, 16)
            sp.dma_start(OTA[:, 0:HA * EA], t["wv"]).then_inc(S["w_in0"], 16)
            sp.dma_start(ident[:, :], t["ident"]).then_inc(consts_loaded, 16)
            sp.dma_start(onesrow[:, :], t["onesrow"]).then_inc(consts_loaded, 16)

            def plain_loads(k):
                for dst, name in plain[k]:
                    sp.dma_start(dst if isinstance(dst, bass.AP) else dst[:, :], t[name]).then_inc(loaded[k], 16)

            def split_load(i):
                (name, parts, cols, hi, lo), after = splits[i]
                if i == SPLIT_A:
                    sp.wait_ge(S["a_ml"], 4)
                if i >= 2:
                    sp.wait_ge(S["w_split"], 2 * (i - 1))
                sp.dma_start(stage[i % 2][0:parts, 0:cols], t[name]).then_inc(S[f"w_in{i % 2}"], 16)

            plain_loads("a")
            plain_loads("x")
            plain_loads("c")
            for i in range(SPLIT_A, SPLIT_C):
                split_load(i)

            def context_load(dst, b, src, s):
                sp.dma_start(dst, src[bass.ds(b, 1)].rearrange("b p n -> p (b n)")).then_inc(s, 16)

            def mask_load(b):
                sp.dma_start(mk8[:, :], t["mask"][bass.ds(b, 1), :]).then_inc(S["b_mask"], 16)

            context_load(CX[:, :], 0, t["ctx"], S["b_ctx"])
            mask_load(0)
            with sp.Fori(1, B) as b:
                sp.wait_ge(S["b_cn"], b)
                sp.wait_ge(S["b_mk"], b)
                context_load(CX[:, :], b, t["ctx"], S["b_ctx"])
                mask_load(b)
            sp.wait_ge(layer_done[0], B)
            plain_loads("e")
            for i in range(SPLIT_C, SPLIT_E):
                split_load(i)
            sp.wait_ge(layer_done[2], B)
            plain_loads("d")
            plain_loads("f")
            for i in range(SPLIT_E, SPLIT_F):
                split_load(i)
            context_load(CTE[0:DC + 1, :], 0, t["ctxT"], S["e_ctx"])
            with sp.Fori(1, B) as b:
                sp.wait_ge(S["e_vo"], 4 * b - 3)
                context_load(CTE[0:DC + 1, :], b, t["ctxT"], S["e_ctx"])
            sp.wait_ge(layer_done[5], B)
            sp.dma_start(out, X[:, :]).then_inc(out_stored, 16)
            sp.wait_ge(out_stored, 16)

        @block.gpsimd
        def _(pool):
            po = Own(pool, pool_own)
            nc.gpsimd.memset(halves[:, :], -0.5)
            po.did(nc.gpsimd.memset(sm[:, 1022:1023], 0.0))
            po.wait()
            po.base, po.k = 1, 0

            def split(i):
                (name, parts, cols, hi, lo), after = splits[i]
                if after is not None:
                    pool.wait_ge(layer_done[after], B)
                pool.wait_ge(S[f"w_in{i % 2}"], 16 * (i // 2 + 1))
                src = (stage[i % 2] if i >= SPLIT_A else OTA)[0:parts, 0:cols]
                nc.gpsimd.tensor_copy(hi[0:parts, 0:cols], src).then_inc(S["w_split"], 1)
                pool.wait_ge(S["w_split"], 2 * i + 1)
                nc.gpsimd.tensor_tensor(lo[0:parts, 0:cols], src, hi[0:parts, 0:cols].bitcast(f32),
                                        ALU.subtract).then_inc(S["w_split"], 1)

            def repeat(b, p):
                wait_alone(pool, S["a_ptc"], 16 * b + 2 * p + 2)
                r = sm[:, 256:256 + NT * HA].rearrange("p (t h) -> p t h", h=HA)[:, :, 2 * p:2 * p + 2]
                nc.gpsimd.tensor_copy(RB[p % 2][:, :].rearrange("p (t h e) -> p t h e", h=2, e=EA),
                                      r.rearrange("p t (h o) -> p t h o", o=1).broadcast_to([P, NT, 2, EA])
                                      ).then_inc(S["a_rb"], 1)

            po.loop(0, 1)
            front_pool(pool, po, fronts[0], 0)
            po.end(1)
            for i in range(SPLIT_A):
                split(i)
            with pool.Fori(0, B - 1) as b:
                po.loop(b, 1)
                for p in range(HA // 2):
                    repeat(b, p)
                    if p == 2:
                        front_pool(pool, po, fronts[0], b + 1)
            po.end(B - 1)

            def split_part(i, part, parts):
                (name, rows, cols, hi, lo), after = splits[i]
                if part == 0:
                    pool.wait_ge(S[f"w_in{i % 2}"], 16 * (i // 2 + 1))
                cs = slice(part * cols // parts, (part + 1) * cols // parts)
                src = stage[i % 2][0:rows, cs]
                po.did(nc.gpsimd.tensor_copy(hi[0:rows, cs], src))
                po.wait()
                last = nc.gpsimd.tensor_tensor(lo[0:rows, cs], src, hi[0:rows, cs].bitcast(f32), ALU.subtract)
                if part == parts - 1:
                    last.then_inc(S["w_split"], 2)

            po.loop(0, HA // 2)
            for p in range(HA // 2):
                repeat(B - 1, p)
                split_part(SPLIT_A + p // 4, p % 4, 4)
            po.end(1)
            assert SPLIT_C - SPLIT_A == 2
            nc.gpsimd.memset(onesb[:, :], 1.0).then_inc(S["b_ones"], 1)

            def norm(k):
                wait_alone(pool, S["b_var"], k + 1)
                nc.gpsimd.tensor_scalar(vs[:, 0:MT], mv3[:, 0:MT, 1], LN_EPS, None, ALU.add)
                po.did(nc.gpsimd.tensor_scalar(vs[:, MT:MT + NT], mv3[:, MT:MT + NT, 1], 1.0 + LN_EPS, LN_EPS * LN_EPS,
                                               ALU.mult, ALU.add))
                po.wait()
                nc.gpsimd.tensor_tensor(rs[:, 0:MT + NT], vs[:, 0:MT + NT], halves[:, 0:MT + NT],
                                        ALU.pow).then_inc(S["b_rstd"], 1)

            def roots(k, half):
                c0 = 8 * half
                wait_alone(pool, S["b_ss"], 2 * k + half + 1)
                po.did(nc.gpsimd.tensor_scalar(sm[:, 16 + c0:24 + c0], sm[:, c0:c0 + 8], 1.0 / EX, 1e-16, ALU.mult,
                                               ALU.max))
                po.wait()
                nc.gpsimd.tensor_tensor(sm[:, 32 + c0:40 + c0], sm[:, 16 + c0:24 + c0], halves[:, 0:8],
                                        ALU.pow).then_inc(S["b_rr"], 1)

            def place_values(k, first=False):
                wait_alone(pool, S["b_rc"], 6 * k + 6)
                if not first:
                    wait_alone(pool, S["b_o"], k)
                nc.gpsimd.tensor_copy(VX[:, :].rearrange("p (t c) -> p t c", c=D),
                                      RKV[:, :].rearrange("p (t c) -> p t c", c=2 * D)[:, :, D:2 * D]
                                      ).then_inc(S["b_vx"], 1)

            po.loop(0, 4)
            norm(0)
            roots(0, 0)
            roots(0, 1)
            norm(1)
            place_values(0, first=True)
            po.end(1)
            with pool.Fori(0, B - 2) as b:
                po.loop(b, 3)
                roots(b + 1, 0)
                roots(b + 1, 1)
                norm(b + 2)
                place_values(b + 1)
            po.end(B - 2)
            po.loop(0, 2)
            roots(B - 1, 0)
            roots(B - 1, 1)
            place_values(B - 1)
            po.end(1)

            def plain_layer(layer):
                wait_alone(pool, layer_done[layer - 1], B)
                with pool.Fori(0, B) as b:
                    po.loop(b, 1)
                    front_pool(pool, po, fronts[layer], b)
                po.end(B)

            plain_layer(2)
            for i in range(SPLIT_C, SPLIT_E):
                split(i)
            plain_layer(3)
            for i in range(SPLIT_E, SPLIT_F):
                split(i)

            pool.wait_ge(layer_done[3], B)
            nc.gpsimd.memset(VO[:, :], 0.0).then_inc(S["e_vo0"], 1)
            pool.wait_ge(S["e_vo0"], 1)
            nc.gpsimd.memset(VO[:, :].rearrange("p (h c) -> p h c", c=32)[:, :, EY:2 * EY], 1.0)
            nc.gpsimd.memset(NMX[:, :], 0.0).then_inc(S["e_vo0"], 1)
            pool.wait_ge(S["e_vo0"], 2)

            def context_split(b):
                wait_alone(pool, S["e_ctx"], 16 * b + 16)
                nc.gpsimd.tensor_copy(CEH[0:DC + 1, :], CTE[0:DC + 1, :]).then_inc(S["e_split"], 1)
                wait_alone(pool, S["e_split"], 2 * b + 1)
                nc.gpsimd.tensor_tensor(CEL[0:DC + 1, :], CTE[0:DC + 1, :], CEH[0:DC + 1, :].bitcast(f32),
                                        ALU.subtract).then_inc(S["e_split"], 1)

            def value_group(b, g):
                dst = VO[:, :].rearrange("p (m h c) -> p m h c", h=HY, c=32)[:, :, 4 * g:4 * g + 4, 0:EY]
                src = VS[:, :].rearrange("p (m h c) -> p m h c", h=HY, c=EY)[:, :, 4 * g:4 * g + 4, :]
                nc.gpsimd.tensor_copy(dst, src).then_inc(S["e_vo"], 1)

            def ahead(b):
                wait_alone(pool, S["e_k"], 4 * b + 4)
                context_split(b + 1)
                front_pool(pool, po, fronts[4], b + 1)
                for g in range(4):
                    wait_alone(pool, S["e_w"], 8 * b + 2 * g + 2)
                    wait_alone(pool, S["e_vc"], b + 2)
                    value_group(b + 1, g)

            context_split(0)
            po.loop(0, 1)
            front_pool(pool, po, fronts[4], 0)
            po.end(1)
            pool.wait_ge(S["e_vc"], 1)
            for g in range(4):
                value_group(0, g)
            with pool.Fori(0, B - 1) as b:
                po.loop(b, 1)
                ahead(b)
            po.end(B - 1)
            plain_layer(5)

        @block.tensor
        def _(pe):
            pe.wait_ge(S["qk_in"], 32)
            for q in range(4):
                for i in range(4):
                    h = 4 * q + i
                    last = mm(PB[q][:, i * D:(i + 1) * D], stage[0][0:EA, h * D:(h + 1) * D],
                              stage[1][0:EA, h * D:(h + 1) * D])
                last.then_inc(S["a_mready"], 1)
            pe.wait_ge(S["a_ml"], 4)
            pe.wait_ge(consts_loaded, 32)

            def self_attention():
                F = fronts[0]

                def values(b, u):
                    half, mt = u // 2, u % 2
                    if u >= 2:
                        pe.wait_ge(S["a_vc"], 4 * b + u - 1)
                    cs = slice(half * 512, half * 512 + 512)
                    mm3(PB[(4, 7)[u % 2]][:, :], XH[:, mt * P:(mt + 1) * P], XL[:, mt * P:(mt + 1) * P], WVH[:, cs],
                        WVL[:, cs]).then_inc(S["a_v"], 1)

                def project(b, p):
                    if p >= 1:
                        pe.wait_ge(S["a_gl"], 8 * b + p)
                    else:
                        pe.wait_ge(S["a_vc"], 4 * b + 3)
                    for i in range(2):
                        hs = slice((2 * p + i) * D, (2 * p + i + 1) * D)
                        last = mm3(PB[4][:, i * N:(i + 1) * N], MH[:, hs], ML[:, hs], XH[:, :], XL[:, :])
                    last.then_inc(S["a_g"], 1)

                def scores(b, h):
                    if h % 2 == 0:
                        pe.wait_ge(S["a_gl"], 8 * b + h // 2 + 1)
                    if h >= 2:
                        pe.wait_ge(S["a_exp"], 16 * b + h - 1)
                    gh, gl = GH[h // 2 % 2], GL[h // 2 % 2]
                    for i in range(NT):
                        cs = slice(h % 2 * N + i * P, h % 2 * N + (i + 1) * P)
                        last = mm3(PB[h % 2][:, i * N:(i + 1) * N], gh[:, cs], gl[:, cs], XH[:, :], XL[:, :])
                    last.then_inc(S["a_s"], 1)

                def turn(b, h):
                    pe.wait_ge(S["a_exp"], 16 * b + h + 1)
                    if h >= 2:
                        pe.wait_ge(S["a_ptc"], 16 * b + h - 1)
                    for mt in range(NT):
                        for i in range(NT):
                            last = nc.tensor.transpose(
                                PB[2 + h % 2][:, mt * N + i * P:mt * N + (i + 1) * P],
                                PA[h % 2][:, i * N + mt * P:i * N + (mt + 1) * P], ident[:, :])
                    last.then_inc(S["a_pt"], 1)

                def weigh(b, p):
                    pe.wait_ge(S["a_ptc"], 16 * b + 2 * p + 2)
                    if p == 0:
                        pe.wait_ge(S["a_vc"], 4 * b + 4)
                    if p >= 2:
                        pe.wait_ge(S["a_on"], 8 * b + p - 1)
                    bank = PB[5 + p % 2]
                    for mt in range(NT):
                        for j in range(2):
                            h = 2 * p + j
                            last = mm(bank[j * EA:(j + 1) * EA, 0:N],
                                      VA[:, mt * HA * EA + h * EA:mt * HA * EA + (h + 1) * EA],
                                      PTA[h % 4][:, mt * N:(mt + 1) * N], first=mt == 0, last=mt == NT - 1)
                    pe.wait_ge(S["a_rb"], 8 * b + p + 1)
                    for i in range(NT):
                        last = nc.tensor.transpose(bank[:, N + i * P:N + (i + 1) * P], RB[p % 2][:, i * P:(i + 1) * P],
                                                   ident[:, :])
                    last.then_inc(S["a_o"], 1)

                def attend(b, more):
                    for s in range(HA):
                        if s >= 1:
                            scores(b, s)
                        if s % 2 == 0 and s + 2 < HA:
                            project(b, s // 2 + 1)
                        if s == HA - 1 and more:
                            front_tensor(pe, F, b + 1)
                        if s % 2 and s >= 3:
                            weigh(b, (s - 3) // 2)
                        if s >= 1:
                            turn(b, s - 1)
                    if more:
                        pe.wait_ge(F.xh_ready, b + 2)
                        pe.wait_ge(F.xl_ready, b + 2)
                        values(b + 1, 0)
                    turn(b, HA - 1)
                    if more:
                        values(b + 1, 1)
                    weigh(b, HA // 2 - 1)
                    if more:
                        values(b + 1, 2)
                        values(b + 1, 3)
                        project(b + 1, 0)
                        pe.wait_ge(S["a_vc"], 4 * b + 8)
                    pe.wait_ge(S["a_on"], 8 * b + 8)
                    for i in range(NT):
                        o = PB[7][:, i * D:(i + 1) * D]
                        for k in range(HA * EA // P):
                            mm(o, OTA[:, k * N + i * P:k * N + (i + 1) * P], WP[:, k * D:(k + 1) * D], first=k == 0,
                               last=False)
                        last = mm(o, onesrow[:, :], bp[:, :], first=False)
                    last.then_inc(S["a_y"], 1)
                    if more:
                        scores(b + 1, 0)

                front_tensor(pe, F, 0)
                pe.wait_ge(F.xh_ready, 1)
                pe.wait_ge(F.xl_ready, 1)
                pe.wait_ge(S["w_split"], 2 * SPLIT_A)
                pe.wait_ge(loaded["a"], 16 * len(plain["a"]))
                for u in range(4):
                    values(0, u)
                project(0, 0)
                scores(0, 0)
                with pe.Fori(0, B - 1) as b:
                    attend(b, True)
                attend(B - 1, False)

            self_attention()

            pe.wait_ge(layer_done[0], B)
            pe.wait_ge(loaded["x"], 16 * len(plain["x"]))
            pe.wait_ge(S["b_ones"], 1)

            def cross_attention():
                ring = PB[7]

                def prepare(k, r):
                    if r == 0:
                        pe.wait_ge(S["b_cn"], k + 1)
                    else:
                        pe.wait_ge(S["b_rc"], 6 * k + r)
                    if r == 0:
                        for i in range(MT):
                            last = nc.tensor.transpose(ring[0:DC, i * P:(i + 1) * P], CN[:, i * DC:(i + 1) * DC],
                                                       ident[:, :])
                    elif r == 1:
                        for i in range(NT):
                            last = nc.tensor.transpose(ring[:, i * P:(i + 1) * P], LN2[:, i * D:(i + 1) * D],
                                                       ident[:, :])
                    elif r == 2:
                        for i in range(NT):
                            last = mm(ring[:, i * D:(i + 1) * D], LT[:, i * P:(i + 1) * P], WQX[:, :])
                    else:
                        for q in range(2):
                            i = 2 * (r - 3) + q
                            o = ring[:, q * 2 * D:(q + 1) * 2 * D]
                            if i < MT:
                                last = mm(o, CXT[0:DC, i * P:(i + 1) * P], WKVX[0:DC, :])
                            else:
                                last = mm(o, LT[:, (i - MT) * P:(i - MT + 1) * P], WLKV[:, :])
                    last.then_inc(S["b_r"], 1)

                def turn_keys(k):
                    pe.wait_ge(S["b_rc"], 6 * k + 6)
                    pe.wait_ge(S["b_qkn"], k + 1)
                    for i in range(MT):
                        last = nc.tensor.transpose(ring[:, i * P:(i + 1) * P], QKN[:, (2 + i) * D:(3 + i) * D],
                                                   ident[:, :])
                    last.then_inc(S["b_kt"], 1)
                    for i, c0 in enumerate((6, 7, 0, 1)):
                        last = nc.tensor.transpose(PB[5][:, i * P:(i + 1) * P], QKN[:, c0 * D:(c0 + 1) * D],
                                                   ident[:, :])
                    last.then_inc(S["b_kt"], 1)

                def scores(b, u):
                    hd, i = u // NT, u % NT
                    if u == 0:
                        pe.wait_ge(S["b_kh"], 2 * b + 2)
                        pe.wait_ge(S["b_kl"], 2 * b + 2)
                        pe.wait_ge(S["b_mk"], b + 1)
                    q = slice(hd * N + i * P, hd * N + (i + 1) * P)
                    lo, hi = PB[2 * (u % 2)], PB[2 * (u % 2) + 1]
                    mm3(lo[:, :], QXH[:, q], QXL[:, q], KXH[:, 0:M], KXL[:, 0:M], last=False)
                    mm(lo[:, :], onesb[:, :], mkb[:, :], first=False)
                    mm3(hi[:, 0:N], QXH[:, q], QXL[:, q], KXH[:, M:TK], KXL[:, M:TK]).then_inc(S["b_s"], 1)

                def turn(b, u):
                    pe.wait_ge(S["b_exp"], 4 * b + u + 1)
                    for mt in range(6):
                        last = nc.tensor.transpose(PB[4 + mt // 4][:, mt % 4 * P:(mt % 4 + 1) * P],
                                                   PX[u % 2][:, mt * P:(mt + 1) * P], ident[:, :])
                    last.then_inc(S["b_pt"], 1)

                def weigh(b, u):
                    hd, i = u // NT, u % NT
                    pe.wait_ge(S["b_ptc"], 4 * b + u + 1)
                    pe.wait_ge(S["b_ptd"], 4 * b + u + 1)
                    if u == 0:
                        pe.wait_ge(S["b_vx"], b + 1)
                    for mt in range(6):
                        last = mm(PB[6][:, i * D + hd * EX:i * D + (hd + 1) * EX], PTX[:, mt * P:(mt + 1) * P],
                                  VX[:, mt * D + hd * EX:mt * D + (hd + 1) * EX], first=mt == 0, last=mt == 5)
                    if u == 3:
                        last.then_inc(S["b_o"], 1)

                def attend(b, more):
                    scores(b, 0)
                    if more:
                        prepare(b + 1, 0)
                    scores(b, 1)
                    if more:
                        prepare(b + 1, 1)
                    for u in range(4):
                        turn(b, u)
                        if u < 2:
                            if more:
                                prepare(b + 1, 2 * u + 2)
                            scores(b, u + 2)
                        weigh(b, u)
                        if u < 2 and more:
                            prepare(b + 1, 2 * u + 3)
                    if more:
                        turn_keys(b + 1)
                    pe.wait_ge(S["b_on"], b + 1)
                    for i in range(NT):
                        last = nc.tensor.transpose(PB[4][:, i * P:(i + 1) * P], ONX[:, i * D:(i + 1) * D], ident[:, :])
                    last.then_inc(S["b_ot"], 1)
                    pe.wait_ge(S["b_otc"], b + 1)
                    for i in range(NT):
                        o = PB[6][:, i * D:(i + 1) * D]
                        mm(o, OTX[:, i * P:(i + 1) * P], WOX[:, :], last=False)
                        last = mm(o, onesrow[:, :], boX[:, :], first=False)
                    last.then_inc(S["b_y"], 1)

                for r in range(6):
                    prepare(0, r)
                turn_keys(0)
                with pe.Fori(0, B - 1) as b:
                    attend(b, True)
                attend(B - 1, False)

            cross_attention()

            def experts(layer, names, inner, wr, nexp, up, ups, gate, gates, down):
                r, hs, sg, h2s, ys, yd = names
                F = fronts[layer]
                pairs = len(inner)
                with pe.Fori(0, B) as b:
                    front_tensor(pe, F, b)
                    pe.wait_ge(F.xh_ready, b + 1)
                    pe.wait_ge(F.xl_ready, b + 1)
                    for i in range(NT):
                        last = mm(PB[6][:, i * 32:i * 32 + nexp], XF2[:, i * P:(i + 1) * P], wr[:, 0:nexp])
                    last.then_inc(S[r], 1)

                    def hidden(q):
                        n = inner[q][0]
                        if q >= 2:
                            pe.wait_ge(S[h2s], pairs * b + q - 1)
                        for k in range(n):
                            cs = slice((2 * q + k) * P, (2 * q + k + 1) * P)
                            mm3(PB[2 * (q % 2)][:, k * N:(k + 1) * N], gate[:, cs], gates[:, cs], XH[:, :], XL[:, :])
                        for k in range(n):
                            cs = slice((2 * q + k) * P, (2 * q + k + 1) * P)
                            last = mm3(PB[2 * (q % 2) + 1][:, k * N:(k + 1) * N], up[:, cs], ups[:, cs], XH[:, :],
                                       XL[:, :])
                        last.then_inc(S[hs], 1)

                    hidden(0)
                    for q in range(pairs):
                        if q + 1 < pairs:
                            hidden(q + 1)
                        pe.wait_ge(S[h2s], pairs * b + q + 1)
                        if q >= 2:
                            pe.wait_ge(S[yd], (pairs - 1) * b + q - 1)
                        n, joint = inner[q]
                        y = PB[4 + q % 2]
                        for i in range(NT):
                            for k in range(n):
                                o = y[:, i * D:(i + 1) * D] if joint else y[:, (k * NT + i) * D:(k * NT + i + 1) * D]
                                last = mm(o, H2[q % 2][:, k * N + i * P:k * N + (i + 1) * P],
                                          down[:, (2 * q + k) * D:(2 * q + k + 1) * D],
                                          first=k == 0 or not joint, last=k == n - 1 or not joint)
                        last.then_inc(S[ys], 1)

            pe.wait_ge(layer_done[1], B)
            pe.wait_ge(S["w_split"], 2 * SPLIT_C)
            pe.wait_ge(loaded["c"], 16 * len(plain["c"]))
            experts(2, ("c_r", "c_h", "c_sg", "c_h2", "c_y", "c_yd"), [(2, True)] * E0, WGC, E0, W3H, W3L, W1H,
                    W1L, W2C)

            pe.wait_ge(layer_done[2], B)
            pe.wait_ge(loaded["d"], 16 * len(plain["d"]))
            with pe.Fori(0, B) as b:
                F = fronts[3]
                front_tensor(pe, F, b)
                pe.wait_ge(F.xh_ready, b + 1)
                mm(PB[0][:, 0:N], WQD[:, :], XF[:, :])
                mm(PB[0][:, N:2 * N], WKD[:, :], XF[:, :]).then_inc(S["d_q"], 1)
                for i in range(NT):
                    mm(PB[1][:, i * D:(i + 1) * D], XF[:, i * P:(i + 1) * P], WVD[:, :], last=False)
                    last = mm(PB[1][:, i * D:(i + 1) * D], onesrow[:, :], bvD[:, :], first=False)
                last.then_inc(S["d_v"], 1)
                pe.wait_ge(S["d_qc"], b + 1)
                for i in range(NT):
                    last = mm(PB[2][:, i * N:(i + 1) * N], QD[:, i * P:(i + 1) * P], KD[:, :])
                last.then_inc(S["d_s"], 1)
                pe.wait_ge(S["d_exp"], b + 1)
                for mt in range(NT):
                    for i in range(NT):
                        last = nc.tensor.transpose(PB[3][:, mt * N + i * P:mt * N + (i + 1) * P],
                                                   PD[:, i * N + mt * P:i * N + (mt + 1) * P], ident[:, :])
                last.then_inc(S["d_pt"], 1)
                pe.wait_ge(S["d_ptc"], b + 1)
                pe.wait_ge(S["d_vc"], b + 1)
                for i in range(NT):
                    for mt in range(NT):
                        last = mm(PB[4][:, i * D:(i + 1) * D], PTD[:, mt * N + i * P:mt * N + (i + 1) * P],
                                  VD[:, mt * D:(mt + 1) * D], first=mt == 0, last=mt == NT - 1)
                last.then_inc(S["d_o"], 1)
                pe.wait_ge(S["d_on"], b + 1)
                for i in range(NT):
                    last = nc.tensor.transpose(PB[5][:, i * P:(i + 1) * P], OND[:, i * D:(i + 1) * D], ident[:, :])
                last.then_inc(S["d_ot"], 1)
                pe.wait_ge(S["d_otc"], b + 1)
                for i in range(NT):
                    mm(PB[6][:, i * D:(i + 1) * D], OTD[:, i * P:(i + 1) * P], WOD[:, :], last=False)
                    last = mm(PB[6][:, i * D:(i + 1) * D], onesrow[:, :], boD[:, :], first=False)
                last.then_inc(S["d_y"], 1)

            pe.wait_ge(layer_done[3], B)
            pe.wait_ge(S["w_split"], 2 * SPLIT_E)
            pe.wait_ge(loaded["e"], 16 * len(plain["e"]))
            pe.wait_ge(S["e_vo0"], 2)
            F4 = fronts[4]

            def keys_queries(b, g):
                cs = slice(g * P, (g + 1) * P)
                if g == 0:
                    pe.wait_ge(S["e_split"], 2 * b + 2)
                    pe.wait_ge(S["e_vc"], b + 1)
                else:
                    pe.wait_ge(S["e_ks"], 4 * b + g)
                mm3(PB[6][:, :], WKSH[0:DC + 1, cs], WKSL[0:DC + 1, cs], CEH[0:DC + 1, :],
                    CEL[0:DC + 1, :]).then_inc(S["e_k"], 1)
                if g == 0:
                    pe.wait_ge(F4.xh_ready, b + 1)
                    pe.wait_ge(F4.xl_ready, b + 1)
                else:
                    pe.wait_ge(S["e_qc"], 4 * b + g)
                mm3(PB[7][:, 0:N], WQSH[:, cs], WQSL[:, cs], XH[:, :], XL[:, :]).then_inc(S["e_q"], 1)

            def score_unit(b, g, n, first=False):
                h, i = 4 * g + n // 2, n % 2
                if n == 0:
                    pe.wait_ge(S["e_qm"], 4 * b + g + 1)
                if not (first and n < 2):
                    pe.wait_ge(S["e_max"], 32 * b + 8 * g + n - 1)
                mm(PB[n % 2][:, :], QM[:, h * N + i * P:h * N + (i + 1) * P],
                   KS[:, g * M:(g + 1) * M]).then_inc(S["e_s"], 1)

            def rows(b, g):
                pe.wait_ge(S["e_max"], 32 * b + 8 * g + 8)
                for i in range(NT):
                    last = nc.tensor.transpose(PB[5][:, i * P:(i + 1) * P], NMX[:, i * P:(i + 1) * P], ident[:, :])
                last.then_inc(S["e_nr"], 1)

            def turned_unit(b, g, k, j):
                h, n = 4 * g + j, 4 * k + j
                if g or n >= 2:
                    pe.wait_ge(S["e_exp"], 32 * b + 8 * g + n - 1)
                for q in range(2):
                    mt = 2 * k + q
                    last = mm(PB[2 + n % 2][:, q * N:(q + 1) * N], KS[:, g * M + mt * P:g * M + (mt + 1) * P],
                              QM[:, h * N:(h + 1) * N])
                last.then_inc(S["e_st"], 1)

            def weigh(b, g, k):
                pe.wait_ge(S["e_exp"], 32 * b + 8 * g + 4 * k + 4)
                if k == 0:
                    pe.wait_ge(S["e_vo"], 4 * b + g + 1)
                    if g >= 1:
                        pe.wait_ge(S["e_uc"], 4 * b + g)
                for q in range(2):
                    mt = 2 * k + q
                    for j in range(4):
                        h = 4 * g + j
                        last = mm(PB[4][32 * j:32 * j + 32, 0:N], VO[:, (mt * HY + h) * 32:(mt * HY + h + 1) * 32],
                                  PTE[k][:, (2 * j + q) * N:(2 * j + q + 1) * N], first=mt == 0, last=mt == MT - 1)
                last.then_inc(S["e_w"], 1)

            def finish(b):
                pe.wait_ge(S["e_uc"], 4 * b + 4)
                for g in range(4):
                    mm(PB[4][:, 0:N], CU[:, g * P:(g + 1) * P], UD[:, g * N:(g + 1) * N], first=g == 0, last=g == 3)
                for g in range(4):
                    last = mm(PB[4][:, N:2 * N], CD[:, g * P:(g + 1) * P], UD[:, g * N:(g + 1) * N], first=g == 0,
                              last=g == 3)
                last.then_inc(S["e_od"], 1)
                pe.wait_ge(S["e_o"], b + 1)
                for k in range(2):
                    last = mm(PB[5][:, k * N:(k + 1) * N], W1E[:, k * P:(k + 1) * P], OE[:, :])
                last.then_inc(S["e_h"], 1)
                pe.wait_ge(S["e_hc"], b + 1)
                for i in range(NT):
                    for k in range(2):
                        mm(PB[4][:, i * D:(i + 1) * D], H1E[:, k * N + i * P:k * N + (i + 1) * P],
                           W2E[:, k * D:(k + 1) * D], first=k == 0, last=False)
                    last = mm(PB[4][:, i * D:(i + 1) * D], onesrow[:, :], b2E[:, :], first=False)
                last.then_inc(S["e_y"], 1)

            def attend(b, more):
                for g in range(4):
                    rows(b, g)
                    if g == 0:
                        keys_queries(b, 3)
                        if more:
                            pe.wait_ge(S["e_qc"], 4 * b + 4)
                            front_tensor(pe, F4, b + 1)
                            pe.wait_ge(S["e_ks"], 4 * b + 4)
                            pe.wait_ge(S["e_ctx"], 16 * b + 32)
                            for i in range(MT):
                                last = mm(PB[6][:, i * D:(i + 1) * D], CTE[0:DC + 1, i * P:(i + 1) * P],
                                          WVE[0:DC + 1, :])
                            last.then_inc(S["e_v"], 1)
                    elif more:
                        keys_queries(b + 1, g - 1)
                    pe.wait_ge(S["e_nm"], 4 * b + g + 1)
                    for k in range(2):
                        for j in range(4):
                            turned_unit(b, g, k, j)
                            if g < 3:
                                score_unit(b, g + 1, 4 * k + j)
                            elif more:
                                score_unit(b + 1, 0, 4 * k + j)
                        if k:
                            weigh(b, g, 0)
                        elif g:
                            weigh(b, g - 1, 1)
                weigh(b, 3, 1)
                finish(b)

            pe.wait_ge(S["e_ctx"], 16)
            for i in range(MT):
                last = mm(PB[6][:, i * D:(i + 1) * D], CTE[0:DC + 1, i * P:(i + 1) * P], WVE[0:DC + 1, :])
            last.then_inc(S["e_v"], 1)
            front_tensor(pe, F4, 0)
            for g in range(3):
                keys_queries(0, g)
            for n in range(8):
                score_unit(0, 0, n, first=True)
            with pe.Fori(0, B - 1) as b:
                attend(b, True)
            attend(B - 1, False)

            pe.wait_ge(layer_done[4], B)
            pe.wait_ge(S["w_split"], 2 * SPLIT_F)
            pe.wait_ge(loaded["f"], 16 * len(plain["f"]))
            experts(5, ("f_r", "f_h", "f_sg", "f_h2", "f_y", "f_yd"), [(2, False)] * (E1 // 2) + [(1, False)],
                    WGF, E1, FUH, FUL, FGH, FGL, FD)

        @block.scalar
        def _(act):
            for q in range(4):
                act.wait_ge(S["a_mready"], q + 1)
                nc.scalar.activation(MH[:, q * 512:(q + 1) * 512], PB[q][:, :], ACT.Copy,
                                     scale=1.0 / math.sqrt(EA)).then_inc(S["a_mh"], 1)

            def self_attention():
                def values(b, u):
                    act.wait_ge(S["a_v"], 4 * b + u + 1)
                    half, mt = u // 2, u % 2
                    nc.scalar.activation(VA[:, mt * HA * EA + half * 512:mt * HA * EA + (half + 1) * 512],
                                         PB[(4, 7)[u % 2]][:, :], ACT.Copy).then_inc(S["a_vc"], 1)

                def high(b, p):
                    act.wait_ge(S["a_g"], 8 * b + p + 1)
                    nc.scalar.activation(GH[p % 2][:, :], PB[4][:, :], ACT.Copy).then_inc(S["a_gh"], 1)

                def exps(b, h):
                    act.wait_ge(S["a_max"], 16 * b + h + 1)
                    for i in range(NT):
                        last = nc.scalar.activation(PA[h % 2][:, i * N:(i + 1) * N], PB[h % 2][:, i * N:(i + 1) * N],
                                                    ACT.Exp, bias=sm[:, 128 + 2 * h + i:129 + 2 * h + i],
                                                    accum_out=sm[:, 192 + i * HA + h:193 + i * HA + h])
                    last.then_inc(S["a_exp"], 1)

                def reciprocals(b, p):
                    act.wait_ge(S["a_o"], 8 * b + p + 1)
                    if p >= 2:
                        act.wait_ge(S["a_on"], 8 * b + p - 1)
                    nc.scalar.activation(RA[p % 2][:, :], PB[5 + p % 2][:, N:2 * N], ACT.Copy).then_inc(S["a_rc"], 1)

                def attend(b, more):
                    for h in range(HA):
                        exps(b, h)
                        if h % 2 == 0 and h + 2 < HA:
                            high(b, h // 2 + 1)
                        if h == HA - 2 and more:
                            front_scalar(act, fronts[0], b + 1)
                        if h % 2 and h >= 5:
                            reciprocals(b, (h - 5) // 2)
                    reciprocals(b, HA // 2 - 2)
                    if more:
                        values(b + 1, 0)
                        values(b + 1, 1)
                    reciprocals(b, HA // 2 - 1)
                    if more:
                        values(b + 1, 2)
                        values(b + 1, 3)
                        high(b + 1, 0)

                front_scalar(act, fronts[0], 0)
                for u in range(4):
                    values(0, u)
                high(0, 0)
                with act.Fori(0, B - 1) as b:
                    attend(b, True)
                attend(B - 1, False)

            self_attention()

            act.wait_ge(loaded["x"], 16 * len(plain["x"]))

            def cross_attention():
                ring = PB[7]

                def squares(dst, src):
                    return nc.scalar.activation(dst, src, ACT.Square)

                def copied(k, r, first=False):
                    if r == 3 and not first:
                        act.wait_ge(S["b_vx"], k)
                    act.wait_ge(S["b_r"], 6 * k + r + 1)
                    if r == 0:
                        last = nc.scalar.activation(CXT[0:DC, :], ring[0:DC, :], ACT.Identity, scale=gcol[0:DC, 0:1],
                                                    bias=gcol[0:DC, 1:2])
                    elif r == 1:
                        last = nc.scalar.activation(LT[:, :], ring[:, 0:N], ACT.Identity, scale=gcol[:, 2:3],
                                                    bias=gcol[:, 3:4])
                    elif r == 2:
                        squares(SQ[:, 0:2 * D], ring[:, 0:2 * D])
                        last = nc.scalar.activation(RQ[:, :], ring[:, 0:2 * D], ACT.Copy)
                    else:
                        c0 = 2 * (r - 3)
                        sq = squares(SQ[:, (2 + c0) * D:(4 + c0) * D].rearrange("p (t c) -> p t c", c=D),
                                     ring[:, :].rearrange("p (t c) -> p t c", c=2 * D)[:, :, 0:D])
                        if r != 4:
                            sq.then_inc(S["b_sq"], 1)
                        last = nc.scalar.activation(RKV[:, c0 * 2 * D:(c0 + 2) * 2 * D], ring[:, :], ACT.Copy)
                    last.then_inc(S["b_rc"], 1)

                def high_keys(k):
                    act.wait_ge(S["b_kt"], 2 * k + 1)
                    nc.scalar.activation(KXH[:, 0:M], ring[:, :], ACT.Copy, scale=gcol[:, 6:7]).then_inc(S["b_kh"], 1)

                def high_queries(k):
                    act.wait_ge(S["b_kt"], 2 * k + 2)
                    nc.scalar.activation(KXH[:, M:TK], PB[5][:, 0:N], ACT.Copy, scale=gcol[:, 6:7])
                    for hd in range(HX):
                        last = nc.scalar.activation(QXH[:, hd * N:(hd + 1) * N], PB[5][:, N:2 * N], ACT.Copy,
                                                    scale=gcol[:, 4 + hd:5 + hd])
                    last.then_inc(S["b_kh"], 1)

                def exps(b, u):
                    act.wait_ge(S["b_max"], 4 * b + u + 1)
                    k = 2 * (u % 2)
                    nc.scalar.activation(PX[u % 2][:, 0:M], PB[k][:, :], ACT.Exp, scale=1.0 / math.sqrt(EX),
                                         bias=sm[:, 64 + u:65 + u], accum_out=sm[:, 68 + u:69 + u])
                    nc.scalar.activation(PX[u % 2][:, M:TK], PB[k + 1][:, 0:N], ACT.Exp, scale=1.0 / math.sqrt(EX),
                                         bias=sm[:, 64 + u:65 + u],
                                         accum_out=sm[:, 72 + u:73 + u]).then_inc(S["b_exp"], 1)

                def attend(b, more):
                    if more:
                        copied(b + 1, 0)
                    exps(b, 0)
                    if more:
                        copied(b + 1, 1)
                    exps(b, 1)
                    for u in range(4):
                        act.wait_ge(S["b_pt"], 4 * b + u + 1)
                        nc.scalar.activation(PTX[:, M:TK], PB[5][:, 0:N], ACT.Copy).then_inc(S["b_ptd"], 1)
                        if u < 2:
                            if more:
                                copied(b + 1, 2 * u + 2)
                            exps(b, u + 2)
                            if more:
                                copied(b + 1, 2 * u + 3)
                    if more:
                        high_keys(b + 1)
                    act.wait_ge(S["b_ot"], b + 1)
                    nc.scalar.activation(OTX[:, :], PB[4][:, 0:N], ACT.Copy).then_inc(S["b_otc"], 1)
                    if more:
                        high_queries(b + 1)

                for r in range(6):
                    copied(0, r, first=True)
                high_keys(0)
                high_queries(0)
                with act.Fori(0, B - 1) as b:
                    attend(b, True)
                attend(B - 1, False)

            cross_attention()

            def experts(layer, names, inner):
                r, hs, sg, h2s, ys, yd = names
                F = fronts[layer]
                pairs = len(inner)
                with act.Fori(0, B) as b:
                    act.wait_ge(F.xt_ready, b + 1)
                    nc.scalar.activation(XF2[:, :], PB[BANK_X][:, 0:N], ACT.Copy)
                    nc.scalar.activation(XH[:, :], PB[BANK_X][:, 0:N], ACT.Copy).then_inc(F.xh_ready, 1)
                    if layer == 5:
                        act.wait_ge(S["f_r"], b + 1)
                        for i in range(NT):
                            last = nc.scalar.activation(gt[:, i * E1:(i + 1) * E1], PB[6][:, i * 32:i * 32 + E1],
                                                        ACT.Sigmoid)
                        last.then_inc(S["f_sig"], 1)
                    else:
                        act.wait_ge(S["c_xf"], b + 1)
                        nc.scalar.activation(gt[:, 96:96 + 2 * E0], gt[:, 64:64 + 2 * E0],
                                             ACT.Sigmoid).then_inc(S["c_sig"], 1)
                    for q in range(pairs):
                        n = inner[q][0]
                        act.wait_ge(S[hs], pairs * b + q + 1)
                        nc.scalar.activation(SG[q % 2][:, 0:n * N], PB[2 * (q % 2)][:, 0:n * N],
                                             ACT.Silu).then_inc(S[sg], 1)

            act.wait_ge(layer_done[1], B)
            experts(2, ("c_r", "c_h", "c_sg", "c_h2", "c_y", "c_yd"), [(2, True)] * E0)

            act.wait_ge(layer_done[2], B)
            act.wait_ge(loaded["d"], 16 * len(plain["d"]))
            with act.Fori(0, B) as b:
                F = fronts[3]
                act.wait_ge(F.xt_ready, b + 1)
                nc.scalar.activation(XF[:, :], PB[BANK_X][:, 0:N], ACT.Copy).then_inc(F.xh_ready, 1)
                act.wait_ge(S["d_q"], b + 1)
                nc.scalar.activation(QD[:, :], PB[0][:, 0:N], ACT.Identity, bias=bqk[:, 0:1])
                nc.scalar.activation(KD[:, :], PB[0][:, N:2 * N], ACT.Identity, bias=bqk[:, 1:2]).then_inc(S["d_qc"], 1)
                act.wait_ge(S["d_v"], b + 1)
                nc.scalar.activation(VD[:, :], PB[1][:, 0:N], ACT.Copy).then_inc(S["d_vc"], 1)
                act.wait_ge(S["d_max"], b + 1)
                for i in range(NT):
                    last = nc.scalar.activation(PD[:, i * N:(i + 1) * N], PB[2][:, i * N:(i + 1) * N], ACT.Exp,
                                                scale=1.0 / math.sqrt(D), bias=sm[:, 64 + i:65 + i],
                                                accum_out=sm[:, 68 + i:69 + i])
                last.then_inc(S["d_exp"], 1)
                act.wait_ge(S["d_ot"], b + 1)
                nc.scalar.activation(OTD[:, :], PB[5][:, 0:N], ACT.Copy).then_inc(S["d_otc"], 1)

            act.wait_ge(layer_done[3], B)
            act.wait_ge(loaded["e"], 16 * len(plain["e"]))
            act.wait_ge(S["e_vo0"], 2)

            def values(b):
                act.wait_ge(S["e_v"], b + 1)
                nc.scalar.activation(VS[:, :], PB[6][:, :], ACT.Copy).then_inc(S["e_vc"], 1)

            def keys_queries(b, g):
                act.wait_ge(S["e_k"], 4 * b + g + 1)
                nc.scalar.activation(KHt[:, :].bitcast(f32r), PB[6][:, :], ACT.Copy).then_inc(S["e_kh"], 1)
                act.wait_ge(S["e_q"], 4 * b + g + 1)
                nc.scalar.activation(QT0[:, :], PB[7][:, 0:N], ACT.Identity, bias=bqs[:, g:g + 1]).then_inc(S["e_qc"], 1)

            def masks(b, g):
                act.wait_ge(S["e_qs"], 8 * b + 2 * g + 2)
                for j in range(4):
                    h = 4 * g + j
                    last = nc.scalar.activation(QM[:, h * N:(h + 1) * N], QSt[:, :], ACT.Copy, scale=hmask[:, j:j + 1])
                last.then_inc(S["e_qm"], 1)

            def exps(b, g, k):
                if g:
                    act.wait_ge(S["e_w"], 8 * b + 2 * g + k - 1)
                for j in range(4):
                    n = 4 * k + j
                    act.wait_ge(S["e_st"], 32 * b + 8 * g + n + 1)
                    nc.scalar.activation(PTE[k][:, 2 * j * N:(2 * j + 2) * N], PB[2 + n % 2][:, :], ACT.Exp,
                                         scale=1.0 / math.sqrt(EY)).then_inc(S["e_exp"], 1)

            def outputs(b, g):
                act.wait_ge(S["e_w"], 8 * b + 2 * g + 2)
                nc.scalar.activation(UD[:, g * N:(g + 1) * N], PB[4][:, 0:N], ACT.Copy).then_inc(S["e_uc"], 1)

            def attend(b, more):
                for g in range(4):
                    if g == 0:
                        keys_queries(b, 3)
                        masks(b, 3)
                        if more:
                            front_scalar(act, fronts[4], b + 1)
                            values(b + 1)
                    elif more:
                        keys_queries(b + 1, g - 1)
                    exps(b, g, 0)
                    if g and more:
                        masks(b + 1, g - 1)
                    if g:
                        outputs(b, g - 1)
                    exps(b, g, 1)
                outputs(b, 3)
                act.wait_ge(S["e_h"], b + 1)
                for k in range(2):
                    last = nc.scalar.activation(H1E[:, k * N:(k + 1) * N], PB[5][:, k * N:(k + 1) * N], ACT.Relu,
                                                bias=b1E[:, k:k + 1])
                last.then_inc(S["e_hc"], 1)

            values(0)
            front_scalar(act, fronts[4], 0)
            for g in range(3):
                keys_queries(0, g)
                masks(0, g)
            with act.Fori(0, B - 1) as b:
                attend(b, True)
            attend(B - 1, False)

            act.wait_ge(layer_done[4], B)
            experts(5, ("f_r", "f_h", "f_sg", "f_h2", "f_y", "f_yd"), [(2, False)] * (E1 // 2) + [(1, False)])

        @block.vector
        def _(dve):
            o = Own(dve, own)

            def add_to_x(b, src, layer):
                nc.vector.tensor_tensor(Xt[:, bass.ds(b * NT, NT), :], Xt[:, bass.ds(b * NT, NT), :],
                                        src.rearrange("p (t d) -> p t d", d=D), ALU.add).then_inc(layer_done[layer], 1)

            dve.wait_ge(x_loaded, 16)

            def self_attention():
                F = fronts[0]

                def low(b, p):
                    dve.wait_ge(S["a_gh"], 8 * b + p + 1)
                    nc.vector.tensor_tensor(GL[p % 2][:, :], PB[4][:, :], GH[p % 2][:, :].bitcast(f32),
                                            ALU.subtract).then_inc(S["a_gl"], 1)

                def maximum(b, h):
                    dve.wait_ge(S["a_s"], 16 * b + h + 1)
                    nc.vector.tensor_reduce(sm[:, 128 + 2 * h:130 + 2 * h],
                                            PB[h % 2][:, :].rearrange("p (t m) -> p t m", m=N), AX.X, ALU.max,
                                            negate=True).then_inc(S["a_max"], 1)

                def copy(b, h):
                    dve.wait_ge(S["a_pt"], 16 * b + h + 1)
                    if h % 2:
                        nc.vector.reciprocal(
                            sm[:, 256:256 + NT * HA].rearrange("p (t h) -> p t h", h=HA)[:, :, h - 1:h + 1],
                            sm[:, 192:192 + NT * HA].rearrange("p (t h) -> p t h", h=HA)[:, :, h - 1:h + 1])
                    nc.vector.tensor_copy(PTA[h % 4][:, :], PB[2 + h % 2][:, :]).then_inc(S["a_ptc"], 1)

                def normalise(b, p):
                    dve.wait_ge(S["a_rc"], 8 * b + p + 1)
                    bank = PB[5 + p % 2]
                    nc.vector.tensor_tensor(OTA[:, p * N:(p + 1) * N], bank[:, 0:N], RA[p % 2][:, :],
                                            ALU.mult).then_inc(S["a_on"], 1)

                def attend(b, more):
                    for s in range(HA):
                        if s >= 1:
                            maximum(b, s)
                        if s % 2 and s + 1 < HA:
                            low(b, s // 2 + 1)
                        if s >= 1:
                            copy(b, s - 1)
                        if s == HA - 1 and more:
                            front_low(dve, F, b + 1)
                        if s % 2 and s >= 5:
                            normalise(b, (s - 5) // 2)
                        if s == 6 and more:
                            front_statistics(o, F, b + 1)
                        if s == 10 and more:
                            front_normalise(dve, F, b + 1)
                    copy(b, HA - 1)
                    normalise(b, HA // 2 - 2)
                    normalise(b, HA // 2 - 1)
                    if more:
                        low(b + 1, 0)
                    dve.wait_ge(S["a_y"], b + 1)
                    add_to_x(b, PB[7][:, 0:N], 0)
                    if more:
                        maximum(b + 1, 0)

                o.loop(0, 1)
                front_vector(dve, o, F, 0)
                for q in range(4):
                    dve.wait_ge(S["a_mh"], q + 1)
                    nc.vector.scalar_tensor_tensor(out=ML[:, q * 512:(q + 1) * 512], in0=PB[q][:, :],
                                                   scalar=1.0 / math.sqrt(EA), in1=MH[:, q * 512:(q + 1) * 512].bitcast(f32),
                                                   op0=ALU.mult, op1=ALU.subtract).then_inc(S["a_ml"], 1)
                front_low(dve, F, 0)
                low(0, 0)
                maximum(0, 0)
                o.end(1)
                with dve.Fori(0, B - 1) as b:
                    o.loop(b, 1)
                    attend(b, True)
                o.end(B - 1)
                attend(B - 1, False)

            self_attention()

            dve.wait_ge(layer_done[0], B)
            dve.wait_ge(loaded["x"], 16 * len(plain["x"]))

            def cross_attention():
                ring = PB[7]

                def statistics(k):
                    for i in range(NT):
                        nc.vector.bn_stats(st3[:, MT + i, :], X[:, bass.ds((k * NT + i) * D, D)])
                    dve.wait_ge(S["b_ctx"], 16 * k + 16)
                    for i in range(MT):
                        last = nc.vector.bn_stats(st3[:, i, :], CX[:, i * DC:(i + 1) * DC])
                    o.did(last)
                    o.wait_alone()
                    for i in range(MT + NT):
                        last = nc.vector.bn_aggr(mv3[:, i, :], st3[:, i, :])
                    last.then_inc(S["b_var"], 1)

                def normalise(k):
                    dve.wait_ge(S["b_rstd"], k + 1)
                    for i in range(MT):
                        nc.vector.tensor_scalar(CN[:, i * DC:(i + 1) * DC], CX[:, i * DC:(i + 1) * DC],
                                                mv3[:, i, 0:1], rs[:, i:i + 1], ALU.subtract, ALU.mult)
                    for i in range(NT):
                        last = nc.vector.tensor_scalar(LN2[:, i * D:(i + 1) * D], X[:, bass.ds((k * NT + i) * D, D)],
                                                       mv3[:, MT + i, 0:1], rs[:, MT + i:MT + i + 1], ALU.subtract,
                                                       ALU.mult)
                    last.then_inc(S["b_cn"], 1)

                def mask_row(k):
                    dve.wait_ge(S["b_mask"], 16 * k + 16)
                    nc.vector.tensor_scalar(mkb[:, :], mk8[:, :], -1.0, 1e30, ALU.add,
                                            ALU.mult).then_inc(S["b_mk"], 1)

                def sums(k, half):
                    dve.wait_ge(S["b_sq"], 2 * k + half + 1)
                    nc.vector.reduce_sum(sm[:, 8 * half:8 * half + 8],
                                         SQ[:, 4 * half * D:4 * (half + 1) * D].rearrange("p (n e) -> p n e", e=EX),
                                         AX.X).then_inc(S["b_ss"], 1)

                def over_norms(k, half):
                    dve.wait_ge(S["b_rr"], 2 * k + half + 1)
                    if half == 0:
                        nc.vector.tensor_tensor(
                            QKN[:, 0:2 * D].rearrange("p (n e) -> p n e", e=EX),
                            RQ[:, :].rearrange("p (n e) -> p n e", e=EX),
                            sm[:, 32:36].rearrange("p (n o) -> p n o", o=1).broadcast_to([P, 4, EX]), ALU.mult)
                    t0, n, r0 = (2, 4, 40) if half else (0, 2, 36)
                    dve.wait_ge(S["b_rc"], 6 * k + 2 * half + 4)
                    for i in range(t0, t0 + n):
                        rr = sm[:, 36 + 2 * i:38 + 2 * i]
                        last = nc.vector.tensor_tensor(
                            QKN[:, (2 + i) * D:(3 + i) * D].rearrange("p (n e) -> p n e", e=EX),
                            RKV[:, i * 2 * D:i * 2 * D + D].rearrange("p (n e) -> p n e", e=EX),
                            rr.rearrange("p (n o) -> p n o", o=1).broadcast_to([P, 2, EX]), ALU.mult)
                    if half:
                        last.then_inc(S["b_qkn"], 1)

                def low(dst, src, gain, high):
                    return nc.vector.scalar_tensor_tensor(out=dst, in0=src, scalar=gcol[:, gain:gain + 1],
                                                          in1=high.bitcast(f32), op0=ALU.mult, op1=ALU.subtract)

                def low_keys(k):
                    dve.wait_ge(S["b_kh"], 2 * k + 1)
                    low(KXL[:, 0:M], ring[:, :], 6, KXH[:, 0:M]).then_inc(S["b_kl"], 1)

                def low_queries(k):
                    dve.wait_ge(S["b_kh"], 2 * k + 2)
                    low(KXL[:, M:TK], PB[5][:, 0:N], 6, KXH[:, M:TK])
                    for hd in range(HX):
                        cs = slice(hd * N, (hd + 1) * N)
                        last = low(QXL[:, cs], PB[5][:, N:2 * N], 4 + hd, QXH[:, cs])
                    last.then_inc(S["b_kl"], 1)

                def maximum(b, u):
                    dve.wait_ge(S["b_s"], 4 * b + u + 1)
                    k = 2 * (u % 2)
                    mx = sm[:, 88 + 2 * u:90 + 2 * u]
                    nc.vector.tensor_reduce(mx[:, 0:1], PB[k][:, :], AX.X, ALU.max)
                    o.did(nc.vector.tensor_reduce(mx[:, 1:2], PB[k + 1][:, 0:N], AX.X, ALU.max))
                    o.wait()
                    nc.vector.tensor_scalar(sm[:, 64 + u:65 + u], mx[:, 0:1], mx[:, 1:2], -1.0 / math.sqrt(EX),
                                            ALU.max, ALU.mult).then_inc(S["b_max"], 1)

                def copy(b, u):
                    dve.wait_ge(S["b_pt"], 4 * b + u + 1)
                    nc.vector.tensor_copy(PTX[:, 0:M], PB[4][:, :]).then_inc(S["b_ptc"], 1)

                def attend(b, more, more2):
                    maximum(b, 0)
                    maximum(b, 1)
                    copy(b, 0)
                    maximum(b, 2)
                    copy(b, 1)
                    maximum(b, 3)
                    if more:
                        mask_row(b + 1)
                        sums(b + 1, 0)
                    copy(b, 2)
                    if more:
                        sums(b + 1, 1)
                        if more2:
                            statistics(b + 2)
                        over_norms(b + 1, 0)
                    copy(b, 3)
                    if more:
                        over_norms(b + 1, 1)
                    dve.wait_ge(S["b_exp"], 4 * b + 4)
                    o.did(nc.vector.tensor_tensor(sm[:, 76:80], sm[:, 68:72], sm[:, 72:76], ALU.add))
                    o.wait()
                    o.did(nc.vector.reciprocal(sm[:, 84:88], sm[:, 76:80]))
                    o.wait()
                    dve.wait_ge(S["b_o"], b + 1)
                    for u in range(4):
                        hd, i = u // NT, u % NT
                        cs = slice(i * D + hd * EX, i * D + (hd + 1) * EX)
                        last = nc.vector.tensor_scalar(ONX[:, cs], PB[6][:, cs], sm[:, 84 + u:85 + u], None, ALU.mult)
                    last.then_inc(S["b_on"], 1)
                    if more:
                        low_keys(b + 1)
                        low_queries(b + 1)
                        if more2:
                            normalise(b + 2)
                    dve.wait_ge(S["b_y"], b + 1)
                    add_to_x(b, PB[6][:, 0:N], 1)

                o.loop(0, 2)
                statistics(0)
                normalise(0)
                mask_row(0)
                sums(0, 0)
                sums(0, 1)
                over_norms(0, 0)
                over_norms(0, 1)
                statistics(1)
                low_keys(0)
                low_queries(0)
                normalise(1)
                o.end(1)
                with dve.Fori(0, B - 2) as b:
                    o.loop(b, 7)
                    attend(b, True, True)
                o.end(B - 2)
                o.loop(0, 6)
                attend(B - 2, True, False)
                o.end(1)
                o.loop(0, 6)
                attend(B - 1, False, False)
                o.end(1)

            cross_attention()

            def experts(layer, names, inner, router, weight):
                r, hs, sg, h2s, ys, yd = names
                F = fronts[layer]
                pairs = len(inner)
                with dve.Fori(0, B) as b:
                    o.loop(b, 6 if layer == 2 else 16)
                    front_vector(dve, o, F, b)
                    front_low(dve, F, b)
                    router(b)

                    def add(q):
                        dve.wait_ge(S[ys], pairs * b + q + 1)
                        n, joint = inner[q]
                        for k in range(1 if joint else n):
                            if k == 0 and q > 0:
                                dve.wait_ge(S[yd], (pairs - 1) * b + q)
                            else:
                                o.wait()
                            for i in range(NT):
                                xs = X[:, bass.ds((b * NT + i) * D, D)]
                                last = nc.vector.scalar_tensor_tensor(
                                    out=xs, in0=PB[4 + q % 2][:, (k * NT + i) * D:(k * NT + i + 1) * D],
                                    scalar=weight(i, q if joint else 2 * q + k), in1=xs, op0=ALU.mult, op1=ALU.add)
                            if not joint and k < n - 1:
                                o.did(last)
                        last.then_inc(S[yd] if q < pairs - 1 else layer_done[layer], 1)

                    for q in range(pairs):
                        n = inner[q][0]
                        dve.wait_ge(S[sg], pairs * b + q + 1)
                        nc.vector.tensor_tensor(H2[q % 2][:, 0:n * N], SG[q % 2][:, 0:n * N],
                                                PB[2 * (q % 2) + 1][:, 0:n * N], ALU.mult).then_inc(S[h2s], 1)
                        if q >= 1:
                            add(q - 1)
                    add(pairs - 1)
                o.end(B)

            LOW, TAKEN = -3e38, -1e38

            def router0(b):
                dve.wait_ge(S["c_r"], b + 1)
                for i in range(NT):
                    last = nc.vector.tensor_copy(gt[:, 16 * i:16 * i + E0], PB[6][:, 32 * i:32 * i + E0])
                o.did(last)
                o.wait_alone()
                for i in range(NT):
                    last = nc.vector.max(gt[:, 32 + 8 * i:40 + 8 * i], gt[:, 16 * i:16 * i + E0])
                o.did(last)
                o.wait()
                for i in range(NT):
                    last = nc.vector.tensor_tensor(gt[:, 48 + i:49 + i], gt[:, 32 + 8 * i:33 + 8 * i],
                                                   gt[:, 33 + 8 * i:34 + 8 * i], ALU.add)
                    nc.vector.memset(gt[:, 34 + 8 * i:40 + 8 * i], LOW)
                o.did(nc.vector.memset(gt[:, 50:51], 0.0))
                o.wait()
                for i in range(NT):
                    last = nc.vector.tensor_scalar(gt[:, 64 + 8 * i:72 + 8 * i], gt[:, 16 * i:16 * i + E0], 2.0,
                                                   gt[:, 48 + i:49 + i], ALU.mult, ALU.subtract)
                last.then_inc(S["c_xf"], 1)
                for i in range(NT):
                    last = nc.vector.match_replace(gt[:, 128 + 16 * i:142 + 16 * i], gt[:, 32 + 8 * i:40 + 8 * i],
                                                   gt[:, 16 * i:16 * i + 14], TAKEN)
                o.did(last)
                o.wait()
                dve.wait_ge(S["c_sig"], b + 1)
                for i in range(NT):
                    last = nc.vector.scalar_tensor_tensor(
                        out=gt[:, 160 + 8 * i:168 + 8 * i], in0=gt[:, 128 + 16 * i:136 + 16 * i], scalar=TAKEN,
                        in1=gt[:, 96 + 8 * i:104 + 8 * i], op0=ALU.is_equal, op1=ALU.mult)
                o.did(last)
                o.wait()

            def router1(b):
                dve.wait_ge(S["f_sig"], b + 1)
                for i in range(NT):
                    last = nc.vector.tensor_tensor(gt[:, 32 + 16 * i:48 + 16 * i], gt[:, 16 * i:16 * i + E1], ebF[:, :],
                                                   ALU.add)
                o.did(last)
                o.wait_alone()
                for i in range(NT):
                    last = nc.vector.max(gt[:, 64 + 8 * i:72 + 8 * i], gt[:, 32 + 16 * i:48 + 16 * i])
                o.did(last)
                o.wait_alone()
                for i in range(NT):
                    last = nc.vector.match_replace(gt[:, 80 + 16 * i:96 + 16 * i], gt[:, 64 + 8 * i:72 + 8 * i],
                                                   gt[:, 32 + 16 * i:48 + 16 * i], TAKEN)
                o.did(last)
                o.wait()
                for i in range(NT):
                    last = nc.vector.scalar_tensor_tensor(
                        out=gt[:, 112 + 16 * i:128 + 16 * i], in0=gt[:, 80 + 16 * i:96 + 16 * i], scalar=TAKEN,
                        in1=gt[:, 16 * i:16 * i + E1], op0=ALU.is_equal, op1=ALU.mult)
                o.did(last)
                o.wait()
                o.did(nc.vector.reduce_sum(gt[:, 144:146], gt[:, 112:144].rearrange("p (t e) -> p t e", e=E1), AX.X))
                o.wait()
                o.did(nc.vector.reciprocal(gt[:, 146:148], gt[:, 144:146]))
                o.wait()
                for i in range(NT):
                    last = nc.vector.tensor_scalar(gt[:, 160 + 32 * i:176 + 32 * i], gt[:, 112 + 16 * i:128 + 16 * i],
                                                   gt[:, 146 + i:147 + i], ROUTE_SCALE, ALU.mult, ALU.mult)
                o.did(last)
                o.wait()

            dve.wait_ge(layer_done[1], B)
            for i in range(NT):
                last = nc.vector.memset(gt[:, 16 * i + E0:16 * i + 16], LOW)
            last.then_inc(own, 1)
            o.base += 1
            o.wait()
            experts(2, ("c_r", "c_h", "c_sg", "c_h2", "c_y", "c_yd"), [(2, True)] * E0, router0,
                    lambda i, x: gt[:, 160 + 8 * i + x:161 + 8 * i + x])

            dve.wait_ge(layer_done[2], B)
            with dve.Fori(0, B) as b:
                o.loop(b, 3)
                F = fronts[3]
                front_vector(dve, o, F, b)
                dve.wait_ge(S["d_s"], b + 1)
                o.did(nc.vector.tensor_reduce(sm[:, 88:90], PB[2][:, :].rearrange("p (t m) -> p t m", m=N), AX.X,
                                              ALU.max))
                o.wait()
                nc.vector.tensor_scalar(sm[:, 64:66], sm[:, 88:90], -1.0 / math.sqrt(D), None,
                                        ALU.mult).then_inc(S["d_max"], 1)
                dve.wait_ge(S["d_pt"], b + 1)
                nc.vector.tensor_copy(PTD[:, :], PB[3][:, :]).then_inc(S["d_ptc"], 1)
                dve.wait_ge(S["d_o"], b + 1)
                o.did(nc.vector.reciprocal(sm[:, 72:74], sm[:, 68:70]))
                o.wait()
                for i in range(NT):
                    last = nc.vector.tensor_scalar(OND[:, i * D:(i + 1) * D], PB[4][:, i * D:(i + 1) * D],
                                                   sm[:, 72 + i:73 + i], None, ALU.mult)
                last.then_inc(S["d_on"], 1)
                dve.wait_ge(S["d_y"], b + 1)
                add_to_x(b, PB[6][:, 0:N], 3)
            o.end(B)

            dve.wait_ge(layer_done[3], B)
            dve.wait_ge(loaded["e"], 16 * len(plain["e"]))
            dve.wait_ge(S["e_vo0"], 2)
            nm4 = NMX[:, :].rearrange("p (t c) -> p t c", c=P)

            def keys(b, g):
                dve.wait_ge(S["e_kh"], 4 * b + g + 1)
                nc.vector.scalar_tensor_tensor(out=KS[:, g * M:(g + 1) * M], in0=KHt[:, :], scalar=selk[:, 0:1],
                                               in1=PB[6][:, :], op0=ALU.mult, op1=ALU.add).then_inc(S["e_ks"], 1)

            def queries(b, g, first=False):
                dve.wait_ge(S["e_qc"], 4 * b + g + 1)
                nc.vector.tensor_copy(QHt[:, :].bitcast(f32r), QT0[:, :]).then_inc(S["e_qs"], 1)
                dve.wait_ge(S["e_qs"], 8 * b + 2 * g + 1)
                if not first:
                    dve.wait_ge(S["e_qm"], 4 * b + g)
                nc.vector.scalar_tensor_tensor(out=QSt[:, :].bitcast(f32r), in0=QHt[:, :], scalar=selq[:, 0:1],
                                               in1=QT0[:, :], op0=ALU.mult, op1=ALU.add).then_inc(S["e_qs"], 1)

            def maxima(b, g, first=False):
                if not first:
                    dve.wait_ge(S["e_nr"], 4 * b + g)
                for n in range(8):
                    j, i = n // 2, n % 2
                    dve.wait_ge(S["e_s"], 32 * b + 8 * g + n + 1)
                    last = nc.vector.tensor_reduce(NMX[:, i * P + 96 + j:i * P + 97 + j], PB[n % 2][:, :], AX.X,
                                                   ALU.max, negate=True)
                    if n < 7:
                        last.then_inc(S["e_max"], 1)
                o.did(last)
                o.wait()
                nc.vector.tensor_copy(nm4[:, :, 100:104], nm4[:, :, 96:100]).then_inc(S["e_max"], 1)

            def place_maxima(b, g):
                dve.wait_ge(S["e_nr"], 4 * b + g + 1)
                o.did(nc.vector.tensor_copy(NRH[96:P, :].bitcast(f32r), PB[5][96:P, 0:N]))
                o.wait()
                o.did(nc.vector.scalar_tensor_tensor(out=NRL[96:P, :].bitcast(f32r), in0=NRH[96:P, :],
                                                     scalar=seln[96:P, 0:1], in1=PB[5][96:P, 0:N], op0=ALU.mult,
                                                     op1=ALU.add))
                o.wait()
                dve.wait_ge(S["e_qm"], 4 * b + g + 1)
                for j in range(4):
                    h = 4 * g + j
                    last = nc.vector.tensor_scalar(QM[96:P, h * N:(h + 1) * N], NRL[96:P, :], hmask[96:P, j:j + 1],
                                                   None, ALU.mult)
                last.then_inc(S["e_nm"], 1)

            def attend(b, more):
                for g in range(4):
                    place_maxima(b, g)
                    if g == 0:
                        keys(b, 3)
                        queries(b, 3)
                        if more:
                            front_vector(dve, o, fronts[4], b + 1)
                    elif more:
                        keys(b + 1, g - 1)
                        queries(b + 1, g - 1)
                    if g < 3:
                        maxima(b, g + 1)
                    elif more:
                        maxima(b + 1, 0)
                    if g == 0 and more:
                        front_low(dve, fronts[4], b + 1)
                dve.wait_ge(S["e_od"], b + 1)
                o.did(nc.vector.reciprocal(RDE[:, :], PB[4][:, N:2 * N]))
                o.wait()
                nc.vector.tensor_tensor(OE[:, :], PB[4][:, 0:N], RDE[:, :], ALU.mult).then_inc(S["e_o"], 1)
                dve.wait_ge(S["e_y"], b + 1)
                add_to_x(b, PB[4][:, 0:N], 4)

            o.loop(0, 2)
            front_vector(dve, o, fronts[4], 0)
            front_low(dve, fronts[4], 0)
            for g in range(3):
                keys(0, g)
                queries(0, g, first=g == 0)
            maxima(0, 0, first=True)
            o.end(1)
            with dve.Fori(0, B - 1) as b:
                o.loop(b, 14)
                attend(b, True)
            o.end(B - 1)
            o.loop(0, 12)
            attend(B - 1, False)
            o.end(1)

            dve.wait_ge(layer_done[4], B)
            dve.wait_ge(loaded["f"], 16 * len(plain["f"]))
            for i in range(NT):
                last = nc.vector.memset(gt[:, 176 + 32 * i:177 + 32 * i], 1.0)
            last.then_inc(own, 1)
            o.base += 1
            o.wait()
            experts(5, ("f_r", "f_h", "f_sg", "f_h2", "f_y", "f_yd"), [(2, False)] * (E1 // 2) + [(1, False)],
                    router1, lambda i, x: gt[:, 160 + 32 * i + x:161 + 32 * i + x])


def kernel(**inputs):
    import numpy as np
    import concourse.bacc as bacc
    from concourse import mybir as mb
    from concourse.bass_utils import run_bass_kernel_spmd

    v = {k: np.asarray(a) for k, a in inputs.items()}
    f4 = np.float32

    def cols(a, k):
        return a.reshape(-1, P, k).transpose(1, 0, 2).reshape(P, -1)

    wq, wk, wv = (v["L0_attn_W" + n] for n in "qkv")
    g4 = np.arange(P)
    quad, off = g4 // 32, g4 % 32
    a = {
        "ident": np.eye(P, dtype=f4), "onesrow": np.ones((1, P), f4),
        "x": cols(v["x"].reshape(B * N, D), D),
        "wqT": wq.transpose(2, 0, 1).reshape(EA, HA * D), "wkT": wk.transpose(2, 0, 1).reshape(EA, HA * D),
        "wv": wv.transpose(1, 0, 2).reshape(D, HA * EA),
        "wp": cols(v["L0_attn_Wp"].reshape(EA, HA, D).transpose(1, 0, 2).reshape(HA * EA, D), D),
        "bp": v["L0_attn_bp"][None],
        "wqx": v["L0_xattn_Wq"].T, "wox": v["L0_xattn_Wo"].T, "wkvx": v["L0_xattn_Wkv"].T, "wlkv": v["L0_xattn_Wlkv"].T,
        "box": v["L0_xattn_bo"][None],
        "ctx": v["ctx_768"].reshape(B, MT, P, DC).transpose(0, 2, 1, 3).reshape(B, P, MT * DC),
        "mask": v["mask_BxS2_bk0"].reshape(B, M),
    }
    gcol = np.zeros((P, 7), f4)
    gcol[:DC, 0], gcol[:DC, 1] = v["L0_xattn_ln_x_g"], v["L0_xattn_ln_x_b"]
    gcol[:, 2], gcol[:, 3] = v["L0_xattn_ln_l_g"], v["L0_xattn_ln_l_b"]
    gcol[:EX, 4], gcol[EX:, 5], gcol[:, 6] = v["L0_xattn_qn_g"], v["L0_xattn_qn_g"], np.tile(v["L0_xattn_kn_g"], HX)
    a["gcol"] = gcol
    a["w1"] = v["L0_ffn_w1"].transpose(2, 0, 1).reshape(D, E0 * I0)
    a["w3"] = v["L0_ffn_w3"].transpose(2, 0, 1).reshape(D, E0 * I0)
    a["w2"] = v["L0_ffn_w2"].transpose(2, 0, 1).reshape(2, P, E0, D).transpose(1, 2, 0, 3).reshape(P, 2 * E0 * D)
    a["wgc"] = v["L0_ffn_wg"].T
    for n, s in (("wqd", "w_q"), ("wkd", "w_k"), ("wvd", "w_v"), ("wod", "w_out")):
        a[n] = v["L1_attn_" + s].T
    a["bqk"] = np.stack([v["L1_attn_b_q"], v["L1_attn_b_k"]], 1)
    a["bvd"], a["bod"] = v["L1_attn_b_v"][None], v["L1_attn_b_out"][None]

    wks, wqs = np.zeros((DC + 1, 4, P), f4), np.zeros((D, 4, P), f4)
    bqs = np.zeros((P, 4), f4)
    for g in range(4):
        for r in range(3):
            hc, to = slice(32 * g, 32 * g + 32), slice(32 * r, 32 * r + 32)
            wks[:DC, g, to], wks[DC, g, to] = v["L1_xattn_Wk"][:, hc], v["L1_xattn_bk"][hc]
            wqs[:, g, to], bqs[to, g] = v["L1_xattn_Wq"][:, hc], v["L1_xattn_bq"][hc]
        wks[DC, g, 96:104] = 1.0
    a["wks"], a["wqs"], a["bqs"] = wks.reshape(DC + 1, 4 * P), wqs.reshape(D, 4 * P), bqs
    wks_full = np.zeros((P, 4 * P), f4)
    wks_full[:DC + 1] = a["wks"]
    a["wks"] = wks_full
    a["wve"] = np.concatenate([v["L1_xattn_Wv"], v["L1_xattn_bv"][None]])
    a["w1e"] = v["L1_xattn_W1"]
    a["w2e"] = cols(v["L1_xattn_W2"], D)
    a["b1e"], a["b2e"] = v["L1_xattn_b1"].reshape(2, P).T, v["L1_xattn_b2"][None]
    a["ctxT"] = np.concatenate([v["ctx_768"].transpose(0, 2, 1), np.ones((B, 1, M), f4)], 1)
    cu, cd = np.zeros((P, 4, P), f4), np.zeros((P, 4, P), f4)
    for g in range(4):
        for j in range(4):
            for d in range(EY):
                cu[32 * j + d, g, 8 * (4 * g + j) + d] = 1.0
                cd[32 * j + EY, g, 8 * (4 * g + j) + d] = 1.0
    a["cu"], a["cd"] = cu.reshape(P, 4 * P), cd.reshape(P, 4 * P)
    a["selq"] = -(quad == 1).astype(f4)[:, None]
    a["selk"] = -(quad == 2).astype(f4)[:, None]
    a["seln"] = -((quad == 3) & (off >= 4) & (off < 8)).astype(f4)[:, None]
    head = np.where(quad < 3, off // EY, np.where(off < 8, off % 4, -1))
    a["hmask"] = (head[:, None] == np.arange(4)[None]).astype(f4)

    def fuse(routed, shared):
        return np.concatenate([routed, shared[None]]).transpose(2, 0, 1).reshape(P, STG)

    a["fg"] = fuse(v["L1_ffn_w_gate"], v["L1_ffn_shared_gate_w"])
    a["fu"] = fuse(v["L1_ffn_w_up"], v["L1_ffn_shared_up_w"])
    a["fd"] = fuse(v["L1_ffn_w_down"], v["L1_ffn_shared_down_w"])
    a["wgf"] = v["L1_ffn_gate_w"].T
    a["ebf"] = np.broadcast_to(v["L1_ffn_expert_bias"][None], (P, E1))

    nc = bacc.Bacc("TRN2", target_bir_lowering=False, num_devices=1)
    arrays, aps = {}, {}
    for name, arr in a.items():
        arr = np.ascontiguousarray(arr)
        arrays[f"in_{name}"] = arr
        aps[name] = nc.dram_tensor(f"in_{name}", arr.shape, mb.dt.from_np(arr.dtype), kind="ExternalInput").ap()
    out = nc.dram_tensor("out_0", (P, B * NT * D), mb.dt.float32, kind="ExternalOutput").ap()
    decoder(nc, aps, out)
    r = run_bass_kernel_spmd(nc, [arrays], core_ids=[0])
    y = r.results[0]["out_0"]
    return y.reshape(P, B * NT, D).transpose(1, 0, 2).reshape(B, N, D)
```

```python
import math
from contextlib import ExitStack

import concourse.bass as bass
from concourse import mybir

B, N, M, D, DC = 8, 256, 512, 128, 96
P = 128
NT, MT = N // P, M // P
HA, EA = 16, 64
HX, EX = 2, 64
HY, EY = 16, 8
E0, I0 = 8, 256
E1, K1, I1 = 16, 8, 128
TK = N + M
ROUTE_SCALE = 2.826
LN_EPS = 1e-5
STG = (E1 + 1) * I1


def decoder(nc, t, out):
    f32, f32r, u8, bf16 = mybir.dt.float32, mybir.dt.float32r, mybir.dt.uint8, mybir.dt.bfloat16
    ALU, ACT, AX = mybir.AluOpType, mybir.ActivationFunctionType, mybir.AxisListType

    ctx = ExitStack()
    with ctx:
        def sem(name):
            return ctx.enter_context(nc.semaphore(name))

        class Arena:

            def __init__(self):
                self.stack = ExitStack()
                self.free = nc.sbuf_bytes_remaining

            def sb(self, name, cols, dt=f32, parts=P):
                made = self.stack.enter_context(nc.sbuf_tensor(name, [parts, cols], dt))
                self.used = self.free - nc.sbuf_bytes_remaining
                return made

        def keep(name, cols, dt=f32, parts=P):
            return ctx.enter_context(nc.sbuf_tensor(name, [parts, cols], dt))

        X = keep("X", B * NT * D)
        Xt = X[:, :].rearrange("p (t d) -> p t d", d=D)
        stage = [keep("stage0", STG), keep("stage1", STG)]
        ident = keep("ident", P)
        onesrow = keep("onesrow", P, parts=1)
        halves = keep("halves", 32)
        st = keep("st", 8 * 6)
        mv = keep("mv", 8 * 2)
        vs = keep("vs", 8)
        rs = keep("rs", 8)
        xn = keep("xn", NT * D)
        XH = keep("XH", N, f32r)
        XL = keep("XL", N, f32r)
        sm = keep("sm", 1024)
        st3 = st[:, :].rearrange("p (t s) -> p t s", s=6)
        mv3 = mv[:, :].rearrange("p (t s) -> p t s", s=2)
        xn3 = xn[:, :].rearrange("p (t d) -> p t d", d=D)

        a = Arena()
        MH, ML = a.sb("MH", HA * D, f32r), a.sb("ML", HA * D, f32r)
        WVH, WVL = a.sb("WVH", HA * EA, f32r), a.sb("WVL", HA * EA, f32r)
        WP = a.sb("WP", HA * EA)
        bp = a.sb("bp", D, parts=1)
        GH = [a.sb(f"GH{i}", 2 * N, f32r) for i in range(2)]
        GL = [a.sb(f"GL{i}", 2 * N, f32r) for i in range(2)]
        PA = [a.sb(f"PA{i}", NT * N) for i in range(2)]
        PTA = [a.sb(f"PTA{i}", NT * N) for i in range(4)]
        VA = a.sb("VA", NT * HA * EA)
        RA = [a.sb(f"RA{i}", N) for i in range(2)]
        RB = [a.sb(f"RB{i}", NT * 2 * EA) for i in range(2)]
        OTA = a.sb("OTA", HA * EA // P * N)
        a.stack.close()
        e = Arena()
        WKSH, WKSL = e.sb("WKSH", 4 * P, f32r), e.sb("WKSL", 4 * P, f32r)
        WQSH, WQSL = e.sb("WQSH", 4 * P, f32r), e.sb("WQSL", 4 * P, f32r)
        WVE = e.sb("WVE", D)
        bqs = e.sb("bqs", 4)
        W1E, W2E = e.sb("W1E", 2 * D), e.sb("W2E", 2 * D)
        b1E, b2E = e.sb("b1E", 2), e.sb("b2E", D, parts=1)
        CU, CD = e.sb("CU", 4 * P), e.sb("CD", 4 * P)
        selq, selk, seln, hmask = e.sb("selq", 1), e.sb("selk", 1), e.sb("seln", 1), e.sb("hmask", 4)
        CTE = e.sb("CTE", M)
        CEH, CEL = e.sb("CEH", M, f32r), e.sb("CEL", M, f32r)
        KS = e.sb("KS", 4 * M, f32r)
        QT0, QHt, QSt = e.sb("QT0", N), e.sb("QHt", N), e.sb("QSt", N)
        QM = e.sb("QM", HY * N, f32r)
        VO = e.sb("VO", MT * HY * 32)
        NMX = e.sb("NMX", NT * P)
        NRH = e.sb("NRH", N)
        NRL = e.sb("NRL", N)
        PTE = [e.sb(f"PTE{i}", 2 * MT * N) for i in range(2)]
        VS = e.sb("VS", M)
        UD = e.sb("UD", 4 * N)
        KHt = e.sb("KHt", M)
        RDE, OE, H1E = e.sb("RDE", N), e.sb("OE", N), e.sb("H1E", 2 * N)
        e.stack.close()
        big = Arena()
        big.sb("arena1_space", max(a.used, e.used) // 4)
        ctx.enter_context(big.stack)

        c = Arena()
        W1H, W1L = c.sb("W1H", E0 * I0, f32r), c.sb("W1L", E0 * I0, f32r)
        W3H, W3L = c.sb("W3H", E0 * I0, f32r), c.sb("W3L", E0 * I0, f32r)
        W2C = c.sb("W2C", 2 * E0 * D)
        WGC = c.sb("WGC", E0)
        c.stack.close()
        f = Arena()
        FGH, FGL = f.sb("FGH", STG, f32r), f.sb("FGL", STG, f32r)
        FUH, FUL = f.sb("FUH", STG, f32r), f.sb("FUL", STG, f32r)
        FD = f.sb("FD", STG)
        WGF = f.sb("WGF", E1)
        ebF = f.sb("ebF", E1)
        f.stack.close()
        big2 = Arena()
        big2.sb("arena2_space", max(c.used, f.used) // 4)
        ctx.enter_context(big2.stack)

        x = Arena()
        WQX, WOX = x.sb("WQX", D), x.sb("WOX", D)
        WKVX, WLKV = x.sb("WKVX", 2 * D), x.sb("WLKV", 2 * D)
        boX = x.sb("boX", D, parts=1)
        gcol = x.sb("gcol", 7)
        CX = x.sb("CX", MT * DC)
        CN = x.sb("CN", MT * DC)
        LN2 = xn
        CXT, LT = x.sb("CXT", M), x.sb("LT", N)
        RQ, RKV = x.sb("RQ", NT * D), x.sb("RKV", 6 * 2 * D)
        QKN = x.sb("QKN", 8 * D)
        SQ = QKN
        VX = x.sb("VX", 6 * D)
        KXH, KXL = x.sb("KXH", TK, f32r), x.sb("KXL", TK, f32r)
        QXH, QXL = x.sb("QXH", HX * N, f32r), x.sb("QXL", HX * N, f32r)
        mk8 = x.sb("mk8", M, u8, parts=1)
        mkb = x.sb("mkb", M, bf16, parts=1)
        onesb = x.sb("onesb", P, bf16, parts=1)
        PX = [x.sb(f"PX{i}", TK) for i in range(2)]
        PTX = x.sb("PTX", TK)
        ONX, OTX = sm[:, 448:448 + N], sm[:, 704:704 + N]
        x.stack.close()
        x = Arena()
        WQD, WKD, WVD, WOD = (x.sb(n, D) for n in ("WQD", "WKD", "WVD", "WOD"))
        bqk = x.sb("bqk", 2)
        bvD, boD = x.sb("bvD", D, parts=1), x.sb("boD", D, parts=1)
        XF = x.sb("XF", N)
        QD, KD = x.sb("QD", N), x.sb("KD", N)
        VD = [x.sb(f"VD{i}", N) for i in range(2)]
        PD, PTD = x.sb("PD", NT * N), x.sb("PTD", NT * N)
        OND, OTD = x.sb("OND", N), x.sb("OTD", N)
        x.stack.close()
        w = Arena()
        SG = [w.sb(f"SG{i}", 2 * N) for i in range(2)]
        H2 = [w.sb(f"H2{i}", 2 * N) for i in range(2)]
        XF2 = w.sb("XF2", N)
        gt = w.sb("gt", 512)
        w.stack.close()

        PB = [ctx.enter_context(nc.psum_tensor(f"PB{i}", [P, 512], f32)) for i in range(8)]

        def mm3(o, lh, ll, rh, rl, first=True, last=True):
            nc.tensor.matmul(o, lh, rh, start=first, stop=False)
            nc.tensor.matmul(o, ll, rh, start=False, stop=False)
            return nc.tensor.matmul(o, lh, rl, start=False, stop=last)

        def mm(o, l, r, first=True, last=True):
            return nc.tensor.matmul(o, l, r, start=first, stop=last)

        consts_loaded = sem("consts_loaded")
        x_loaded = sem("x_loaded")
        out_stored = sem("out_stored")
        own = sem("vector_own")
        pool_own = sem("pool_own")
        layer_done = [sem(f"layer{i}_done") for i in range(6)]

        class Front:

            def __init__(self, n):
                self.var_ready = sem(f"var{n}_ready")
                self.rstd_ready = sem(f"rstd{n}_ready")
                self.xn_ready = sem(f"xn{n}_ready")
                self.xt_ready = sem(f"xt{n}_ready")
                self.xh_ready = sem(f"xh{n}_ready")
                self.xl_ready = sem(f"xl{n}_ready")
                self.xf_ready = sem(f"xf{n}_ready") if n in (2, 5) else None

        fronts = [Front(i) if i != 1 else None for i in range(6)]
        own_count = [0]

        class Own:

            def __init__(self, eng, s):
                self.eng, self.s, self.base, self.k, self.per, self.b = eng, s, 0, 0, 0, 0

            def loop(self, b, per):
                self.b, self.per, self.k = b, per, 0

            def end(self, times):
                assert self.k == self.per, (self.k, self.per)
                self.base += self.per * times
                self.k = self.per = self.b = 0

            def did(self, ins):
                self.k += 1
                ins.then_inc(self.s, 1)

            def wait(self):
                self.eng.wait_ge(self.s, self.b * self.per + (self.base + self.k))

            def wait_alone(self):
                wait_alone(self.eng, self.s, self.b * self.per + (self.base + self.k))

        BANK_X = 7

        def front_statistics(o, F, b):
            for i in range(NT):
                last = nc.vector.bn_stats(st3[:, i, :], X[:, bass.ds((b * NT + i) * D, D)])
            o.did(last)
            o.wait_alone()
            for i in range(NT):
                last = nc.vector.bn_aggr(mv3[:, i, :], st3[:, i, :])
            last.then_inc(F.var_ready, 1)

        def front_normalise(dve, F, b):
            dve.wait_ge(F.rstd_ready, b + 1)
            for i in range(NT):
                last = nc.vector.tensor_scalar(xn3[:, i, :], X[:, bass.ds((b * NT + i) * D, D)], mv3[:, i, 0:1],
                                               rs[:, i:i + 1], ALU.subtract, ALU.mult)
            last.then_inc(F.xn_ready, 1)

        def front_vector(dve, o, F, b):
            front_statistics(o, F, b)
            front_normalise(dve, F, b)

        def front_pool(pool, po, F, b):
            wait_alone(pool, F.var_ready, b + 1)
            po.did(nc.gpsimd.tensor_scalar(vs[:, 0:NT], mv3[:, 0:NT, 1], LN_EPS, None, ALU.add))
            po.wait()
            nc.gpsimd.tensor_tensor(rs[:, 0:NT], vs[:, 0:NT], halves[:, 0:NT], ALU.pow).then_inc(F.rstd_ready, 1)

        def front_tensor(pe, F, b):
            pe.wait_ge(F.xn_ready, b + 1)
            for i in range(NT):
                last = nc.tensor.transpose(PB[BANK_X][:, i * P:(i + 1) * P], xn3[:, i, :], ident[:, :])
            last.then_inc(F.xt_ready, 1)

        def front_scalar(act, F, b):
            act.wait_ge(F.xt_ready, b + 1)
            nc.scalar.activation(XH[:, :], PB[BANK_X][:, 0:N], ACT.Copy).then_inc(F.xh_ready, 1)

        def front_low(dve, F, b):
            dve.wait_ge(F.xh_ready, b + 1)
            nc.vector.tensor_tensor(XL[:, :], PB[BANK_X][:, 0:N], XH[:, :].bitcast(f32),
                                    ALU.subtract).then_inc(F.xl_ready, 1)

        S = {}
        for name in ("a_mready a_mh a_ml a_v a_vc a_g a_gh a_gl a_s a_max a_exp a_pt a_ptc a_rb a_o a_rc a_on a_y "
                     "b_ctx b_mask b_ones b_var b_rstd b_cn b_r b_rc b_sq b_ss b_rr b_qkn b_kt b_kh b_kl b_vx b_mk "
                     "b_s b_max b_exp b_pt b_ptc b_ptd b_o b_on b_ot b_otc b_y "
                     "c_r c_h c_sg c_h2 c_y c_yd c_xf c_sig "
                     "d_q d_qc d_v d_vc d_v2 d_s d_max d_exp d_pt d_ptc d_o d_on d_ot d_otc d_y "
                     "e_ctx e_w e_vo e_split e_k e_kh e_ks e_v e_vc e_q e_qc e_qs e_qm e_s e_max e_nr e_nl e_nm e_st e_exp e_uc "
                     "e_od e_o e_h e_hc e_y e_vo0 "
                     "f_r f_sig f_h f_sg f_h2 f_y f_yd "
                     "qk_in w_in0 w_in1 w_split").split():
            S[name] = sem(name)

        wait_passed = sem("wait_passed")

        def wait_alone(eng, s, value):
            eng.wait_ge(s, value)
            eng.sem_inc(wait_passed, 1)

        split_a = [("wv", P, HA * EA, WVH, WVL)]
        split_c = [("w1", P, E0 * I0, W1H, W1L), ("w3", P, E0 * I0, W3H, W3L)]
        split_e = [("wks", P, 4 * P, WKSH, WKSL), ("wqs", P, 4 * P, WQSH, WQSL)]
        split_f = [("fg", P, STG, FGH, FGL), ("fu", P, STG, FUH, FUL)]
        splits = [(i, None) for i in split_a] + [(i, None) for i in split_c] + [(i, 0) for i in split_e] \
            + [(i, 2) for i in split_f]
        SPLIT_A, SPLIT_C, SPLIT_E, SPLIT_F = 1, 3, 5, 7

        plain = {
            "a": [(WP, "wp"), (bp, "bp")],
            "x": [(WQX, "wqx"), (WOX, "wox"), (WKVX[0:DC, :], "wkvx"), (WLKV, "wlkv"), (boX, "box"), (gcol, "gcol")],
            "c": [(W2C, "w2"), (WGC, "wgc")],
            "d": [(WQD, "wqd"), (WKD, "wkd"), (WVD, "wvd"), (WOD, "wod"), (bqk, "bqk"), (bvD, "bvd"), (boD, "bod")],
            "e": [(WVE[0:DC + 1, :], "wve"), (bqs, "bqs"), (W1E, "w1e"), (W2E, "w2e"), (b1E, "b1e"), (b2E, "b2e"),
                  (CU, "cu"), (CD, "cd"), (selq, "selq"), (selk, "selk"), (seln, "seln"), (hmask, "hmask")],
            "f": [(FD, "fd"), (WGF, "wgf"), (ebF, "ebf")],
        }
        loaded = {k: sem(f"loaded_{k}") for k in plain}

        block = ctx.enter_context(nc.Block())

        @block.sync
        def _(sp):
            sp.dma_start(stage[0][0:EA, 0:HA * D], t["wqT"]).then_inc(S["qk_in"], 16)
            sp.dma_start(stage[1][0:EA, 0:HA * D], t["wkT"]).then_inc(S["qk_in"], 16)
            sp.dma_start(X[:, :], t["x"]).then_inc(x_loaded, 16)
            sp.dma_start(OTA[:, 0:HA * EA], t["wv"]).then_inc(S["w_in0"], 16)
            sp.dma_start(ident[:, :], t["ident"]).then_inc(consts_loaded, 16)
            sp.dma_start(onesrow[:, :], t["onesrow"]).then_inc(consts_loaded, 16)

            def plain_loads(k):
                for dst, name in plain[k]:
                    sp.dma_start(dst if isinstance(dst, bass.AP) else dst[:, :], t[name]).then_inc(loaded[k], 16)

            def split_load(i):
                (name, parts, cols, hi, lo), after = splits[i]
                if i == SPLIT_A:
                    sp.wait_ge(S["a_ml"], 4)
                if i >= 2:
                    sp.wait_ge(S["w_split"], 2 * (i - 1))
                sp.dma_start(stage[i % 2][0:parts, 0:cols], t[name]).then_inc(S[f"w_in{i % 2}"], 16)

            plain_loads("a")
            plain_loads("x")
            plain_loads("c")
            for i in range(SPLIT_A, SPLIT_C):
                split_load(i)

            def context_load(dst, b, src, s):
                sp.dma_start(dst, src[bass.ds(b, 1)].rearrange("b p n -> p (b n)")).then_inc(s, 16)

            def mask_load(b):
                sp.dma_start(mk8[:, :], t["mask"][bass.ds(b, 1), :]).then_inc(S["b_mask"], 16)

            context_load(CX[:, :], 0, t["ctx"], S["b_ctx"])
            mask_load(0)
            with sp.Fori(1, B) as b:
                sp.wait_ge(S["b_cn"], b)
                sp.wait_ge(S["b_mk"], b)
                context_load(CX[:, :], b, t["ctx"], S["b_ctx"])
                mask_load(b)
            sp.wait_ge(layer_done[0], B)
            plain_loads("e")
            context_load(CTE[0:DC + 1, :], 0, t["ctxT"], S["e_ctx"])
            for i in range(SPLIT_C, SPLIT_E):
                split_load(i)
            sp.wait_ge(layer_done[2], B)
            plain_loads("d")
            plain_loads("f")
            for i in range(SPLIT_E, SPLIT_F):
                split_load(i)
            with sp.Fori(1, B) as b:
                sp.wait_ge(S["e_vo"], 4 * b - 3)
                context_load(CTE[0:DC + 1, :], b, t["ctxT"], S["e_ctx"])
            sp.wait_ge(layer_done[5], B)
            sp.dma_start(out, X[:, :]).then_inc(out_stored, 16)
            sp.wait_ge(out_stored, 16)

        @block.gpsimd
        def _(pool):
            po = Own(pool, pool_own)
            nc.gpsimd.memset(halves[:, :], -0.5)
            po.did(nc.gpsimd.memset(sm[:, 1022:1023], 0.0))
            po.wait()
            po.base, po.k = 1, 0

            def split(i):
                (name, parts, cols, hi, lo), after = splits[i]
                if after is not None:
                    pool.wait_ge(layer_done[after], B)
                pool.wait_ge(S[f"w_in{i % 2}"], 16 * (i // 2 + 1))
                src = (stage[i % 2] if i >= SPLIT_A else OTA)[0:parts, 0:cols]
                nc.gpsimd.tensor_copy(hi[0:parts, 0:cols], src).then_inc(S["w_split"], 1)
                pool.wait_ge(S["w_split"], 2 * i + 1)
                nc.gpsimd.tensor_tensor(lo[0:parts, 0:cols], src, hi[0:parts, 0:cols].bitcast(f32),
                                        ALU.subtract).then_inc(S["w_split"], 1)

            nc.gpsimd.memset(onesb[:, :], 1.0).then_inc(S["b_ones"], 1)

            def norm(k):
                wait_alone(pool, S["b_var"], k + 1)
                nc.gpsimd.tensor_scalar(vs[:, 0:MT], mv3[:, 0:MT, 1], LN_EPS, None, ALU.add)
                po.did(nc.gpsimd.tensor_scalar(vs[:, MT:MT + NT], mv3[:, MT:MT + NT, 1], 1.0 + LN_EPS, LN_EPS * LN_EPS,
                                               ALU.mult, ALU.add))
                po.wait()
                nc.gpsimd.tensor_tensor(rs[:, 0:MT + NT], vs[:, 0:MT + NT], halves[:, 0:MT + NT],
                                        ALU.pow).then_inc(S["b_rstd"], 1)

            def roots(k, half):
                c0 = 8 * half
                wait_alone(pool, S["b_ss"], 2 * k + half + 1)
                po.did(nc.gpsimd.tensor_scalar(sm[:, 16 + c0:24 + c0], sm[:, c0:c0 + 8], 1.0 / EX, 1e-16, ALU.mult,
                                               ALU.max))
                po.wait()
                nc.gpsimd.tensor_tensor(sm[:, 32 + c0:40 + c0], sm[:, 16 + c0:24 + c0], halves[:, 0:8],
                                        ALU.pow).then_inc(S["b_rr"], 1)

            def place_values(k, first=False):
                wait_alone(pool, S["b_rc"], 6 * k + 6)
                if not first:
                    wait_alone(pool, S["b_o"], k)
                nc.gpsimd.tensor_copy(VX[:, :].rearrange("p (t c) -> p t c", c=D),
                                      RKV[:, :].rearrange("p (t c) -> p t c", c=2 * D)[:, :, D:2 * D]
                                      ).then_inc(S["b_vx"], 1)

            def repeat(b, p):
                wait_alone(pool, S["a_ptc"], 16 * b + 2 * p + 2)
                r = sm[:, 256:256 + NT * HA].rearrange("p (t h) -> p t h", h=HA)[:, :, 2 * p:2 * p + 2]
                nc.gpsimd.tensor_copy(RB[p % 2][:, :].rearrange("p (t h e) -> p t h e", h=2, e=EA),
                                      r.rearrange("p t (h o) -> p t h o", o=1).broadcast_to([P, NT, 2, EA])
                                      ).then_inc(S["a_rb"], 1)

            po.loop(0, 1)
            front_pool(pool, po, fronts[0], 0)
            po.end(1)
            for i in range(SPLIT_A):
                split(i)
            with pool.Fori(0, B - 1) as b:
                po.loop(b, 1)
                for p in range(HA // 2):
                    repeat(b, p)
                    if p == 2:
                        front_pool(pool, po, fronts[0], b + 1)
            po.end(B - 1)

            def split_part(i, part, parts):
                (name, rows, cols, hi, lo), after = splits[i]
                if part == 0:
                    pool.wait_ge(S[f"w_in{i % 2}"], 16 * (i // 2 + 1))
                cs = slice(part * cols // parts, (part + 1) * cols // parts)
                src = stage[i % 2][0:rows, cs]
                po.did(nc.gpsimd.tensor_copy(hi[0:rows, cs], src))
                po.wait()
                last = nc.gpsimd.tensor_tensor(lo[0:rows, cs], src, hi[0:rows, cs].bitcast(f32), ALU.subtract)
                if part == parts - 1:
                    last.then_inc(S["w_split"], 2)

            po.loop(0, HA // 2 + 3)
            norm(0)
            for p in range(HA // 2):
                repeat(B - 1, p)
                if p == 3:
                    roots(0, 0)
                if p == 5:
                    roots(0, 1)
                split_part(SPLIT_A + p // 4, p % 4, 4)
            po.end(1)
            assert SPLIT_C - SPLIT_A == 2
            po.loop(0, 1)
            norm(1)
            place_values(0, first=True)
            po.end(1)
            with pool.Fori(0, B - 2) as b:
                po.loop(b, 3)
                roots(b + 1, 0)
                roots(b + 1, 1)
                norm(b + 2)
                place_values(b + 1)
            po.end(B - 2)
            po.loop(0, 2)
            roots(B - 1, 0)
            roots(B - 1, 1)
            place_values(B - 1)
            po.end(1)

            def plain_layer(layer):
                wait_alone(pool, layer_done[layer - 1], B)
                with pool.Fori(0, B) as b:
                    po.loop(b, 1)
                    front_pool(pool, po, fronts[layer], b)
                po.end(B)

            plain_layer(2)
            for i in range(SPLIT_C, SPLIT_E):
                split(i)

            nc.gpsimd.memset(VO[:, :], 0.0).then_inc(S["e_vo0"], 1)
            pool.wait_ge(S["e_vo0"], 1)
            nc.gpsimd.memset(VO[:, :].rearrange("p (h c) -> p h c", c=32)[:, :, EY:2 * EY], 1.0)
            nc.gpsimd.memset(NMX[:, :], 0.0).then_inc(S["e_vo0"], 1)
            pool.wait_ge(S["e_vo0"], 2)

            def context_split(b):
                wait_alone(pool, S["e_ctx"], 16 * b + 16)
                nc.gpsimd.tensor_copy(CEH[0:DC + 1, :], CTE[0:DC + 1, :]).then_inc(S["e_split"], 1)
                wait_alone(pool, S["e_split"], 2 * b + 1)
                nc.gpsimd.tensor_tensor(CEL[0:DC + 1, :], CTE[0:DC + 1, :], CEH[0:DC + 1, :].bitcast(f32),
                                        ALU.subtract).then_inc(S["e_split"], 1)

            context_split(0)

            wait_alone(pool, layer_done[2], B)

            def step(b3, b2, b1):
                if b1 is not None:
                    front_pool(pool, po, fronts[3], b1)
                if b2 is not None:
                    wait_alone(pool, S["d_vc"], b2 + 1)
                    if b3 is not None:
                        wait_alone(pool, S["d_o"], b3 + 1)
                    nc.gpsimd.tensor_copy(VD[1][:, :], VD[0][:, :]).then_inc(S["d_v2"], 1)

            po.loop(0, 2)
            step(None, None, 0)
            step(None, 0, 1)
            po.end(1)
            with pool.Fori(0, B - 2) as b:
                po.loop(b, 1)
                step(b, b + 1, b + 2)
            po.end(B - 2)
            step(B - 2, B - 1, None)

            pool.wait_ge(layer_done[3], B)
            def value_group(b, g):
                dst = VO[:, :].rearrange("p (m h c) -> p m h c", h=HY, c=32)[:, :, 4 * g:4 * g + 4, 0:EY]
                src = VS[:, :].rearrange("p (m h c) -> p m h c", h=HY, c=EY)[:, :, 4 * g:4 * g + 4, :]
                nc.gpsimd.tensor_copy(dst, src).then_inc(S["e_vo"], 1)

            def place_maxima(b, g, before):
                if before is not None:
                    wait_alone(pool, *before)
                wait_alone(pool, S["e_nl"], 4 * b + g + 1)
                wait_alone(pool, S["e_qm"], 4 * b + g + 1)
                for j in range(4):
                    h = 4 * g + j
                    last = nc.gpsimd.tensor_scalar(QM[96:P, h * N:(h + 1) * N], NRL[96:P, :], hmask[96:P, j:j + 1],
                                                   None, ALU.mult)
                last.then_inc(S["e_nm"], 1)
                wait_alone(pool, S["e_nm"], 4 * b + g + 1)

            def attend(b, prev, more):
                for g in range(4):
                    if g == 0 and more:
                        front_pool(pool, po, fronts[4], b + 1)
                    if more:
                        before = ((fronts[4].rstd_ready, b + 2), (S["e_split"], 2 * b + 4), (S["e_vo"], 4 * b + 5),
                                  (S["e_vo"], 4 * b + 6))[g]
                    else:
                        before = ((S["e_vo"], 4 * b + 3), (S["e_vo"], 4 * b + 4), None, None)[g]
                    if g < 3:
                        place_maxima(b, g + 1, before)
                    elif more:
                        place_maxima(b + 1, 0, before)
                    if g == 0:
                        if prev:
                            wait_alone(pool, S["e_w"], 8 * b)
                            value_group(b, 3)
                        if more:
                            wait_alone(pool, S["e_k"], 4 * b + 4)
                            context_split(b + 1)
                    elif more:
                        wait_alone(pool, S["e_w"], 8 * b + 2 * g)
                        wait_alone(pool, S["e_vc"], b + 2)
                        value_group(b + 1, g - 1)

            po.loop(0, 2)
            front_pool(pool, po, fronts[4], 0)
            pool.wait_ge(S["e_vc"], 1)
            for g in range(4):
                value_group(0, g)
            place_maxima(0, 0, (S["e_vo"], 4))
            attend(0, False, True)
            po.end(1)
            with pool.Fori(1, B - 1) as b:
                po.loop(b - 1, 1)
                attend(b, True, True)
            po.end(B - 2)
            attend(B - 1, True, False)
            for i in range(SPLIT_E, SPLIT_F):
                split(i)
            plain_layer(5)

        @block.tensor
        def _(pe):
            pe.wait_ge(S["qk_in"], 32)
            for q in range(4):
                for i in range(4):
                    h = 4 * q + i
                    last = mm(PB[q][:, i * D:(i + 1) * D], stage[0][0:EA, h * D:(h + 1) * D],
                              stage[1][0:EA, h * D:(h + 1) * D])
                last.then_inc(S["a_mready"], 1)
            pe.wait_ge(S["a_ml"], 4)
            pe.wait_ge(consts_loaded, 32)

            ring = PB[7]

            def prepare(k, r):
                if r == 0:
                    pe.wait_ge(S["b_cn"], k + 1)
                else:
                    pe.wait_ge(S["b_rc"], 6 * k + r)
                if r == 0:
                    for i in range(MT):
                        last = nc.tensor.transpose(ring[0:DC, i * P:(i + 1) * P], CN[:, i * DC:(i + 1) * DC],
                                                   ident[:, :])
                elif r == 1:
                    for i in range(NT):
                        last = nc.tensor.transpose(ring[:, i * P:(i + 1) * P], LN2[:, i * D:(i + 1) * D],
                                                   ident[:, :])
                elif r == 2:
                    for i in range(NT):
                        last = mm(ring[:, i * D:(i + 1) * D], LT[:, i * P:(i + 1) * P], WQX[:, :])
                else:
                    for q in range(2):
                        i = 2 * (r - 3) + q
                        o = ring[:, q * 2 * D:(q + 1) * 2 * D]
                        if i < MT:
                            last = mm(o, CXT[0:DC, i * P:(i + 1) * P], WKVX[0:DC, :])
                        else:
                            last = mm(o, LT[:, (i - MT) * P:(i - MT + 1) * P], WLKV[:, :])
                last.then_inc(S["b_r"], 1)

            def turn_keys(k):
                pe.wait_ge(S["b_rc"], 6 * k + 6)
                pe.wait_ge(S["b_qkn"], k + 1)
                for i in range(MT):
                    last = nc.tensor.transpose(ring[:, i * P:(i + 1) * P], QKN[:, (2 + i) * D:(3 + i) * D],
                                               ident[:, :])
                last.then_inc(S["b_kt"], 1)
                for i, c0 in enumerate((6, 7, 0, 1)):
                    last = nc.tensor.transpose(PB[5][:, i * P:(i + 1) * P], QKN[:, c0 * D:(c0 + 1) * D],
                                               ident[:, :])
                last.then_inc(S["b_kt"], 1)

            def scores(b, u):
                hd, i = u // NT, u % NT
                if u == 0:
                    pe.wait_ge(S["b_kh"], 2 * b + 2)
                    pe.wait_ge(S["b_kl"], 2 * b + 2)
                    pe.wait_ge(S["b_mk"], b + 1)
                q = slice(hd * N + i * P, hd * N + (i + 1) * P)
                lo, hi = PB[2 * (u % 2)], PB[2 * (u % 2) + 1]
                mm3(lo[:, :], QXH[:, q], QXL[:, q], KXH[:, 0:M], KXL[:, 0:M], last=False)
                mm(lo[:, :], onesb[:, :], mkb[:, :], first=False)
                mm3(hi[:, 0:N], QXH[:, q], QXL[:, q], KXH[:, M:TK], KXL[:, M:TK]).then_inc(S["b_s"], 1)

            def turn(b, u):
                pe.wait_ge(S["b_exp"], 4 * b + u + 1)
                for mt in range(6):
                    last = nc.tensor.transpose(PB[4 + mt // 4][:, mt % 4 * P:(mt % 4 + 1) * P],
                                               PX[u % 2][:, mt * P:(mt + 1) * P], ident[:, :])
                last.then_inc(S["b_pt"], 1)

            def weigh(b, u):
                hd, i = u // NT, u % NT
                pe.wait_ge(S["b_ptc"], 4 * b + u + 1)
                pe.wait_ge(S["b_ptd"], 4 * b + u + 1)
                if u == 0:
                    pe.wait_ge(S["b_vx"], b + 1)
                for mt in range(6):
                    last = mm(PB[6][:, i * D + hd * EX:i * D + (hd + 1) * EX], PTX[:, mt * P:(mt + 1) * P],
                              VX[:, mt * D + hd * EX:mt * D + (hd + 1) * EX], first=mt == 0, last=mt == 5)
                if u == 3:
                    last.then_inc(S["b_o"], 1)

            def attend(b, more):
                scores(b, 0)
                if more:
                    prepare(b + 1, 0)
                scores(b, 1)
                if more:
                    prepare(b + 1, 1)
                for u in range(4):
                    turn(b, u)
                    if u < 2:
                        if more:
                            prepare(b + 1, 2 * u + 2)
                        scores(b, u + 2)
                    weigh(b, u)
                    if u < 2 and more:
                        prepare(b + 1, 2 * u + 3)
                if more:
                    turn_keys(b + 1)
                pe.wait_ge(S["b_on"], b + 1)
                for i in range(NT):
                    last = nc.tensor.transpose(PB[4][:, i * P:(i + 1) * P], ONX[:, i * D:(i + 1) * D], ident[:, :])
                last.then_inc(S["b_ot"], 1)
                pe.wait_ge(S["b_otc"], b + 1)
                for i in range(NT):
                    o = PB[6][:, i * D:(i + 1) * D]
                    mm(o, OTX[:, i * P:(i + 1) * P], WOX[:, :], last=False)
                    last = mm(o, onesrow[:, :], boX[:, :], first=False)
                last.then_inc(S["b_y"], 1)

            def self_attention():
                F = fronts[0]

                def values(b, u):
                    half, mt = u // 2, u % 2
                    if u >= 2:
                        pe.wait_ge(S["a_vc"], 4 * b + u - 1)
                    cs = slice(half * 512, half * 512 + 512)
                    mm3(PB[(4, 7)[u % 2]][:, :], XH[:, mt * P:(mt + 1) * P], XL[:, mt * P:(mt + 1) * P], WVH[:, cs],
                        WVL[:, cs]).then_inc(S["a_v"], 1)

                def project(b, p):
                    if p >= 1:
                        pe.wait_ge(S["a_gl"], 8 * b + p)
                    else:
                        pe.wait_ge(S["a_vc"], 4 * b + 3)
                    for i in range(2):
                        hs = slice((2 * p + i) * D, (2 * p + i + 1) * D)
                        last = mm3(PB[4][:, i * N:(i + 1) * N], MH[:, hs], ML[:, hs], XH[:, :], XL[:, :])
                    last.then_inc(S["a_g"], 1)

                def scores(b, h):
                    if h % 2 == 0:
                        pe.wait_ge(S["a_gl"], 8 * b + h // 2 + 1)
                    if h >= 2:
                        pe.wait_ge(S["a_exp"], 16 * b + h - 1)
                    gh, gl = GH[h // 2 % 2], GL[h // 2 % 2]
                    for i in range(NT):
                        cs = slice(h % 2 * N + i * P, h % 2 * N + (i + 1) * P)
                        last = mm3(PB[h % 2][:, i * N:(i + 1) * N], gh[:, cs], gl[:, cs], XH[:, :], XL[:, :])
                    last.then_inc(S["a_s"], 1)

                def turn(b, h):
                    pe.wait_ge(S["a_exp"], 16 * b + h + 1)
                    if h >= 2:
                        pe.wait_ge(S["a_ptc"], 16 * b + h - 1)
                    for mt in range(NT):
                        for i in range(NT):
                            last = nc.tensor.transpose(
                                PB[2 + h % 2][:, mt * N + i * P:mt * N + (i + 1) * P],
                                PA[h % 2][:, i * N + mt * P:i * N + (mt + 1) * P], ident[:, :])
                    last.then_inc(S["a_pt"], 1)

                def weigh(b, p):
                    pe.wait_ge(S["a_ptc"], 16 * b + 2 * p + 2)
                    if p == 0:
                        pe.wait_ge(S["a_vc"], 4 * b + 4)
                    if p >= 2:
                        pe.wait_ge(S["a_on"], 8 * b + p - 1)
                    bank = PB[5 + p % 2]
                    for mt in range(NT):
                        for j in range(2):
                            h = 2 * p + j
                            mm(bank[j * EA:(j + 1) * EA, 0:N],
                               VA[:, mt * HA * EA + h * EA:mt * HA * EA + (h + 1) * EA],
                               PTA[h % 4][:, mt * N:(mt + 1) * N], first=mt == 0, last=mt == NT - 1)

                def reciprocals(b, p):
                    bank = PB[5 + p % 2]
                    pe.wait_ge(S["a_rb"], 8 * b + p + 1)
                    for i in range(NT):
                        last = nc.tensor.transpose(bank[:, N + i * P:N + (i + 1) * P], RB[p % 2][:, i * P:(i + 1) * P],
                                                   ident[:, :])
                    last.then_inc(S["a_o"], 1)

                def attend(b, more):
                    for s in range(HA):
                        if s >= 1:
                            scores(b, s)
                        if s % 2 == 0 and s + 2 < HA:
                            project(b, s // 2 + 1)
                        if not more and 4 <= s < 10:
                            if s == 4:
                                pe.wait_ge(loaded["x"], 16 * len(plain["x"]))
                            prepare(0, s - 4)
                        if s == HA - 1 and more:
                            front_tensor(pe, F, b + 1)
                        if s % 2 and s >= 3:
                            weigh(b, (s - 3) // 2)
                        if s >= 1:
                            turn(b, s - 1)
                        if s % 2 and s >= 3:
                            reciprocals(b, (s - 3) // 2)
                    if more:
                        pe.wait_ge(F.xh_ready, b + 2)
                        pe.wait_ge(F.xl_ready, b + 2)
                        values(b + 1, 0)
                    turn(b, HA - 1)
                    if more:
                        values(b + 1, 1)
                    weigh(b, HA // 2 - 1)
                    if more:
                        values(b + 1, 2)
                    reciprocals(b, HA // 2 - 1)
                    if more:
                        values(b + 1, 3)
                        project(b + 1, 0)
                        pe.wait_ge(S["a_vc"], 4 * b + 8)
                    else:
                        pe.wait_ge(S["b_rc"], 6)
                    pe.wait_ge(S["a_on"], 8 * b + 8)
                    for i in range(NT):
                        o = PB[7][:, i * D:(i + 1) * D]
                        for k in range(HA * EA // P):
                            mm(o, OTA[:, k * N + i * P:k * N + (i + 1) * P], WP[:, k * D:(k + 1) * D], first=k == 0,
                               last=False)
                        last = mm(o, onesrow[:, :], bp[:, :], first=False)
                    last.then_inc(S["a_y"], 1)
                    if more:
                        scores(b + 1, 0)

                front_tensor(pe, F, 0)
                pe.wait_ge(F.xh_ready, 1)
                pe.wait_ge(F.xl_ready, 1)
                pe.wait_ge(S["w_split"], 2 * SPLIT_A)
                pe.wait_ge(loaded["a"], 16 * len(plain["a"]))
                for u in range(4):
                    values(0, u)
                project(0, 0)
                scores(0, 0)
                with pe.Fori(0, B - 1) as b:
                    attend(b, True)
                attend(B - 1, False)

            self_attention()

            pe.wait_ge(layer_done[0], B)
            pe.wait_ge(loaded["x"], 16 * len(plain["x"]))
            pe.wait_ge(S["b_ones"], 1)

            turn_keys(0)
            with pe.Fori(0, B - 1) as b:
                attend(b, True)
            attend(B - 1, False)

            def experts(layer, names, inner, wr, nexp, up, ups, gate, gates, down):
                r, hs, sg, h2s, ys, yd = names
                F = fronts[layer]
                pairs = len(inner)

                def route(b):
                    pe.wait_ge(F.xf_ready, b + 1)
                    for i in range(NT):
                        last = mm(PB[6][:, i * 32:i * 32 + nexp], XF2[:, i * P:(i + 1) * P], wr[:, 0:nexp])
                    last.then_inc(S[r], 1)

                def hidden(b, q):
                    n = inner[q][0]
                    if q >= 2:
                        pe.wait_ge(S[h2s], pairs * b + q - 1)
                    if q == 0:
                        pe.wait_ge(F.xh_ready, b + 1)
                        pe.wait_ge(F.xl_ready, b + 1)
                    for k in range(n):
                        cs = slice((2 * q + k) * P, (2 * q + k + 1) * P)
                        mm3(PB[2 * (q % 2)][:, k * N:(k + 1) * N], gate[:, cs], gates[:, cs], XH[:, :], XL[:, :])
                    for k in range(n):
                        cs = slice((2 * q + k) * P, (2 * q + k + 1) * P)
                        last = mm3(PB[2 * (q % 2) + 1][:, k * N:(k + 1) * N], up[:, cs], ups[:, cs], XH[:, :],
                                   XL[:, :])
                    last.then_inc(S[hs], 1)

                def output(b, q):
                    pe.wait_ge(S[h2s], pairs * b + q + 1)
                    if q >= 2:
                        pe.wait_ge(S[yd], (pairs - 1) * b + q - 1)
                    n, joint = inner[q]
                    y = PB[4 + q % 2]
                    for i in range(NT):
                        for k in range(n):
                            o = y[:, i * D:(i + 1) * D] if joint else y[:, (k * NT + i) * D:(k * NT + i + 1) * D]
                            last = mm(o, H2[q % 2][:, k * N + i * P:k * N + (i + 1) * P],
                                      down[:, (2 * q + k) * D:(2 * q + k + 1) * D],
                                      first=k == 0 or not joint, last=k == n - 1 or not joint)
                    last.then_inc(S[ys], 1)

                def batch(b, more):
                    for q in range(pairs):
                        if q + 1 < pairs:
                            hidden(b, q + 1)
                        elif more:
                            if pairs % 2:
                                pe.wait_ge(S[h2s], pairs * b + pairs)
                            hidden(b + 1, 0)
                        if q == 2 and more:
                            front_tensor(pe, F, b + 1)
                        output(b, q)
                        if q == 4 and more:
                            route(b + 1)

                front_tensor(pe, F, 0)
                route(0)
                hidden(0, 0)
                with pe.Fori(0, B - 1) as b:
                    batch(b, True)
                batch(B - 1, False)

            pe.wait_ge(layer_done[1], B)
            pe.wait_ge(S["w_split"], 2 * SPLIT_C)
            pe.wait_ge(loaded["c"], 16 * len(plain["c"]))
            experts(2, ("c_r", "c_h", "c_sg", "c_h2", "c_y", "c_yd"), [(2, True)] * E0, WGC, E0, W3H, W3L, W1H,
                    W1L, W2C)

            pe.wait_ge(layer_done[2], B)
            pe.wait_ge(loaded["d"], 16 * len(plain["d"]))

            def step(b3, b2, b1):
                F = fronts[3]
                if b2 is not None:
                    pe.wait_ge(S["d_qc"], b2 + 1)
                    for i in range(NT):
                        last = mm(PB[2][:, i * N:(i + 1) * N], QD[:, i * P:(i + 1) * P], KD[:, :])
                    last.then_inc(S["d_s"], 1)
                if b3 is not None:
                    pe.wait_ge(S["d_ptc"], b3 + 1)
                    pe.wait_ge(S["d_v2"], b3 + 1)
                    for i in range(NT):
                        for mt in range(NT):
                            last = mm(PB[4][:, i * D:(i + 1) * D], PTD[:, mt * N + i * P:mt * N + (i + 1) * P],
                                      VD[1][:, mt * D:(mt + 1) * D], first=mt == 0, last=mt == NT - 1)
                    last.then_inc(S["d_o"], 1)
                    pe.wait_ge(S["d_on"], b3 + 1)
                    for i in range(NT):
                        last = nc.tensor.transpose(PB[5][:, i * P:(i + 1) * P], OND[:, i * D:(i + 1) * D], ident[:, :])
                    last.then_inc(S["d_ot"], 1)
                if b2 is not None:
                    pe.wait_ge(S["d_exp"], b2 + 1)
                    for mt in range(NT):
                        for i in range(NT):
                            last = nc.tensor.transpose(PB[3][:, mt * N + i * P:mt * N + (i + 1) * P],
                                                       PD[:, i * N + mt * P:i * N + (mt + 1) * P], ident[:, :])
                    last.then_inc(S["d_pt"], 1)
                if b1 is not None:
                    front_tensor(pe, F, b1)
                if b3 is not None:
                    pe.wait_ge(S["d_otc"], b3 + 1)
                    for i in range(NT):
                        mm(PB[6][:, i * D:(i + 1) * D], OTD[:, i * P:(i + 1) * P], WOD[:, :], last=False)
                        last = mm(PB[6][:, i * D:(i + 1) * D], onesrow[:, :], boD[:, :], first=False)
                    last.then_inc(S["d_y"], 1)
                if b1 is not None:
                    pe.wait_ge(F.xh_ready, b1 + 1)
                    mm(PB[0][:, 0:N], WQD[:, :], XF[:, :])
                    mm(PB[0][:, N:2 * N], WKD[:, :], XF[:, :]).then_inc(S["d_q"], 1)
                    for i in range(NT):
                        mm(PB[1][:, i * D:(i + 1) * D], XF[:, i * P:(i + 1) * P], WVD[:, :], last=False)
                        last = mm(PB[1][:, i * D:(i + 1) * D], onesrow[:, :], bvD[:, :], first=False)
                    last.then_inc(S["d_v"], 1)

            def self_attention1():
                step(None, None, 0)
                step(None, 0, 1)
                with pe.Fori(0, B - 2) as b:
                    step(b, b + 1, b + 2)
                step(B - 2, B - 1, None)
                step(B - 1, None, None)

            self_attention1()

            pe.wait_ge(layer_done[3], B)
            pe.wait_ge(S["w_split"], 2 * SPLIT_E)
            pe.wait_ge(loaded["e"], 16 * len(plain["e"]))
            pe.wait_ge(S["e_vo0"], 2)
            F4 = fronts[4]

            def keys_queries(b, g):
                cs = slice(g * P, (g + 1) * P)
                if g == 0:
                    pe.wait_ge(S["e_split"], 2 * b + 2)
                    pe.wait_ge(S["e_vc"], b + 1)
                else:
                    pe.wait_ge(S["e_ks"], 4 * b + g)
                mm3(PB[6][:, :], WKSH[0:DC + 1, cs], WKSL[0:DC + 1, cs], CEH[0:DC + 1, :],
                    CEL[0:DC + 1, :]).then_inc(S["e_k"], 1)
                if g == 0:
                    pe.wait_ge(F4.xh_ready, b + 1)
                    pe.wait_ge(F4.xl_ready, b + 1)
                else:
                    pe.wait_ge(S["e_qc"], 4 * b + g)
                mm3(PB[7][:, 0:N], WQSH[:, cs], WQSL[:, cs], XH[:, :], XL[:, :]).then_inc(S["e_q"], 1)

            def score_unit(b, g, n, first=False):
                h, i = 4 * g + n // 2, n % 2
                if n == 0:
                    pe.wait_ge(S["e_qm"], 4 * b + g + 1)
                if not (first and n < 2):
                    pe.wait_ge(S["e_max"], 32 * b + 8 * g + n - 1)
                mm(PB[n % 2][:, :], QM[:, h * N + i * P:h * N + (i + 1) * P],
                   KS[:, g * M:(g + 1) * M]).then_inc(S["e_s"], 1)

            def rows(b, g):
                pe.wait_ge(S["e_max"], 32 * b + 8 * g + 8)
                for i in range(NT):
                    last = nc.tensor.transpose(PB[5][:, i * P:(i + 1) * P], NMX[:, i * P:(i + 1) * P], ident[:, :])
                last.then_inc(S["e_nr"], 1)

            def turned_unit(b, g, k, j, prev):
                h, n = 4 * g + j, 4 * k + j
                if g or n >= 2 or prev:
                    pe.wait_ge(S["e_exp"], 32 * b + 8 * g + n - 1)
                for q in range(2):
                    mt = 2 * k + q
                    last = mm(PB[2 + n % 2][:, q * N:(q + 1) * N], KS[:, g * M + mt * P:g * M + (mt + 1) * P],
                              QM[:, h * N:(h + 1) * N])
                last.then_inc(S["e_st"], 1)

            def weigh(b, g, k, prev=True):
                pe.wait_ge(S["e_exp"], 32 * b + 8 * g + 4 * k + 4)
                if k == 0:
                    pe.wait_ge(S["e_vo"], 4 * b + g + 1)
                    if g or prev:
                        pe.wait_ge(S["e_uc"], 4 * b + g)
                for q in range(2):
                    mt = 2 * k + q
                    for j in range(4):
                        h = 4 * g + j
                        last = mm(PB[4][32 * j:32 * j + 32, 0:N], VO[:, (mt * HY + h) * 32:(mt * HY + h + 1) * 32],
                                  PTE[k][:, (2 * j + q) * N:(2 * j + q + 1) * N], first=mt == 0, last=mt == MT - 1)
                last.then_inc(S["e_w"], 1)

            def gather(b):
                pe.wait_ge(S["e_uc"], 4 * b + 4)
                for g in range(4):
                    mm(PB[5][:, 0:N], CU[:, g * P:(g + 1) * P], UD[:, g * N:(g + 1) * N], first=g == 0, last=g == 3)
                for g in range(4):
                    last = mm(PB[5][:, N:2 * N], CD[:, g * P:(g + 1) * P], UD[:, g * N:(g + 1) * N], first=g == 0,
                              last=g == 3)
                last.then_inc(S["e_od"], 1)

            def inner(b):
                pe.wait_ge(S["e_o"], b + 1)
                for k in range(2):
                    last = mm(PB[5][:, k * N:(k + 1) * N], W1E[:, k * P:(k + 1) * P], OE[:, :])
                last.then_inc(S["e_h"], 1)

            def outer(b):
                pe.wait_ge(S["e_hc"], b + 1)
                for i in range(NT):
                    for k in range(2):
                        mm(PB[5][:, i * D:(i + 1) * D], H1E[:, k * N + i * P:k * N + (i + 1) * P],
                           W2E[:, k * D:(k + 1) * D], first=k == 0, last=False)
                    last = mm(PB[5][:, i * D:(i + 1) * D], onesrow[:, :], b2E[:, :], first=False)
                last.then_inc(S["e_y"], 1)

            def attend(b, prev, more):
                for g in range(4):
                    if g == 2 and prev:
                        pe.wait_ge(S["e_o"], b)
                    if g == 3 and prev:
                        pe.wait_ge(S["e_hc"], b)
                    if g < 3:
                        rows(b, g + 1)
                    elif more:
                        rows(b + 1, 0)
                    pe.wait_ge(S["e_nm"], 4 * b + g + 1)
                    for k in range(2):
                        for j in range(4):
                            turned_unit(b, g, k, j, prev)
                            if g < 2:
                                score_unit(b, g + 2, 4 * k + j)
                            elif more:
                                score_unit(b + 1, g - 2, 4 * k + j)
                        if k:
                            weigh(b, g, 0, prev)
                            continue
                        if g == 0:
                            keys_queries(b, 3)
                        elif more:
                            keys_queries(b + 1, g - 1)
                        if prev and g:
                            if g < 3 or more:
                                pe.wait_ge(S["e_nl"], 4 * b + g + 2)
                            (gather, inner, outer)[g - 1](b - 1)
                        if g:
                            weigh(b, g - 1, 1)
                        elif prev:
                            weigh(b - 1, 3, 1)
                    if g == 0 and more:
                        pe.wait_ge(S["e_qc"], 4 * b + 4)
                        front_tensor(pe, F4, b + 1)
                        pe.wait_ge(S["e_ks"], 4 * b + 4)
                        pe.wait_ge(S["e_ctx"], 16 * b + 32)
                        values(b + 1)

            def values(b):
                for i in range(MT):
                    last = mm(PB[6][:, i * D:(i + 1) * D], CTE[0:DC + 1, i * P:(i + 1) * P], WVE[0:DC + 1, :])
                last.then_inc(S["e_v"], 1)

            pe.wait_ge(S["e_ctx"], 16)
            values(0)
            front_tensor(pe, F4, 0)
            keys_queries(0, 0)
            keys_queries(0, 1)
            for n in range(8):
                score_unit(0, 0, n, first=True)
            keys_queries(0, 2)
            rows(0, 0)
            for n in range(8):
                score_unit(0, 1, n)
            attend(0, False, True)
            with pe.Fori(1, B - 1) as b:
                attend(b, True, True)
            attend(B - 1, True, False)
            weigh(B - 1, 3, 1)
            pe.wait_ge(layer_done[4], B - 1)
            gather(B - 1)
            inner(B - 1)
            outer(B - 1)

            pe.wait_ge(layer_done[4], B)
            pe.wait_ge(S["w_split"], 2 * SPLIT_F)
            pe.wait_ge(loaded["f"], 16 * len(plain["f"]))
            experts(5, ("f_r", "f_h", "f_sg", "f_h2", "f_y", "f_yd"), [(2, False)] * (E1 // 2) + [(1, False)],
                    WGF, E1, FUH, FUL, FGH, FGL, FD)

        @block.scalar
        def _(act):
            for q in range(4):
                act.wait_ge(S["a_mready"], q + 1)
                nc.scalar.activation(MH[:, q * 512:(q + 1) * 512], PB[q][:, :], ACT.Copy,
                                     scale=1.0 / math.sqrt(EA)).then_inc(S["a_mh"], 1)

            ring = PB[7]

            def squares(dst, src):
                return nc.scalar.activation(dst, src, ACT.Square)

            def copied(k, r, first=False):
                if r == 3 and not first:
                    act.wait_ge(S["b_vx"], k)
                act.wait_ge(S["b_r"], 6 * k + r + 1)
                if r == 0:
                    last = nc.scalar.activation(CXT[0:DC, :], ring[0:DC, :], ACT.Identity, scale=gcol[0:DC, 0:1],
                                                bias=gcol[0:DC, 1:2])
                elif r == 1:
                    last = nc.scalar.activation(LT[:, :], ring[:, 0:N], ACT.Identity, scale=gcol[:, 2:3],
                                                bias=gcol[:, 3:4])
                elif r == 2:
                    squares(SQ[:, 0:2 * D], ring[:, 0:2 * D])
                    last = nc.scalar.activation(RQ[:, :], ring[:, 0:2 * D], ACT.Copy)
                else:
                    c0 = 2 * (r - 3)
                    sq = squares(SQ[:, (2 + c0) * D:(4 + c0) * D].rearrange("p (t c) -> p t c", c=D),
                                 ring[:, :].rearrange("p (t c) -> p t c", c=2 * D)[:, :, 0:D])
                    if r != 4:
                        sq.then_inc(S["b_sq"], 1)
                    last = nc.scalar.activation(RKV[:, c0 * 2 * D:(c0 + 2) * 2 * D], ring[:, :], ACT.Copy)
                last.then_inc(S["b_rc"], 1)

            def high_keys(k):
                act.wait_ge(S["b_kt"], 2 * k + 1)
                nc.scalar.activation(KXH[:, 0:M], ring[:, :], ACT.Copy, scale=gcol[:, 6:7]).then_inc(S["b_kh"], 1)

            def high_queries(k):
                act.wait_ge(S["b_kt"], 2 * k + 2)
                nc.scalar.activation(KXH[:, M:TK], PB[5][:, 0:N], ACT.Copy, scale=gcol[:, 6:7])
                for hd in range(HX):
                    last = nc.scalar.activation(QXH[:, hd * N:(hd + 1) * N], PB[5][:, N:2 * N], ACT.Copy,
                                                scale=gcol[:, 4 + hd:5 + hd])
                last.then_inc(S["b_kh"], 1)

            def exps(b, u):
                act.wait_ge(S["b_max"], 4 * b + u + 1)
                k = 2 * (u % 2)
                nc.scalar.activation(PX[u % 2][:, 0:M], PB[k][:, :], ACT.Exp, scale=1.0 / math.sqrt(EX),
                                     bias=sm[:, 64 + u:65 + u], accum_out=sm[:, 68 + u:69 + u])
                nc.scalar.activation(PX[u % 2][:, M:TK], PB[k + 1][:, 0:N], ACT.Exp, scale=1.0 / math.sqrt(EX),
                                     bias=sm[:, 64 + u:65 + u],
                                     accum_out=sm[:, 72 + u:73 + u]).then_inc(S["b_exp"], 1)

            def attend(b, more):
                if more:
                    copied(b + 1, 0)
                exps(b, 0)
                if more:
                    copied(b + 1, 1)
                exps(b, 1)
                for u in range(4):
                    act.wait_ge(S["b_pt"], 4 * b + u + 1)
                    nc.scalar.activation(PTX[:, M:TK], PB[5][:, 0:N], ACT.Copy).then_inc(S["b_ptd"], 1)
                    if u < 2:
                        if more:
                            copied(b + 1, 2 * u + 2)
                        exps(b, u + 2)
                        if more:
                            copied(b + 1, 2 * u + 3)
                if more:
                    high_keys(b + 1)
                act.wait_ge(S["b_ot"], b + 1)
                nc.scalar.activation(OTX[:, :], PB[4][:, 0:N], ACT.Copy).then_inc(S["b_otc"], 1)
                if more:
                    high_queries(b + 1)

            def self_attention():
                def values(b, u):
                    act.wait_ge(S["a_v"], 4 * b + u + 1)
                    half, mt = u // 2, u % 2
                    nc.scalar.activation(VA[:, mt * HA * EA + half * 512:mt * HA * EA + (half + 1) * 512],
                                         PB[(4, 7)[u % 2]][:, :], ACT.Copy).then_inc(S["a_vc"], 1)

                def high(b, p):
                    act.wait_ge(S["a_g"], 8 * b + p + 1)
                    nc.scalar.activation(GH[p % 2][:, :], PB[4][:, :], ACT.Copy).then_inc(S["a_gh"], 1)

                def exps(b, h):
                    act.wait_ge(S["a_max"], 16 * b + h + 1)
                    for i in range(NT):
                        last = nc.scalar.activation(PA[h % 2][:, i * N:(i + 1) * N], PB[h % 2][:, i * N:(i + 1) * N],
                                                    ACT.Exp, bias=sm[:, 128 + 2 * h + i:129 + 2 * h + i],
                                                    accum_out=sm[:, 192 + i * HA + h:193 + i * HA + h])
                    last.then_inc(S["a_exp"], 1)

                def reciprocals(b, p):
                    act.wait_ge(S["a_o"], 8 * b + p + 1)
                    if p >= 2:
                        act.wait_ge(S["a_on"], 8 * b + p - 1)
                    nc.scalar.activation(RA[p % 2][:, :], PB[5 + p % 2][:, N:2 * N], ACT.Copy).then_inc(S["a_rc"], 1)

                def attend(b, more):
                    for h in range(HA):
                        exps(b, h)
                        if h % 2 == 0 and h + 2 < HA:
                            high(b, h // 2 + 1)
                        if h == HA - 2 and more:
                            front_scalar(act, fronts[0], b + 1)
                        if not more and 4 <= h < 10:
                            if h == 4:
                                act.wait_ge(loaded["x"], 16 * len(plain["x"]))
                            copied(0, h - 4, first=True)
                        if h % 2 and h >= 5:
                            reciprocals(b, (h - 5) // 2)
                    reciprocals(b, HA // 2 - 2)
                    if more:
                        values(b + 1, 0)
                        values(b + 1, 1)
                    reciprocals(b, HA // 2 - 1)
                    if more:
                        values(b + 1, 2)
                        values(b + 1, 3)
                        high(b + 1, 0)

                front_scalar(act, fronts[0], 0)
                for u in range(4):
                    values(0, u)
                high(0, 0)
                with act.Fori(0, B - 1) as b:
                    attend(b, True)
                attend(B - 1, False)

            self_attention()

            act.wait_ge(loaded["x"], 16 * len(plain["x"]))

            high_keys(0)
            high_queries(0)
            with act.Fori(0, B - 1) as b:
                attend(b, True)
            attend(B - 1, False)

            def experts(layer, names, inner):
                r, hs, sg, h2s, ys, yd = names
                F = fronts[layer]
                pairs = len(inner)

                def tokens(b):
                    act.wait_ge(F.xt_ready, b + 1)
                    nc.scalar.activation(XF2[:, :], PB[BANK_X][:, 0:N], ACT.Copy).then_inc(F.xf_ready, 1)

                def high(b):
                    act.wait_ge(F.xf_ready, b + 1)
                    nc.scalar.activation(XH[:, :], XF2[:, :], ACT.Copy).then_inc(F.xh_ready, 1)

                def sigmoids(b):
                    if layer == 5:
                        act.wait_ge(S["f_r"], b + 1)
                        for i in range(NT):
                            last = nc.scalar.activation(gt[:, i * E1:(i + 1) * E1], PB[6][:, i * 32:i * 32 + E1],
                                                        ACT.Sigmoid)
                        last.then_inc(S["f_sig"], 1)
                    else:
                        act.wait_ge(S["c_xf"], b + 1)
                        nc.scalar.activation(gt[:, 96:96 + 2 * E0], gt[:, 64:64 + 2 * E0],
                                             ACT.Sigmoid).then_inc(S["c_sig"], 1)

                def batch(b, more):
                    for q in range(pairs):
                        n = inner[q][0]
                        act.wait_ge(S[hs], pairs * b + q + 1)
                        if q == pairs - 1 and more:
                            high(b + 1)
                        nc.scalar.activation(SG[q % 2][:, 0:n * N], PB[2 * (q % 2)][:, 0:n * N],
                                             ACT.Silu).then_inc(S[sg], 1)
                        if q == 3 and more:
                            tokens(b + 1)
                        if q == (5 if layer == 5 else 6) and more:
                            sigmoids(b + 1)

                tokens(0)
                high(0)
                sigmoids(0)
                nc.scalar.activation(gt[:, 500:501], XF2[:, 0:1], ACT.Silu)
                with act.Fori(0, B - 1) as b:
                    batch(b, True)
                batch(B - 1, False)

            act.wait_ge(layer_done[1], B)
            experts(2, ("c_r", "c_h", "c_sg", "c_h2", "c_y", "c_yd"), [(2, True)] * E0)

            act.wait_ge(layer_done[2], B)
            act.wait_ge(loaded["d"], 16 * len(plain["d"]))

            def step(b3, b2, b1):
                F = fronts[3]
                if b2 is not None:
                    act.wait_ge(S["d_max"], b2 + 1)
                    for i in range(NT):
                        last = nc.scalar.activation(PD[:, i * N:(i + 1) * N], PB[2][:, i * N:(i + 1) * N], ACT.Exp,
                                                    scale=1.0 / math.sqrt(D), bias=sm[:, 64 + i:65 + i],
                                                    accum_out=sm[:, 68 + i:69 + i])
                    last.then_inc(S["d_exp"], 1)
                if b3 is not None:
                    act.wait_ge(S["d_ot"], b3 + 1)
                    nc.scalar.activation(OTD[:, :], PB[5][:, 0:N], ACT.Copy).then_inc(S["d_otc"], 1)
                if b1 is not None:
                    act.wait_ge(F.xt_ready, b1 + 1)
                    nc.scalar.activation(XF[:, :], PB[BANK_X][:, 0:N], ACT.Copy).then_inc(F.xh_ready, 1)
                    act.wait_ge(S["d_q"], b1 + 1)
                    nc.scalar.activation(QD[:, :], PB[0][:, 0:N], ACT.Identity, bias=bqk[:, 0:1])
                    nc.scalar.activation(KD[:, :], PB[0][:, N:2 * N], ACT.Identity,
                                         bias=bqk[:, 1:2]).then_inc(S["d_qc"], 1)
                    act.wait_ge(S["d_v"], b1 + 1)
                    if b2 is not None:
                        act.wait_ge(S["d_v2"], b2 + 1)
                    nc.scalar.activation(VD[0][:, :], PB[1][:, 0:N], ACT.Copy).then_inc(S["d_vc"], 1)

            def self_attention1():
                step(None, None, 0)
                step(None, 0, 1)
                with act.Fori(0, B - 2) as b:
                    step(b, b + 1, b + 2)
                step(B - 2, B - 1, None)
                step(B - 1, None, None)

            self_attention1()

            act.wait_ge(layer_done[3], B)
            act.wait_ge(loaded["e"], 16 * len(plain["e"]))
            act.wait_ge(S["e_vo0"], 2)

            def values(b):
                act.wait_ge(S["e_v"], b + 1)
                nc.scalar.activation(VS[:, :], PB[6][:, :], ACT.Copy).then_inc(S["e_vc"], 1)

            def keys_queries(b, g):
                act.wait_ge(S["e_k"], 4 * b + g + 1)
                nc.scalar.activation(KHt[:, :].bitcast(f32r), PB[6][:, :], ACT.Copy).then_inc(S["e_kh"], 1)
                act.wait_ge(S["e_q"], 4 * b + g + 1)
                nc.scalar.activation(QT0[:, :], PB[7][:, 0:N], ACT.Identity, bias=bqs[:, g:g + 1]).then_inc(S["e_qc"], 1)

            def masks(b, g, js=range(4)):
                if 0 in js:
                    act.wait_ge(S["e_qs"], 8 * b + 2 * g + 2)
                for j in js:
                    h = 4 * g + j
                    last = nc.scalar.activation(QM[:, h * N:(h + 1) * N], QSt[:, :], ACT.Copy, scale=hmask[:, j:j + 1])
                if 3 in js:
                    last.then_inc(S["e_qm"], 1)

            def exps(b, g, k, js, prev):
                if 0 in js and (g or prev):
                    act.wait_ge(S["e_w"], 8 * b + 2 * g + k - 1)
                for j in js:
                    n = 4 * k + j
                    act.wait_ge(S["e_st"], 32 * b + 8 * g + n + 1)
                    nc.scalar.activation(PTE[k][:, 2 * j * N:(2 * j + 2) * N], PB[2 + n % 2][:, :], ACT.Exp,
                                         scale=1.0 / math.sqrt(EY)).then_inc(S["e_exp"], 1)

            def outputs(b, g):
                act.wait_ge(S["e_w"], 8 * b + 2 * g + 2)
                nc.scalar.activation(UD[:, g * N:(g + 1) * N], PB[4][:, 0:N], ACT.Copy).then_inc(S["e_uc"], 1)

            def inner(b):
                act.wait_ge(S["e_h"], b + 1)
                for k in range(2):
                    last = nc.scalar.activation(H1E[:, k * N:(k + 1) * N], PB[5][:, k * N:(k + 1) * N], ACT.Relu,
                                                bias=b1E[:, k:k + 1])
                last.then_inc(S["e_hc"], 1)

            def attend(b, prev, more):
                for g in range(4):
                    exps(b, g, 0, (0, 1), prev)
                    if g == 1 and more:
                        act.wait_ge(S["e_vo"], 4 * b + 4)
                        values(b + 1)
                    exps(b, g, 0, (2, 3), prev)
                    if g == 0:
                        keys_queries(b, 3)
                    elif more:
                        keys_queries(b + 1, g - 1)
                    if g == 2 and prev:
                        inner(b - 1)
                    if g:
                        outputs(b, g - 1)
                    elif prev:
                        outputs(b - 1, 3)
                    exps(b, g, 1, (0, 1), prev)
                    for j in (2, 3):
                        if g == 0:
                            masks(b, 3, (j - 2,))
                        elif more:
                            masks(b + 1, g - 1, (j - 2,))
                        exps(b, g, 1, (j,), prev)
                    if g == 0:
                        masks(b, 3, (2, 3))
                    elif more:
                        masks(b + 1, g - 1, (2, 3))
                    if g == 0 and more:
                        front_scalar(act, fronts[4], b + 1)

            values(0)
            front_scalar(act, fronts[4], 0)
            for g in range(3):
                keys_queries(0, g)
                masks(0, g)
            attend(0, False, True)
            with act.Fori(1, B - 1) as b:
                attend(b, True, True)
            attend(B - 1, True, False)
            outputs(B - 1, 3)
            inner(B - 1)

            act.wait_ge(layer_done[4], B)
            experts(5, ("f_r", "f_h", "f_sg", "f_h2", "f_y", "f_yd"), [(2, False)] * (E1 // 2) + [(1, False)])

        @block.vector
        def _(dve):
            o = Own(dve, own)

            def add_to_x(b, src, layer):
                nc.vector.tensor_tensor(Xt[:, bass.ds(b * NT, NT), :], Xt[:, bass.ds(b * NT, NT), :],
                                        src.rearrange("p (t d) -> p t d", d=D), ALU.add).then_inc(layer_done[layer], 1)

            dve.wait_ge(x_loaded, 16)

            ring = PB[7]

            def statistics(k):
                for i in range(NT):
                    nc.vector.bn_stats(st3[:, MT + i, :], X[:, bass.ds((k * NT + i) * D, D)])
                dve.wait_ge(S["b_ctx"], 16 * k + 16)
                for i in range(MT):
                    last = nc.vector.bn_stats(st3[:, i, :], CX[:, i * DC:(i + 1) * DC])
                o.did(last)
                o.wait_alone()
                for i in range(MT + NT):
                    last = nc.vector.bn_aggr(mv3[:, i, :], st3[:, i, :])
                last.then_inc(S["b_var"], 1)

            def normalise(k):
                dve.wait_ge(S["b_rstd"], k + 1)
                for i in range(MT):
                    nc.vector.tensor_scalar(CN[:, i * DC:(i + 1) * DC], CX[:, i * DC:(i + 1) * DC],
                                            mv3[:, i, 0:1], rs[:, i:i + 1], ALU.subtract, ALU.mult)
                for i in range(NT):
                    last = nc.vector.tensor_scalar(LN2[:, i * D:(i + 1) * D], X[:, bass.ds((k * NT + i) * D, D)],
                                                   mv3[:, MT + i, 0:1], rs[:, MT + i:MT + i + 1], ALU.subtract,
                                                   ALU.mult)
                last.then_inc(S["b_cn"], 1)

            def mask_row(k):
                dve.wait_ge(S["b_mask"], 16 * k + 16)
                nc.vector.tensor_scalar(mkb[:, :], mk8[:, :], -1.0, 1e30, ALU.add,
                                        ALU.mult).then_inc(S["b_mk"], 1)

            def sums(k, half):
                dve.wait_ge(S["b_sq"], 2 * k + half + 1)
                nc.vector.reduce_sum(sm[:, 8 * half:8 * half + 8],
                                     SQ[:, 4 * half * D:4 * (half + 1) * D].rearrange("p (n e) -> p n e", e=EX),
                                     AX.X).then_inc(S["b_ss"], 1)

            def over_norms(k, half):
                dve.wait_ge(S["b_rr"], 2 * k + half + 1)
                if half == 0:
                    nc.vector.tensor_tensor(
                        QKN[:, 0:2 * D].rearrange("p (n e) -> p n e", e=EX),
                        RQ[:, :].rearrange("p (n e) -> p n e", e=EX),
                        sm[:, 32:36].rearrange("p (n o) -> p n o", o=1).broadcast_to([P, 4, EX]), ALU.mult)
                t0, n, r0 = (2, 4, 40) if half else (0, 2, 36)
                dve.wait_ge(S["b_rc"], 6 * k + 2 * half + 4)
                for i in range(t0, t0 + n):
                    rr = sm[:, 36 + 2 * i:38 + 2 * i]
                    last = nc.vector.tensor_tensor(
                        QKN[:, (2 + i) * D:(3 + i) * D].rearrange("p (n e) -> p n e", e=EX),
                        RKV[:, i * 2 * D:i * 2 * D + D].rearrange("p (n e) -> p n e", e=EX),
                        rr.rearrange("p (n o) -> p n o", o=1).broadcast_to([P, 2, EX]), ALU.mult)
                if half:
                    last.then_inc(S["b_qkn"], 1)

            def low(dst, src, gain, high):
                return nc.vector.scalar_tensor_tensor(out=dst, in0=src, scalar=gcol[:, gain:gain + 1],
                                                      in1=high.bitcast(f32), op0=ALU.mult, op1=ALU.subtract)

            def low_keys(k):
                dve.wait_ge(S["b_kh"], 2 * k + 1)
                low(KXL[:, 0:M], ring[:, :], 6, KXH[:, 0:M]).then_inc(S["b_kl"], 1)

            def low_queries(k):
                dve.wait_ge(S["b_kh"], 2 * k + 2)
                low(KXL[:, M:TK], PB[5][:, 0:N], 6, KXH[:, M:TK])
                for hd in range(HX):
                    cs = slice(hd * N, (hd + 1) * N)
                    last = low(QXL[:, cs], PB[5][:, N:2 * N], 4 + hd, QXH[:, cs])
                last.then_inc(S["b_kl"], 1)

            def maximum(b, u):
                dve.wait_ge(S["b_s"], 4 * b + u + 1)
                k = 2 * (u % 2)
                mx = sm[:, 88 + 2 * u:90 + 2 * u]
                nc.vector.tensor_reduce(mx[:, 0:1], PB[k][:, :], AX.X, ALU.max)
                o.did(nc.vector.tensor_reduce(mx[:, 1:2], PB[k + 1][:, 0:N], AX.X, ALU.max))
                o.wait()
                nc.vector.tensor_scalar(sm[:, 64 + u:65 + u], mx[:, 0:1], mx[:, 1:2], -1.0 / math.sqrt(EX),
                                        ALU.max, ALU.mult).then_inc(S["b_max"], 1)

            def copy(b, u):
                dve.wait_ge(S["b_pt"], 4 * b + u + 1)
                nc.vector.tensor_copy(PTX[:, 0:M], PB[4][:, :]).then_inc(S["b_ptc"], 1)

            def attend(b, more, more2):
                maximum(b, 0)
                maximum(b, 1)
                copy(b, 0)
                maximum(b, 2)
                copy(b, 1)
                maximum(b, 3)
                if more:
                    mask_row(b + 1)
                    sums(b + 1, 0)
                copy(b, 2)
                if more:
                    sums(b + 1, 1)
                copy(b, 3)
                if more:
                    over_norms(b + 1, 0)
                    over_norms(b + 1, 1)
                dve.wait_ge(S["b_exp"], 4 * b + 4)
                o.did(nc.vector.tensor_tensor(sm[:, 76:80], sm[:, 68:72], sm[:, 72:76], ALU.add))
                o.wait()
                o.did(nc.vector.reciprocal(sm[:, 84:88], sm[:, 76:80]))
                o.wait()
                dve.wait_ge(S["b_o"], b + 1)
                for u in range(4):
                    hd, i = u // NT, u % NT
                    cs = slice(i * D + hd * EX, i * D + (hd + 1) * EX)
                    last = nc.vector.tensor_scalar(ONX[:, cs], PB[6][:, cs], sm[:, 84 + u:85 + u], None, ALU.mult)
                last.then_inc(S["b_on"], 1)
                if more:
                    low_keys(b + 1)
                    if more2:
                        statistics(b + 2)
                    low_queries(b + 1)
                dve.wait_ge(S["b_y"], b + 1)
                add_to_x(b, PB[6][:, 0:N], 1)
                if more2:
                    normalise(b + 2)

            def start_next(s):
                if s == 1:
                    dve.wait_ge(layer_done[0], B - 1)
                    statistics(0)
                if s == 3:
                    normalise(0)
                    mask_row(0)
                if s == 8:
                    sums(0, 0)
                if s == 11:
                    sums(0, 1)
                    over_norms(0, 0)
                if s == 14:
                    over_norms(0, 1)

            def self_attention():
                F = fronts[0]

                def low(b, p):
                    dve.wait_ge(S["a_gh"], 8 * b + p + 1)
                    nc.vector.tensor_tensor(GL[p % 2][:, :], PB[4][:, :], GH[p % 2][:, :].bitcast(f32),
                                            ALU.subtract).then_inc(S["a_gl"], 1)

                def maximum(b, h):
                    dve.wait_ge(S["a_s"], 16 * b + h + 1)
                    nc.vector.tensor_reduce(sm[:, 128 + 2 * h:130 + 2 * h],
                                            PB[h % 2][:, :].rearrange("p (t m) -> p t m", m=N), AX.X, ALU.max,
                                            negate=True).then_inc(S["a_max"], 1)

                def copy(b, h):
                    dve.wait_ge(S["a_pt"], 16 * b + h + 1)
                    if h % 2:
                        nc.vector.reciprocal(
                            sm[:, 256:256 + NT * HA].rearrange("p (t h) -> p t h", h=HA)[:, :, h - 1:h + 1],
                            sm[:, 192:192 + NT * HA].rearrange("p (t h) -> p t h", h=HA)[:, :, h - 1:h + 1])
                    nc.vector.tensor_copy(PTA[h % 4][:, :], PB[2 + h % 2][:, :]).then_inc(S["a_ptc"], 1)

                def normalise(b, p):
                    dve.wait_ge(S["a_rc"], 8 * b + p + 1)
                    bank = PB[5 + p % 2]
                    nc.vector.tensor_tensor(OTA[:, p * N:(p + 1) * N], bank[:, 0:N], RA[p % 2][:, :],
                                            ALU.mult).then_inc(S["a_on"], 1)

                def attend(b, more):
                    for s in range(HA):
                        if s >= 1:
                            maximum(b, s)
                        if s % 2 and s + 1 < HA:
                            low(b, s // 2 + 1)
                        if s == HA - 1 and more:
                            front_low(dve, F, b + 1)
                        if s >= 1:
                            copy(b, s - 1)
                        if s % 2 and s >= 5:
                            normalise(b, (s - 5) // 2)
                        if not more:
                            start_next(s)
                        if s == 6 and more:
                            front_statistics(o, F, b + 1)
                        if s == 10 and more:
                            front_normalise(dve, F, b + 1)
                    copy(b, HA - 1)
                    normalise(b, HA // 2 - 2)
                    normalise(b, HA // 2 - 1)
                    if more:
                        low(b + 1, 0)
                    dve.wait_ge(S["a_y"], b + 1)
                    add_to_x(b, PB[7][:, 0:N], 0)
                    if more:
                        maximum(b + 1, 0)

                o.loop(0, 1)
                front_vector(dve, o, F, 0)
                for q in range(4):
                    dve.wait_ge(S["a_mh"], q + 1)
                    nc.vector.scalar_tensor_tensor(out=ML[:, q * 512:(q + 1) * 512], in0=PB[q][:, :],
                                                   scalar=1.0 / math.sqrt(EA), in1=MH[:, q * 512:(q + 1) * 512].bitcast(f32),
                                                   op0=ALU.mult, op1=ALU.subtract).then_inc(S["a_ml"], 1)
                front_low(dve, F, 0)
                low(0, 0)
                maximum(0, 0)
                o.end(1)
                with dve.Fori(0, B - 1) as b:
                    o.loop(b, 1)
                    attend(b, True)
                o.end(B - 1)
                o.loop(0, 1)
                attend(B - 1, False)
                o.end(1)

            self_attention()

            dve.wait_ge(layer_done[0], B)
            dve.wait_ge(loaded["x"], 16 * len(plain["x"]))

            o.loop(0, 1)
            statistics(1)
            low_keys(0)
            low_queries(0)
            normalise(1)
            o.end(1)
            with dve.Fori(0, B - 2) as b:
                o.loop(b, 7)
                attend(b, True, True)
            o.end(B - 2)
            o.loop(0, 6)
            attend(B - 2, True, False)
            o.end(1)
            o.loop(0, 6)
            attend(B - 1, False, False)
            o.end(1)

            def experts(layer, names, inner, router, weigh, weight, steps):
                r, hs, sg, h2s, ys, yd = names
                F = fronts[layer]
                pairs = len(inner)

                def low(b):
                    dve.wait_ge(F.xh_ready, b + 1)
                    nc.vector.tensor_tensor(XL[:, :], XF2[:, :], XH[:, :].bitcast(f32),
                                            ALU.subtract).then_inc(F.xl_ready, 1)

                def add(b, q):
                    dve.wait_ge(S[ys], pairs * b + q + 1)
                    n, joint = inner[q]
                    for k in range(1 if joint else n):
                        if k == 0 and q > 0:
                            dve.wait_ge(S[yd], (pairs - 1) * b + q)
                        else:
                            o.wait()
                        for i in range(NT):
                            xs = X[:, bass.ds((b * NT + i) * D, D)]
                            last = nc.vector.scalar_tensor_tensor(
                                out=xs, in0=PB[4 + q % 2][:, (k * NT + i) * D:(k * NT + i + 1) * D],
                                scalar=weight(i, q if joint else 2 * q + k), in1=xs, op0=ALU.mult, op1=ALU.add)
                        if not joint and k < n - 1:
                            o.did(last)
                    last.then_inc(S[yd] if q < pairs - 1 else layer_done[layer], 1)

                def gated(b, q):
                    n = inner[q][0]
                    dve.wait_ge(S[sg], pairs * b + q + 1)
                    nc.vector.tensor_tensor(H2[q % 2][:, 0:n * N], SG[q % 2][:, 0:n * N],
                                            PB[2 * (q % 2) + 1][:, 0:n * N], ALU.mult).then_inc(S[h2s], 1)

                def batch(b, more):
                    for q in range(pairs):
                        if q == pairs - 1 and more:
                            low(b + 1)
                        if q:
                            gated(b, q)
                        if q >= 1:
                            add(b, q - 1)
                        if q == 0 and more:
                            front_statistics(o, F, b + 1)
                        if q == 1 and more:
                            front_normalise(dve, F, b + 1)
                        if q == (8 if layer == 5 else 5) and more:
                            router(b + 1)
                    if more and pairs % 2 == 0:
                        gated(b + 1, 0)
                    add(b, pairs - 1)
                    if more and pairs % 2:
                        gated(b + 1, 0)
                    if more:
                        dve.wait_ge(layer_done[layer], b + 1)
                        weigh(b + 1)

                router_steps, add_steps = steps
                o.loop(0, 1 + router_steps)
                front_vector(dve, o, F, 0)
                low(0)
                router(0)
                gated(0, 0)
                weigh(0)
                o.end(1)
                with dve.Fori(0, B - 1) as b:
                    o.loop(b, 1 + router_steps + add_steps)
                    batch(b, True)
                o.end(B - 1)
                o.loop(0, add_steps)
                batch(B - 1, False)
                o.end(1)

            LOW, TAKEN = -3e38, -1e38

            def router0(b):
                dve.wait_ge(S["c_r"], b + 1)
                for i in range(NT):
                    last = nc.vector.tensor_copy(gt[:, 16 * i:16 * i + E0], PB[6][:, 32 * i:32 * i + E0])
                o.did(last)
                o.wait_alone()
                for i in range(NT):
                    last = nc.vector.max(gt[:, 32 + 8 * i:40 + 8 * i], gt[:, 16 * i:16 * i + E0])
                o.did(last)
                o.wait()
                for i in range(NT):
                    last = nc.vector.tensor_tensor(gt[:, 48 + i:49 + i], gt[:, 32 + 8 * i:33 + 8 * i],
                                                   gt[:, 33 + 8 * i:34 + 8 * i], ALU.add)
                    nc.vector.memset(gt[:, 34 + 8 * i:40 + 8 * i], LOW)
                o.did(nc.vector.memset(gt[:, 50:51], 0.0))
                o.wait()
                for i in range(NT):
                    last = nc.vector.tensor_scalar(gt[:, 64 + 8 * i:72 + 8 * i], gt[:, 16 * i:16 * i + E0], 2.0,
                                                   gt[:, 48 + i:49 + i], ALU.mult, ALU.subtract)
                last.then_inc(S["c_xf"], 1)
                for i in range(NT):
                    last = nc.vector.match_replace(gt[:, 128 + 16 * i:142 + 16 * i], gt[:, 32 + 8 * i:40 + 8 * i],
                                                   gt[:, 16 * i:16 * i + 14], TAKEN)
                o.did(last)

            def weigh0(b):
                o.wait()
                dve.wait_ge(S["c_sig"], b + 1)
                for i in range(NT):
                    last = nc.vector.scalar_tensor_tensor(
                        out=gt[:, 160 + 8 * i:168 + 8 * i], in0=gt[:, 128 + 16 * i:136 + 16 * i], scalar=TAKEN,
                        in1=gt[:, 96 + 8 * i:104 + 8 * i], op0=ALU.is_equal, op1=ALU.mult)
                o.did(last)

            def router1(b):
                dve.wait_ge(S["f_sig"], b + 1)
                for i in range(NT):
                    last = nc.vector.tensor_tensor(gt[:, 32 + 16 * i:48 + 16 * i], gt[:, 16 * i:16 * i + E1], ebF[:, :],
                                                   ALU.add)
                o.did(last)
                o.wait_alone()
                for i in range(NT):
                    last = nc.vector.max(gt[:, 64 + 8 * i:72 + 8 * i], gt[:, 32 + 16 * i:48 + 16 * i])
                o.did(last)
                o.wait_alone()
                for i in range(NT):
                    last = nc.vector.match_replace(gt[:, 80 + 16 * i:96 + 16 * i], gt[:, 64 + 8 * i:72 + 8 * i],
                                                   gt[:, 32 + 16 * i:48 + 16 * i], TAKEN)
                o.did(last)
                o.wait()
                for i in range(NT):
                    last = nc.vector.scalar_tensor_tensor(
                        out=gt[:, 112 + 16 * i:128 + 16 * i], in0=gt[:, 80 + 16 * i:96 + 16 * i], scalar=TAKEN,
                        in1=gt[:, 16 * i:16 * i + E1], op0=ALU.is_equal, op1=ALU.mult)
                o.did(last)
                o.wait()
                o.did(nc.vector.reduce_sum(gt[:, 144:146], gt[:, 112:144].rearrange("p (t e) -> p t e", e=E1), AX.X))
                o.wait()
                o.did(nc.vector.reciprocal(gt[:, 146:148], gt[:, 144:146]))

            def weigh1(b):
                o.wait()
                for i in range(NT):
                    last = nc.vector.tensor_scalar(gt[:, 160 + 32 * i:176 + 32 * i], gt[:, 112 + 16 * i:128 + 16 * i],
                                                   gt[:, 146 + i:147 + i], ROUTE_SCALE, ALU.mult, ALU.mult)
                o.did(last)

            dve.wait_ge(layer_done[1], B)
            for i in range(NT):
                last = nc.vector.memset(gt[:, 16 * i + E0:16 * i + 16], LOW)
            last.then_inc(own, 1)
            o.base += 1
            o.wait()
            experts(2, ("c_r", "c_h", "c_sg", "c_h2", "c_y", "c_yd"), [(2, True)] * E0, router0, weigh0,
                    lambda i, x: gt[:, 160 + 8 * i + x:161 + 8 * i + x], (5, 0))

            dve.wait_ge(layer_done[2], B)

            def step(b3, b2, b1):
                F = fronts[3]
                if b1 is not None:
                    front_statistics(o, F, b1)
                if b2 is not None:
                    dve.wait_ge(S["d_s"], b2 + 1)
                    o.did(nc.vector.tensor_reduce(sm[:, 88:90], PB[2][:, :].rearrange("p (t m) -> p t m", m=N), AX.X,
                                                  ALU.max))
                    o.wait()
                    nc.vector.tensor_scalar(sm[:, 64:66], sm[:, 88:90], -1.0 / math.sqrt(D), None,
                                            ALU.mult).then_inc(S["d_max"], 1)
                if b3 is not None:
                    dve.wait_ge(S["d_o"], b3 + 1)
                    o.wait()
                    for i in range(NT):
                        last = nc.vector.tensor_scalar(OND[:, i * D:(i + 1) * D], PB[4][:, i * D:(i + 1) * D],
                                                       sm[:, 72 + i:73 + i], None, ALU.mult)
                    last.then_inc(S["d_on"], 1)
                if b1 is not None:
                    front_normalise(dve, F, b1)
                if b2 is not None:
                    dve.wait_ge(S["d_pt"], b2 + 1)
                    nc.vector.tensor_copy(PTD[:, :], PB[3][:, :]).then_inc(S["d_ptc"], 1)
                    if b3 is not None:
                        dve.wait_ge(S["d_on"], b3 + 1)
                    o.did(nc.vector.reciprocal(sm[:, 72:74], sm[:, 68:70]))
                if b3 is not None:
                    dve.wait_ge(S["d_y"], b3 + 1)
                    add_to_x(b3, PB[6][:, 0:N], 3)

            o.loop(0, 4)
            step(None, None, 0)
            step(None, 0, 1)
            o.end(1)
            with dve.Fori(0, B - 2) as b:
                o.loop(b, 3)
                step(b, b + 1, b + 2)
            o.end(B - 2)
            o.loop(0, 2)
            step(B - 2, B - 1, None)
            step(B - 1, None, None)
            o.end(1)

            dve.wait_ge(layer_done[3], B)
            dve.wait_ge(loaded["e"], 16 * len(plain["e"]))
            dve.wait_ge(S["e_vo0"], 2)
            nm4 = NMX[:, :].rearrange("p (t c) -> p t c", c=P)

            def keys(b, g):
                dve.wait_ge(S["e_kh"], 4 * b + g + 1)
                nc.vector.scalar_tensor_tensor(out=KS[:, g * M:(g + 1) * M], in0=KHt[:, :], scalar=selk[:, 0:1],
                                               in1=PB[6][:, :], op0=ALU.mult, op1=ALU.add).then_inc(S["e_ks"], 1)

            def queries(b, g, first=False):
                dve.wait_ge(S["e_qc"], 4 * b + g + 1)
                nc.vector.tensor_copy(QHt[:, :].bitcast(f32r), QT0[:, :]).then_inc(S["e_qs"], 1)
                dve.wait_ge(S["e_qs"], 8 * b + 2 * g + 1)
                if not first:
                    dve.wait_ge(S["e_qm"], 4 * b + g)
                nc.vector.scalar_tensor_tensor(out=QSt[:, :].bitcast(f32r), in0=QHt[:, :], scalar=selq[:, 0:1],
                                               in1=QT0[:, :], op0=ALU.mult, op1=ALU.add).then_inc(S["e_qs"], 1)

            def maxima(b, g, ns, first=False):
                if 0 in ns and not first:
                    dve.wait_ge(S["e_nr"], 4 * b + g)
                for n in ns:
                    j, i = n // 2, n % 2
                    dve.wait_ge(S["e_s"], 32 * b + 8 * g + n + 1)
                    last = nc.vector.tensor_reduce(NMX[:, i * P + 96 + j:i * P + 97 + j], PB[n % 2][:, :], AX.X,
                                                   ALU.max, negate=True)
                    if n < 7:
                        last.then_inc(S["e_max"], 1)
                if 7 in ns:
                    o.did(last)
                    o.wait()
                    nc.vector.tensor_copy(nm4[:, :, 100:104], nm4[:, :, 96:100]).then_inc(S["e_max"], 1)

            def split_maxima(b, g, first=False):
                dve.wait_ge(S["e_nr"], 4 * b + g + 1)
                o.did(nc.vector.tensor_copy(NRH[96:P, :].bitcast(f32r), PB[5][96:P, 0:N]))
                if not first:
                    dve.wait_ge(S["e_nm"], 4 * b + g)
                o.wait()
                nc.vector.scalar_tensor_tensor(out=NRL[96:P, :].bitcast(f32r), in0=NRH[96:P, :],
                                               scalar=seln[96:P, 0:1], in1=PB[5][96:P, 0:N], op0=ALU.mult,
                                               op1=ALU.add).then_inc(S["e_nl"], 1)

            def gathered(b):
                dve.wait_ge(S["e_od"], b + 1)
                o.did(nc.vector.reciprocal(RDE[:, :], PB[5][:, N:2 * N]))
                o.wait()
                nc.vector.tensor_tensor(OE[:, :], PB[5][:, 0:N], RDE[:, :], ALU.mult).then_inc(S["e_o"], 1)

            def outer(b):
                dve.wait_ge(S["e_y"], b + 1)
                add_to_x(b, PB[5][:, 0:N], 4)

            def attend(b, prev, more):
                for g in range(4):
                    if g == 1 and more:
                        front_low(dve, fronts[4], b + 1)
                    ahead = (b, g + 2) if g < 2 else (b + 1, g - 2)
                    if g < 2 or more:
                        maxima(*ahead, (0, 1))
                    if g < 3:
                        split_maxima(b, g + 1)
                    elif more:
                        split_maxima(b + 1, 0)
                    if g == 0 and more:
                        front_statistics(o, fronts[4], b + 1)
                    if g < 2 or more:
                        maxima(*ahead, (2, 3))
                    if g == 3 and prev:
                        outer(b - 1)
                    if g == 0:
                        keys(b, 3)
                        queries(b, 3)
                        if more:
                            front_normalise(dve, fronts[4], b + 1)
                    elif more:
                        keys(b + 1, g - 1)
                        queries(b + 1, g - 1)
                    if g < 2 or more:
                        maxima(*ahead, range(4, 8))
                    if g == 1 and prev:
                        gathered(b - 1)

            o.loop(0, 13)
            front_vector(dve, o, fronts[4], 0)
            front_low(dve, fronts[4], 0)
            for g in range(2):
                keys(0, g)
                queries(0, g, first=g == 0)
            maxima(0, 0, range(8), first=True)
            keys(0, 2)
            queries(0, 2)
            split_maxima(0, 0, first=True)
            maxima(0, 1, range(8))
            attend(0, False, True)
            o.end(1)
            with dve.Fori(1, B - 1) as b:
                o.loop(b - 1, 10)
                attend(b, True, True)
            o.end(B - 2)
            o.loop(0, 7)
            attend(B - 1, True, False)
            gathered(B - 1)
            outer(B - 1)
            o.end(1)

            dve.wait_ge(layer_done[4], B)
            dve.wait_ge(loaded["f"], 16 * len(plain["f"]))
            for i in range(NT):
                last = nc.vector.memset(gt[:, 176 + 32 * i:177 + 32 * i], 1.0)
            last.then_inc(own, 1)
            o.base += 1
            o.wait()
            experts(5, ("f_r", "f_h", "f_sg", "f_h2", "f_y", "f_yd"), [(2, False)] * (E1 // 2) + [(1, False)],
                    router1, weigh1, lambda i, x: gt[:, 160 + 32 * i + x:161 + 32 * i + x], (7, E1 // 2))


def kernel(**inputs):
    import numpy as np
    import concourse.bacc as bacc
    from concourse import mybir as mb
    from concourse.bass_utils import run_bass_kernel_spmd

    v = {k: np.asarray(a) for k, a in inputs.items()}
    f4 = np.float32

    def cols(a, k):
        return a.reshape(-1, P, k).transpose(1, 0, 2).reshape(P, -1)

    wq, wk, wv = (v["L0_attn_W" + n] for n in "qkv")
    g4 = np.arange(P)
    quad, off = g4 // 32, g4 % 32
    a = {
        "ident": np.eye(P, dtype=f4), "onesrow": np.ones((1, P), f4),
        "x": cols(v["x"].reshape(B * N, D), D),
        "wqT": wq.transpose(2, 0, 1).reshape(EA, HA * D), "wkT": wk.transpose(2, 0, 1).reshape(EA, HA * D),
        "wv": wv.transpose(1, 0, 2).reshape(D, HA * EA),
        "wp": cols(v["L0_attn_Wp"].reshape(EA, HA, D).transpose(1, 0, 2).reshape(HA * EA, D), D),
        "bp": v["L0_attn_bp"][None],
        "wqx": v["L0_xattn_Wq"].T, "wox": v["L0_xattn_Wo"].T, "wkvx": v["L0_xattn_Wkv"].T, "wlkv": v["L0_xattn_Wlkv"].T,
        "box": v["L0_xattn_bo"][None],
        "ctx": v["ctx_768"].reshape(B, MT, P, DC).transpose(0, 2, 1, 3).reshape(B, P, MT * DC),
        "mask": v["mask_BxS2_bk0"].reshape(B, M),
    }
    gcol = np.zeros((P, 7), f4)
    gcol[:DC, 0], gcol[:DC, 1] = v["L0_xattn_ln_x_g"], v["L0_xattn_ln_x_b"]
    gcol[:, 2], gcol[:, 3] = v["L0_xattn_ln_l_g"], v["L0_xattn_ln_l_b"]
    gcol[:EX, 4], gcol[EX:, 5], gcol[:, 6] = v["L0_xattn_qn_g"], v["L0_xattn_qn_g"], np.tile(v["L0_xattn_kn_g"], HX)
    a["gcol"] = gcol
    a["w1"] = v["L0_ffn_w1"].transpose(2, 0, 1).reshape(D, E0 * I0)
    a["w3"] = v["L0_ffn_w3"].transpose(2, 0, 1).reshape(D, E0 * I0)
    a["w2"] = v["L0_ffn_w2"].transpose(2, 0, 1).reshape(2, P, E0, D).transpose(1, 2, 0, 3).reshape(P, 2 * E0 * D)
    a["wgc"] = v["L0_ffn_wg"].T
    for n, s in (("wqd", "w_q"), ("wkd", "w_k"), ("wvd", "w_v"), ("wod", "w_out")):
        a[n] = v["L1_attn_" + s].T
    a["bqk"] = np.stack([v["L1_attn_b_q"], v["L1_attn_b_k"]], 1)
    a["bvd"], a["bod"] = v["L1_attn_b_v"][None], v["L1_attn_b_out"][None]

    wks, wqs = np.zeros((DC + 1, 4, P), f4), np.zeros((D, 4, P), f4)
    bqs = np.zeros((P, 4), f4)
    for g in range(4):
        for r in range(3):
            hc, to = slice(32 * g, 32 * g + 32), slice(32 * r, 32 * r + 32)
            wks[:DC, g, to], wks[DC, g, to] = v["L1_xattn_Wk"][:, hc], v["L1_xattn_bk"][hc]
            wqs[:, g, to], bqs[to, g] = v["L1_xattn_Wq"][:, hc], v["L1_xattn_bq"][hc]
        wks[DC, g, 96:104] = 1.0
    a["wks"], a["wqs"], a["bqs"] = wks.reshape(DC + 1, 4 * P), wqs.reshape(D, 4 * P), bqs
    wks_full = np.zeros((P, 4 * P), f4)
    wks_full[:DC + 1] = a["wks"]
    a["wks"] = wks_full
    a["wve"] = np.concatenate([v["L1_xattn_Wv"], v["L1_xattn_bv"][None]])
    a["w1e"] = v["L1_xattn_W1"]
    a["w2e"] = cols(v["L1_xattn_W2"], D)
    a["b1e"], a["b2e"] = v["L1_xattn_b1"].reshape(2, P).T, v["L1_xattn_b2"][None]
    a["ctxT"] = np.concatenate([v["ctx_768"].transpose(0, 2, 1), np.ones((B, 1, M), f4)], 1)
    cu, cd = np.zeros((P, 4, P), f4), np.zeros((P, 4, P), f4)
    for g in range(4):
        for j in range(4):
            for d in range(EY):
                cu[32 * j + d, g, 8 * (4 * g + j) + d] = 1.0
                cd[32 * j + EY, g, 8 * (4 * g + j) + d] = 1.0
    a["cu"], a["cd"] = cu.reshape(P, 4 * P), cd.reshape(P, 4 * P)
    a["selq"] = -(quad == 1).astype(f4)[:, None]
    a["selk"] = -(quad == 2).astype(f4)[:, None]
    a["seln"] = -((quad == 3) & (off >= 4) & (off < 8)).astype(f4)[:, None]
    head = np.where(quad < 3, off // EY, np.where(off < 8, off % 4, -1))
    a["hmask"] = (head[:, None] == np.arange(4)[None]).astype(f4)

    def fuse(routed, shared):
        return np.concatenate([routed, shared[None]]).transpose(2, 0, 1).reshape(P, STG)

    a["fg"] = fuse(v["L1_ffn_w_gate"], v["L1_ffn_shared_gate_w"])
    a["fu"] = fuse(v["L1_ffn_w_up"], v["L1_ffn_shared_up_w"])
    a["fd"] = fuse(v["L1_ffn_w_down"], v["L1_ffn_shared_down_w"])
    a["wgf"] = v["L1_ffn_gate_w"].T
    a["ebf"] = np.broadcast_to(v["L1_ffn_expert_bias"][None], (P, E1))

    nc = bacc.Bacc("TRN2", target_bir_lowering=False, num_devices=1)
    arrays, aps = {}, {}
    for name, arr in a.items():
        arr = np.ascontiguousarray(arr)
        arrays[f"in_{name}"] = arr
        aps[name] = nc.dram_tensor(f"in_{name}", arr.shape, mb.dt.from_np(arr.dtype), kind="ExternalInput").ap()
    out = nc.dram_tensor("out_0", (P, B * NT * D), mb.dt.float32, kind="ExternalOutput").ap()
    decoder(nc, aps, out)
    r = run_bass_kernel_spmd(nc, [arrays], core_ids=[0])
    y = r.results[0]["out_0"]
    return y.reshape(P, B * NT, D).transpose(1, 0, 2).reshape(B, N, D)
```
